# Optimizing a Trainium2 kernel written in Bass

```python
import numpy as np
import jax
import jax.numpy as jnp

def _softmax(x, axis=-1):
    return jax.nn.softmax(x, axis=axis)

def _gelu(x):
    return jax.nn.gelu(x, approximate=True)

def _silu(x):
    return jax.nn.silu(x)

def _sigmoid(x):
    return jax.nn.sigmoid(x)

def _layernorm(x, axis=-1, eps=1e-05):
    m = jnp.mean(x, axis=axis, keepdims=True)
    v = jnp.var(x, axis=axis, keepdims=True)
    return (x - m) / jnp.sqrt(v + eps)

def _scatter_add(tgt, idx, src, axis=0):
    return tgt.at[idx].add(src)

def _segment_sum(src, seg, n):
    return jax.ops.segment_sum(src, seg, n)
kernel_name = 'mk_hybrid_d1_jaxref_r8_64b8ea'

def setup_inputs(seed: int=0):
    np.random.seed(seed)
    _w = jnp.asarray

    def _L0_attn_a_setup():
        import jax, jax.numpy as jnp
        import numpy as np
        B, S, D = (4, 256, 128)

        def _xavier(key, shape):
            bound = float(np.sqrt(6.0 / (shape[0] + shape[1])))
            return jax.random.uniform(key, shape, dtype=jnp.float32, minval=-bound, maxval=bound)
        key = jax.random.key(seed)
        k0, k1, k2, k3 = jax.random.split(key, 4)
        return {'embeddings': jax.random.normal(k0, (B, S, D), dtype=jnp.float32), 'W_Q': _xavier(k1, (D, D)), 'W_K': _xavier(k2, (D, D)), 'W_V': _xavier(k3, (D, D))}
    _L0_attn_a_in = _L0_attn_a_setup()

    def _L0_attn_b_setup():
        import jax, jax.numpy as jnp
        import numpy as np
        import math
        B, T, C = (8, 256, 128)
        DIM_ATT, DIM_FFN = (128, 512)
        N_LAYER, LAYER_ID = (12, 1)
        EPS = 1e-05

        def layer_norm(x, w, b):
            mu = jnp.mean(x, axis=-1, keepdims=True)
            var = jnp.mean(jnp.square(x - mu), axis=-1, keepdims=True)
            return (x - mu) * jax.lax.rsqrt(var + EPS) * w + b

        def time_shift(x):
            return jnp.pad(x, ((0, 0), (1, 0), (0, 0)))[:, :-1, :]

        def wkv(time_decay, time_first, k, v):
            w = -jnp.exp(time_decay)
            u = time_first

            def step(carry, kv_t):
                aa, bb, pp = carry
                kt, vt = kv_t
                ww = u + kt
                qq = jnp.maximum(pp, ww)
                e1 = jnp.exp(pp - qq)
                e2 = jnp.exp(ww - qq)
                y = (e1 * aa + e2 * vt) / (e1 * bb + e2)
                ww2 = pp + w
                qq2 = jnp.maximum(ww2, kt)
                e1b = jnp.exp(ww2 - qq2)
                e2b = jnp.exp(kt - qq2)
                return ((e1b * aa + e2b * vt, e1b * bb + e2b, qq2), y)
            init = (jnp.zeros_like(k[:, 0]), jnp.zeros_like(k[:, 0]), jnp.full_like(k[:, 0], -1e+38))
            kT = jnp.swapaxes(k, 0, 1)
            vT = jnp.swapaxes(v, 0, 1)
            _, yT = jax.lax.scan(step, init, (kT, vT))
            return jnp.swapaxes(yT, 0, 1)
        key = jax.random.key(seed)
        ks = jax.random.split(key, 16)
        r01 = LAYER_ID / (N_LAYER - 1)
        r1a0 = 1.0 - LAYER_ID / N_LAYER
        ddd = (np.arange(C, dtype=np.float32) / C)[None, None, :]
        decay_speed = -5.0 + 8.0 * (np.arange(DIM_ATT, dtype=np.float32) / (DIM_ATT - 1)) ** (0.7 + 1.3 * r01)
        zigzag = np.array([(i + 1) % 3 - 1 for i in range(DIM_ATT)], dtype=np.float32) * 0.5

        def lin(k, out_d, in_d):
            return jax.random.normal(k, (out_d, in_d), jnp.float32) * (1.0 / math.sqrt(in_d))
        return {'x': jax.random.normal(ks[0], (B, T, C), jnp.float32), 'ln1_w': jnp.ones((C,), jnp.float32), 'ln1_b': jnp.zeros((C,), jnp.float32), 'ln2_w': jnp.ones((C,), jnp.float32), 'ln2_b': jnp.zeros((C,), jnp.float32), 'att_tmk': jnp.asarray(ddd ** r1a0), 'att_tmv': jnp.asarray(ddd ** r1a0 + 0.3 * r01), 'att_tmr': jnp.asarray(ddd ** (0.5 * r1a0)), 'time_decay': jnp.asarray(decay_speed), 'time_first': jnp.asarray(np.full(DIM_ATT, math.log(0.3), np.float32) + zigzag), 'Wk': lin(ks[1], DIM_ATT, C), 'Wv': lin(ks[2], DIM_ATT, C), 'Wr': lin(ks[3], DIM_ATT, C), 'Wo': lin(ks[4], C, DIM_ATT), 'ffn_tmk': jnp.asarray(ddd ** r1a0), 'ffn_tmr': jnp.asarray(ddd ** r1a0), 'Wkey': lin(ks[5], DIM_FFN, C), 'Wrec': lin(ks[6], C, C), 'Wval': lin(ks[7], C, DIM_FFN)}
    _L0_attn_b_in = _L0_attn_b_setup()

    def _L0_ffn_setup():
        import jax, jax.numpy as jnp
        import numpy as np
        TOP_K = 4
        CAP_FACTOR = 4

        def swiglu(x, w1, w2, w3):
            return jax.nn.silu(x @ w1) * (x @ w3) @ w2
        key = jax.random.key(seed)
        ks = jax.random.split(key, 8)
        B, S, D, H, E = (2, 256, 128, 64, 32)
        Hs = 2 * H
        sd = lambda *sh: 1.0 / np.sqrt(sh[-2])
        x = jax.random.normal(ks[0], (B, S, D), dtype=jnp.float32)
        Wg = jax.random.normal(ks[1], (D, E), dtype=jnp.float32) * (1.0 / np.sqrt(D))
        W1 = jax.random.normal(ks[2], (E, D, H), dtype=jnp.float32) * (1.0 / np.sqrt(D))
        W3 = jax.random.normal(ks[3], (E, D, H), dtype=jnp.float32) * (1.0 / np.sqrt(D))
        W2 = jax.random.normal(ks[4], (E, H, D), dtype=jnp.float32) * (1.0 / np.sqrt(H))
        Ws1 = jax.random.normal(ks[5], (D, Hs), dtype=jnp.float32) * (1.0 / np.sqrt(D))
        Ws3 = jax.random.normal(ks[6], (D, Hs), dtype=jnp.float32) * (1.0 / np.sqrt(D))
        Ws2 = jax.random.normal(ks[7], (Hs, D), dtype=jnp.float32) * (1.0 / np.sqrt(Hs))
        return {'x': x, 'Wg': Wg, 'W1': W1, 'W2': W2, 'W3': W3, 'Ws1': Ws1, 'Ws2': Ws2, 'Ws3': Ws3}
    _L0_ffn_in = _L0_ffn_setup()
    _d = {'L0_attn_a_embeddings': _L0_attn_a_in['embeddings'], 'L0_attn_a_W_Q': _L0_attn_a_in['W_Q'], 'L0_attn_a_W_K': _L0_attn_a_in['W_K'], 'L0_attn_a_W_V': _L0_attn_a_in['W_V'], 'L0_attn_b_ln1_w': _L0_attn_b_in['ln1_w'], 'L0_attn_b_ln1_b': _L0_attn_b_in['ln1_b'], 'L0_attn_b_ln2_w': _L0_attn_b_in['ln2_w'], 'L0_attn_b_ln2_b': _L0_attn_b_in['ln2_b'], 'L0_attn_b_att_tmk': _L0_attn_b_in['att_tmk'], 'L0_attn_b_att_tmv': _L0_attn_b_in['att_tmv'], 'L0_attn_b_att_tmr': _L0_attn_b_in['att_tmr'], 'L0_attn_b_time_decay': _L0_attn_b_in['time_decay'], 'L0_attn_b_time_first': _L0_attn_b_in['time_first'], 'L0_attn_b_Wk': _L0_attn_b_in['Wk'], 'L0_attn_b_Wv': _L0_attn_b_in['Wv'], 'L0_attn_b_Wr': _L0_attn_b_in['Wr'], 'L0_attn_b_Wo': _L0_attn_b_in['Wo'], 'L0_attn_b_ffn_tmk': _L0_attn_b_in['ffn_tmk'], 'L0_attn_b_ffn_tmr': _L0_attn_b_in['ffn_tmr'], 'L0_attn_b_Wkey': _L0_attn_b_in['Wkey'], 'L0_attn_b_Wrec': _L0_attn_b_in['Wrec'], 'L0_attn_b_Wval': _L0_attn_b_in['Wval'], 'L0_ffn_Wg': _L0_ffn_in['Wg'], 'L0_ffn_W1': _L0_ffn_in['W1'], 'L0_ffn_W2': _L0_ffn_in['W2'], 'L0_ffn_W3': _L0_ffn_in['W3'], 'L0_ffn_Ws1': _L0_ffn_in['Ws1'], 'L0_ffn_Ws2': _L0_ffn_in['Ws2'], 'L0_ffn_Ws3': _L0_ffn_in['Ws3']}
    _x0 = _d['L0_attn_a_embeddings']
    _d['L0_attn_a_embeddings'] = jax.random.normal(jax.random.fold_in(jax.random.key(seed), 1), (8, 512, 128), dtype=_x0.dtype)
    del _x0
    return _d

def reference(L0_attn_a_embeddings, L0_attn_a_W_Q, L0_attn_a_W_K, L0_attn_a_W_V, L0_attn_b_ln1_w, L0_attn_b_ln1_b, L0_attn_b_ln2_w, L0_attn_b_ln2_b, L0_attn_b_att_tmk, L0_attn_b_att_tmv, L0_attn_b_att_tmr, L0_attn_b_time_decay, L0_attn_b_time_first, L0_attn_b_Wk, L0_attn_b_Wv, L0_attn_b_Wr, L0_attn_b_Wo, L0_attn_b_ffn_tmk, L0_attn_b_ffn_tmr, L0_attn_b_Wkey, L0_attn_b_Wrec, L0_attn_b_Wval, L0_ffn_Wg, L0_ffn_W1, L0_ffn_W2, L0_ffn_W3, L0_ffn_Ws1, L0_ffn_Ws2, L0_ffn_Ws3):

    def _L0_attn_a_ref(embeddings, W_Q, W_K, W_V):
        import jax, jax.numpy as jnp
        import numpy as np
        B, S, D = (4, 256, 128)

        def _xavier(key, shape):
            bound = float(np.sqrt(6.0 / (shape[0] + shape[1])))
            return jax.random.uniform(key, shape, dtype=jnp.float32, minval=-bound, maxval=bound)
        _, seq_len, d = embeddings.shape
        Q = embeddings @ W_Q
        K = embeddings @ W_K
        V = embeddings @ W_V
        scale = 1.0 / jnp.sqrt(jnp.float32(d))
        scores = jnp.einsum('bqd,bkd->bqk', Q, K) * scale
        causal = jnp.tril(jnp.ones((seq_len, seq_len), dtype=bool))
        scores = jnp.where(causal[None, :, :], scores, -jnp.inf)
        probs = jax.nn.softmax(scores, axis=-1)
        return jnp.einsum('bqk,bkd->bqd', probs, V)

    def _L0_attn_b_ref(x, ln1_w, ln1_b, ln2_w, ln2_b, att_tmk, att_tmv, att_tmr, time_decay, time_first, Wk, Wv, Wr, Wo, ffn_tmk, ffn_tmr, Wkey, Wrec, Wval):
        import jax, jax.numpy as jnp
        import numpy as np
        import math
        B, T, C = (8, 256, 128)
        DIM_ATT, DIM_FFN = (128, 512)
        N_LAYER, LAYER_ID = (12, 1)
        EPS = 1e-05

        def layer_norm(x, w, b):
            mu = jnp.mean(x, axis=-1, keepdims=True)
            var = jnp.mean(jnp.square(x - mu), axis=-1, keepdims=True)
            return (x - mu) * jax.lax.rsqrt(var + EPS) * w + b

        def time_shift(x):
            return jnp.pad(x, ((0, 0), (1, 0), (0, 0)))[:, :-1, :]

        def wkv(time_decay, time_first, k, v):
            w = -jnp.exp(time_decay)
            u = time_first

            def step(carry, kv_t):
                aa, bb, pp = carry
                kt, vt = kv_t
                ww = u + kt
                qq = jnp.maximum(pp, ww)
                e1 = jnp.exp(pp - qq)
                e2 = jnp.exp(ww - qq)
                y = (e1 * aa + e2 * vt) / (e1 * bb + e2)
                ww2 = pp + w
                qq2 = jnp.maximum(ww2, kt)
                e1b = jnp.exp(ww2 - qq2)
                e2b = jnp.exp(kt - qq2)
                return ((e1b * aa + e2b * vt, e1b * bb + e2b, qq2), y)
            init = (jnp.zeros_like(k[:, 0]), jnp.zeros_like(k[:, 0]), jnp.full_like(k[:, 0], -1e+38))
            kT = jnp.swapaxes(k, 0, 1)
            vT = jnp.swapaxes(v, 0, 1)
            _, yT = jax.lax.scan(step, init, (kT, vT))
            return jnp.swapaxes(yT, 0, 1)
        h = layer_norm(x, ln1_w, ln1_b)
        hh = time_shift(h)
        xk = h * att_tmk + hh * (1 - att_tmk)
        xv = h * att_tmv + hh * (1 - att_tmv)
        xr = h * att_tmr + hh * (1 - att_tmr)
        k = xk @ Wk.T
        v = xv @ Wv.T
        sr = jax.nn.sigmoid(xr @ Wr.T)
        rwkv = sr * wkv(time_decay, time_first, k, v)
        x = x + rwkv @ Wo.T
        h = layer_norm(x, ln2_w, ln2_b)
        hh = time_shift(h)
        xk = h * ffn_tmk + hh * (1 - ffn_tmk)
        xr = h * ffn_tmr + hh * (1 - ffn_tmr)
        kk = jnp.square(jax.nn.relu(xk @ Wkey.T))
        kv = kk @ Wval.T
        x = x + jax.nn.sigmoid(xr @ Wrec.T) * kv
        return x

    def _L0_ffn_ref(x, Wg, W1, W2, W3, Ws1, Ws2, Ws3):
        import jax, jax.numpy as jnp
        import numpy as np
        TOP_K = 4
        CAP_FACTOR = 4

        def swiglu(x, w1, w2, w3):
            return jax.nn.silu(x @ w1) * (x @ w3) @ w2
        B, S, D = x.shape
        E = Wg.shape[1]
        T = B * S
        xf = x.reshape(T, D)
        scores = jax.nn.softmax(xf @ Wg, axis=-1)
        weights, indices = jax.lax.top_k(scores, TOP_K)
        P = T * TOP_K
        pair_expert = indices.reshape(-1)
        pair_token = jnp.repeat(jnp.arange(T), TOP_K)
        pair_weight = weights.reshape(-1).astype(xf.dtype)
        C = CAP_FACTOR * P // E
        y = jnp.zeros_like(xf)
        for e in range(E):
            pos = jnp.nonzero(pair_expert == e, size=C, fill_value=P)[0]
            valid = pos < P
            safe = jnp.minimum(pos, P - 1)
            tok = jnp.where(valid, pair_token[safe], 0)
            w = jnp.where(valid, pair_weight[safe], 0.0)
            xg = xf[tok]
            out = swiglu(xg, W1[e], W2[e], W3[e]) * w[:, None]
            y = y.at[tok].add(out)
        z = swiglu(xf, Ws1, Ws2, Ws3)
        return (y + z).reshape(B, S, D)
    x = L0_attn_a_embeddings
    x = x + _L0_attn_a_ref(_layernorm(x, axis=-1), L0_attn_a_W_Q, L0_attn_a_W_K, L0_attn_a_W_V)
    x = x + _L0_ffn_ref(_layernorm(x, axis=-1), L0_ffn_Wg, L0_ffn_W1, L0_ffn_W2, L0_ffn_W3, L0_ffn_Ws1, L0_ffn_Ws2, L0_ffn_Ws3)
    x = x + _L0_attn_b_ref(_layernorm(x, axis=-1), L0_attn_b_ln1_w, L0_attn_b_ln1_b, L0_attn_b_ln2_w, L0_attn_b_ln2_b, L0_attn_b_att_tmk, L0_attn_b_att_tmv, L0_attn_b_att_tmr, L0_attn_b_time_decay, L0_attn_b_time_first, L0_attn_b_Wk, L0_attn_b_Wv, L0_attn_b_Wr, L0_attn_b_Wo, L0_attn_b_ffn_tmk, L0_attn_b_ffn_tmr, L0_attn_b_Wkey, L0_attn_b_Wrec, L0_attn_b_Wval)
    x = x + _L0_ffn_ref(_layernorm(x, axis=-1), L0_ffn_Wg, L0_ffn_W1, L0_ffn_W2, L0_ffn_W3, L0_ffn_Ws1, L0_ffn_Ws2, L0_ffn_Ws3)
    return x

_drawn_inputs = setup_inputs


def setup_inputs(seed=0):
    import zlib

    import numpy as np

    out = dict(_drawn_inputs(seed))
    spreads = {'L0_attn_b_ln1_w': (1.0, 0.2),
     'L0_attn_b_ln1_b': (0.0, 0.1),
     'L0_attn_b_ln2_w': (1.0, 0.2),
     'L0_attn_b_ln2_b': (0.0, 0.268)}
    factors = {'L0_attn_b_time_first': 104.032}
    for name, (base, spread) in spreads.items():
        noise = np.random.default_rng([zlib.crc32(name.encode()), seed]).standard_normal(out[name].shape)
        drawn = base * np.exp(spread * noise) if base else spread * noise
        out[name] = jnp.asarray(drawn.astype(out[name].dtype))
    for name, factor in factors.items():
        out[name] = (out[name] * factor).astype(out[name].dtype)
    return out
```

```python
from contextlib import ExitStack

import concourse.bass as bass
from concourse import mybir

ALU = mybir.AluOpType
ACT = mybir.ActivationFunctionType
AX_X = mybir.AxisListType.X
F32 = mybir.dt.float32
BF16 = mybir.dt.bfloat16

P = 128
B = 8
S = 512
D = 128
T = S // P
E = 32
H = 64
TOP_K = 4
CAPACITY = 4 * (B * S * TOP_K) // E
PAIRS = E * H // P
UNITS = PAIRS + 1
GROUPS = 4
GP = PAIRS // GROUPS
FB = 4
EPS = 1e-5
SCALE = 1.0 / float(D) ** 0.5
MASKED = -1.0e30
NEVER = -1.0e38
BASE = 1

LN1_W, LN1_B, LN2_W, LN2_B, MIX_K, MIX_V, MIX_R, DECAY, FIRST, FMIX_K, FMIX_R = range(11)
M_K, M_V, M_R, M_O, M_REC, M_S1, M_S3, M_S2, M_KEY, M_VAL = 0, 1, 2, 3, 4, 5, 6, 7, 8, 12
N_MATS = 16


def hybrid_kernel(nc, x_in, att_mats, mats, vecs, w_gate, w1_in, w3_in, w2_in, x_out):
    with ExitStack() as ctx:
        def sb(name, shape, dt=F32):
            return ctx.enter_context(nc.sbuf_tensor(name, shape, dt))

        def bank(name, dt=F32):
            return ctx.enter_context(nc.psum_tensor(name, [P, 512], dt))

        def sem(name):
            return ctx.enter_context(nc.semaphore(name))

        x_sb = sb("x_sb", [P, B, T, D])
        am = sb("am", [P, 3, D])
        mt = sb("mt", [P, N_MATS, D])
        vec = sb("vec", [P, 11])
        wg = sb("wg", [P, E])
        w1 = sb("w1", [P, PAIRS, P])
        w3 = sb("w3", [P, PAIRS, P])
        w2 = sb("w2", [P, PAIRS, P])
        qk_m = sb("qk_m", [P, D])
        ident = sb("ident", [P, P])
        ident_b = sb("ident_b", [P, P], BF16)
        causal_b = sb("causal_b", [P, P], BF16)
        tri_b = sb("tri_b", [P, P], BF16)
        ones_b = sb("ones_b", [P, P], BF16)
        minus_half = sb("minus_half", [P, 2 * T])
        half = sb("half", [P, 1])
        decay = sb("decay", [P, 1])

        a_st = sb("a_st", [P, T, 6])
        a_mv = sb("a_mv", [P, T, 2])
        a_ve = sb("a_ve", [P, 2 * T])
        a_rs = sb("a_rs", [P, 2 * T])
        a_xn = sb("a_xn", [P, T, D])
        a_xT = sb("a_xT", [P, S])
        a_g = sb("a_g", [P, S])
        a_v = sb("a_v", [P, T, D])
        a_p = sb("a_p", [P, S])
        a_pT = sb("a_pT", [P, S])
        a_mx = sb("a_mx", [P, T])
        a_nm = sb("a_nm", [P, T])
        a_sum = sb("a_sum", [P, T])
        a_ri = sb("a_ri", [P, T])

        r_st = sb("r_st", [P, T, 6])
        r_mv = sb("r_mv", [P, T, 2])
        r_ve = sb("r_ve", [P, T])
        r_rs = sb("r_rs", [P, T])
        r_xn = sb("r_xn", [P, T, D])
        r_xT = sb("r_xT", [P, S])
        r_mx = sb("r_mx", [P, T])
        r_lg = sb("r_lg", [P, T, E])
        r_ex = sb("r_ex", [P, T, E])
        r_sum = sb("r_sum", [P, T])
        r_ri = sb("r_ri", [P, T])
        r_p = sb("r_p", [P, T, E + TOP_K])
        r_top = sb("r_top", [P, T, 8])
        r_rep = sb("r_rep", [P, T, E + TOP_K])
        r_sel = sb("r_sel", [P, T, E], BF16)
        r_ws = sb("r_ws", [P, T, E])
        r_pos = sb("r_pos", [P, T, E])
        r_w = sb("r_w", [P, T, E])
        r_carry = sb("r_carry", [P, E])
        r_wT = sb("r_wT", [E, S])

        m_xT = sb("m_xT", [P, B, S])
        m_wb = sb("m_wb", [P, PAIRS, S])
        m_th = sb("m_th", [P, 2, S])
        m_u = sb("m_u", [P, 2, S])
        m_v = sb("m_v", [P, 2, S])
        m_h = sb("m_h", [P, 3, S])
        m_y = sb("m_y", [P, S])

        t_u = sb("t_u", [P, T, D])
        t_hn = sb("t_hn", [P, T, D])
        t_h = sb("t_h", [P, 1 + S])
        t_d = sb("t_d", [P, S])
        t_xk = sb("t_xk", [P, S])
        t_xv = sb("t_xv", [P, S])
        t_xr = sb("t_xr", [P, S])
        t_k = sb("t_k", [P, S])
        t_v = sb("t_v", [P, S])
        t_r = sb("t_r", [P, S])
        t_pp = sb("t_pp", [P, 1 + S])
        t_aa = sb("t_aa", [P, 1 + S])
        t_bb = sb("t_bb", [P, 1 + S])
        t_qq = sb("t_qq", [P, S])
        t_ea = sb("t_ea", [P, 2, S])
        t_eb = sb("t_eb", [P, 2, S])
        t_ev = sb("t_ev", [P, S])
        t_n1 = sb("t_n1", [P, S])
        t_n2 = sb("t_n2", [P, S])
        t_d1 = sb("t_d1", [P, S])
        t_ri = sb("t_ri", [P, S])
        t_u2 = sb("t_u2", [P, T, D])
        t_rk = sb("t_rk", [P, 2, S])
        t_kk = sb("t_kk", [P, FB, S])
        t_tr = sb("t_tr", [P, S])
        t_g = sb("t_g", [P, S])

        pa = [bank("pa0"), bank("pa1")]
        pb = [bank("pb0"), bank("pb1")]
        py = bank("py")
        pq = bank("pq")
        pu, pv = bank("pu"), bank("pv")

        w_scratch = nc.dram_tensor("w_scratch", [2 * B, GROUPS, GP, 2, S], F32, kind="Internal").ap()

        names = (
            "in_x0 in_x1 in_xr in_am in_vec in_wg in_w1 in_w3 in_w2 in_mt c_pool c_dve c_dec0 c_dec c_qkm_ps c_qkm "
            "a_stats a_mvs a_vedone a_rstd a_xn a_tr a_xT a_gps a_vps a_g a_v a_s a_mx a_nm a_exp a_pT a_pTs a_o a_ri a_add "
            "r_stats r_mvs r_vedone r_rstd r_xn r_tr r_xT m_xT r_lgps r_mx r_lg r_ex r_sum r_ri r_p r_top r_pad r_rep "
            "r_sel r_ws r_cnt r_pos r_w r_carry r_wTps r_wT w_out "
            "m_a m_b m_th m_u m_v m_h m_y m_ys m_yT m_x "
            "t_stats t_mvs t_ve t_rstd t_hn t_tr t_h t_d t_xk t_kps t_vps t_rps t_k t_v t_r t_pp t_a0 t_a1 t_qq t_b0 t_b1 "
            "t_expa t_expb t_ev t_n2 t_aa t_bb t_n1 t_d1 t_den t_num t_ri t_y t_rw t_ops t_u t_u2 t_xu "
            "f_stats f_mvs f_ve f_rstd f_hn f_tr f_h f_d f_xk f_key f_rk f_kk f_rec f_tr2 f_kv f_g f_x "
            "out_done stats_seen"
        ).split()
        sig = {n: sem("s_" + n) for n in names}
        wb_in = [sem(f"s_wb_in{j}") for j in range(GROUPS)]

        def wait(eng, name, value):
            if not (isinstance(value, int) and value <= 0):
                eng.wait_ge(sig[name], value)

        def done(n):
            return n + BASE

        block = ctx.enter_context(nc.Block())
        xv = x_in.rearrange("b (t p) d -> b p t d", p=P)
        ov = x_out.rearrange("b (t p) d -> b p t d", p=P)

        def chunk(c):
            return x_sb[:, c, :, :]

        def wide(ap):
            return ap.rearrange("p t d -> p (t d)")

        @block.sync
        def _(sp):
            sp.dma_start(chunk(0), xv[0]).then_inc(sig["in_x0"], 16)
            sp.dma_start(chunk(1), xv[1]).then_inc(sig["in_x1"], 16)
            sp.dma_start(wg[:, :], w_gate).then_inc(sig["in_wg"], 16)
            sp.dma_start(w1[:, :, :], w1_in).then_inc(sig["in_w1"], 16)
            sp.dma_start(w3[:, :, :], w3_in).then_inc(sig["in_w3"], 16)
            sp.dma_start(mt[:, :, :], mats).then_inc(sig["in_mt"], 16)
            sp.dma_start(w2[:, :, :], w2_in).then_inc(sig["in_w2"], 16)
            for c in range(2, B):
                sp.dma_start(chunk(c), xv[c]).then_inc(sig["in_xr"], 16)
            for name in ("m_u", "m_v", "m_h", "m_y", "m_x"):
                sp.sem_inc(sig[name], BASE)

            def spread_weights(q):
                sp.wait_ge(sig["r_wT"], q + 1)
                sp.dma_start(w_scratch[q].rearrange("j a h s -> (j a h) s"), r_wT[:, :]).then_inc(sig["w_out"], 16)
                sp.wait_ge(sig["w_out"], 16 * q + 16)
                for j in range(GROUPS):
                    if not (isinstance(q, int) and q == 0):
                        sp.wait_ge(sig["m_h"], done(UNITS * (q - 1) + GP * (j + 1)))
                    for h in range(2):
                        sp.dma_start(m_wb[H * h:H * (h + 1), GP * j:GP * (j + 1), :],
                                     w_scratch[q, j, :, h, :].partition_broadcast(H)).then_inc(wb_in[j], 16)

            def store(c):
                sp.wait_ge(sig["m_x"], done(B + c + 1))
                sp.dma_start(ov[c], chunk(c)).then_inc(sig["out_done"], 16)

            spread_weights(0)
            with sp.Fori(1, B + 2) as q:
                spread_weights(q)
            with sp.Fori(B + 2, 2 * B) as q:
                spread_weights(q)
                store(q - (B + 2))
            store(B - 2)
            store(B - 1)
            sp.wait_ge(sig["out_done"], 16 * B)

        @block.gpsimd
        def _(pool):
            pool.memset(ident[:, :], 0.0).then_inc(sig["c_pool"], 1)
            pool.memset(ident_b[:, :], 0.0).then_inc(sig["c_pool"], 1)
            pool.memset(causal_b[:, :], 0.0).then_inc(sig["c_pool"], 1)
            pool.memset(tri_b[:, :], 1.0).then_inc(sig["c_pool"], 1)
            pool.memset(ones_b[:, :], 1.0).then_inc(sig["c_pool"], 1)
            pool.memset(minus_half[:, :], -0.5).then_inc(sig["c_pool"], 1)
            pool.memset(half[:, :], 0.5).then_inc(sig["c_pool"], 1)
            pool.wait_ge(sig["c_pool"], 7)
            for m in (ident, ident_b):
                pool.affine_select(out=m[:, :], in_=m[:, :], compare_op=ALU.not_equal, fill=1.0, base=0,
                                   pattern=[[-1, P]], channel_multiplier=1).then_inc(sig["c_pool"], 1)
            pool.affine_select(out=causal_b[:, :], in_=causal_b[:, :], compare_op=ALU.is_ge, fill=MASKED, base=0,
                               pattern=[[-1, P]], channel_multiplier=1).then_inc(sig["c_pool"], 1)
            pool.affine_select(out=tri_b[:, :], in_=tri_b[:, :], compare_op=ALU.is_ge, fill=0.0, base=0,
                               pattern=[[1, P]], channel_multiplier=-1).then_inc(sig["c_pool"], 1)

            def rsqrt(out, in_, ready, n, signal):
                pool.wait_ge(sig[ready], n)
                pool.tensor_tensor(out, in_, minus_half[:, 0:out.shape[1]], ALU.pow).then_inc(sig[signal], 1)

            def unit(g, p):
                k = UNITS * g + p
                if p < PAIRS and p % GP == 0:
                    pool.wait_ge(wb_in[p // GP], 32 * g + 32)
                pool.wait_ge(sig["m_v"], done(k + 1))
                pool.wait_ge(sig["m_y"], done(k - 1) if p == 1 else done(k) if p == 0 else done(k - 2))
                if p < PAIRS:
                    pool.tensor_tensor(m_h[:, p % 3, :], m_v[:, p % 2, :], m_wb[:, p, :], ALU.mult).then_inc(sig["m_h"], 1)
                else:
                    pool.tensor_tensor(m_h[:, p % 3, :], m_v[:, p % 2, :], half[:, 0:1].to_broadcast([P, S]),
                                       ALU.mult).then_inc(sig["m_h"], 1)

            def rwkv_step(m, slot):
                if slot == 0:
                    rsqrt(a_rs[:, :], a_ve[:, :], "t_ve", 2 * m + 2, "t_rstd")
                if slot == 3:
                    pool.wait_ge(sig["t_h"], m + 1)
                    pool.tensor_tensor(t_d[:, :], t_h[:, 1:1 + S], t_h[:, 0:S], ALU.subtract).then_inc(sig["t_d"], 1)
                if slot == 6:
                    pool.wait_ge(sig["t_pp"], m + 1)
                    pool.tensor_tensor(t_ea[:, 1, :], t_k[:, :], t_pp[:, 1:1 + S], ALU.subtract).then_inc(sig["t_a1"], 1)
                    pool.wait_ge(sig["t_qq"], m + 1)
                    pool.tensor_tensor(t_eb[:, 0, :], t_pp[:, 0:S], t_qq[:, :], ALU.subtract).then_inc(sig["t_b0"], 1)
                if slot == 7:
                    pool.wait_ge(sig["t_expa"], m + 1)
                    pool.tensor_tensor(t_ev[:, :], t_ea[:, 1, :], t_v[:, :], ALU.mult).then_inc(sig["t_ev"], 1)
                    pool.wait_ge(sig["t_expb"], m + 1)
                    pool.tensor_tensor(t_n2[:, :], t_eb[:, 1, :], t_v[:, :], ALU.mult).then_inc(sig["t_n2"], 1)
                if slot == 12:
                    rsqrt(a_rs[:, 0:T], a_ve[:, 0:T], "f_ve", m + 1, "f_rstd")
                if slot == 14:
                    pool.wait_ge(sig["f_h"], m + 1)
                    pool.tensor_tensor(t_d[:, :], t_h[:, 1:1 + S], t_h[:, 0:S], ALU.subtract).then_inc(sig["f_d"], 1)
                if slot == 17:
                    for j in range(FB):
                        pool.wait_ge(sig["f_rk"], FB * m + j + 1)
                        pool.tensor_tensor(t_kk[:, j, :], t_rk[:, j % 2, :], t_rk[:, j % 2, :],
                                           ALU.mult).then_inc(sig["f_kk"], 1)

            def iteration(g=None, bb=None, att=None, rwkv=None, pro=None, pb_=None):
                for slot in range(UNITS + 1):
                    if g is not None and slot < UNITS:
                        unit(g, slot)
                    if att is not None and slot == 0:
                        rsqrt(a_rs[:, 0:T], a_ve[:, 0:T], "a_vedone", att + 1, "a_rstd")
                    if pro is not None and slot == 1:
                        rsqrt(r_rs[:, :], r_ve[:, :], "r_vedone", pro + 1, "r_rstd")
                    if rwkv is not None:
                        rwkv_step(rwkv, slot)

            iteration(att=0)
            iteration(att=1, pro=0, pb_=0)
            with pool.Fori(0, B - 2) as g:
                iteration(g, g, att=g + 2, pro=g + 1, pb_=g + 1)
            iteration(B - 2, B - 2, rwkv=0, pro=B - 1, pb_=B - 1)
            iteration(B - 1, B - 1, rwkv=1, pro=B, pb_=0)
            with pool.Fori(B, 2 * B - 2) as g:
                iteration(g, g - B, rwkv=g - (B - 2), pro=g + 1, pb_=g - (B - 1))
            iteration(2 * B - 2, B - 2, pro=2 * B - 1, pb_=B - 1)
            iteration(2 * B - 1, B - 1)

        @block.scalar
        def _(act):
            act.dma_start(am[:, :, :], att_mats).then_inc(sig["in_am"], 16)
            act.dma_start(vec[:, :], vecs).then_inc(sig["in_vec"], 16)
            act.wait_ge(sig["in_vec"], 16)
            act.activation(decay[:, :], vec[:, DECAY:DECAY + 1], ACT.Exp).then_inc(sig["c_dec0"], 1)
            act.wait_ge(sig["c_qkm_ps"], 1)
            act.activation(qk_m[:, :], pv[:, 0:D], ACT.Copy).then_inc(sig["c_qkm"], 1)

            def unit(g, p):
                k = UNITS * g + p
                act.wait_ge(sig["m_a"], k + 1)
                act.wait_ge(sig["m_u"], done(k) if p == 0 else done(k - 1))
                act.activation(m_th[:, p % 2, :], pa[p % 2][:, :], ACT.Tanh, scale=0.5).then_inc(sig["m_th"], 1)

            def att_step(n, slot):
                if slot == 3:
                    act.wait_ge(sig["a_tr"], n + 1)
                    act.activation(a_xT[:, :], pu[:, :], ACT.Copy).then_inc(sig["a_xT"], 1)
                if slot == 5:
                    act.wait_ge(sig["a_gps"], n + 1)
                    act.activation(a_g[:, :], pv[:, :], ACT.Copy).then_inc(sig["a_g"], 1)
                    act.wait_ge(sig["a_vps"], n + 1)
                    act.activation(wide(a_v[:, :, :]), pu[:, :], ACT.Copy).then_inc(sig["a_v"], 1)
                if slot == 7:
                    att_exp(n, 0, (0, 1), (0, P))
                if slot == 9:
                    turn_probs(n, 0, 3)
                    att_exp(n, 1, (2,), (0,))
                if slot == 12:
                    turn_probs(n, 1, 3)
                    att_exp(n, 2, (3,), (0,))
                if slot == 14:
                    turn_probs(n, 2, 4)

            def att_exp(n, i, tiles, at):
                act.wait_ge(sig["a_nm"], 3 * n + i + 1)
                wait(act, "a_pT", 3 * n + i)
                for t, o in zip(tiles, at):
                    ins = act.activation(a_p[:, o:o + P * (t + 1)], pv[:, o:o + P * (t + 1)], ACT.Exp,
                                         bias=a_nm[:, t:t + 1], scale=SCALE, accum_out=a_sum[:, t:t + 1])
                ins.then_inc(sig["a_exp"], 1)

            def turn_probs(n, i, blocks):
                act.wait_ge(sig["a_pT"], 3 * n + i + 1)
                act.activation(a_pT[:, 0:P * blocks], pu[:, 0:P * blocks], ACT.Copy).then_inc(sig["a_pTs"], 1)

            def pro_step(q, c, slot):
                if slot == 4:
                    act.wait_ge(sig["r_tr"], q + 1)
                    act.activation(r_xT[:, :], pq[:, :], ACT.Copy).then_inc(sig["r_xT"], 1)
                    act.activation(m_xT[:, c, :], pq[:, :], ACT.Copy).then_inc(sig["m_xT"], 1)
                if slot == 7:
                    act.wait_ge(sig["r_lg"], q + 1)
                    act.activation(wide(r_ex[:, :, :]), wide(r_lg[:, :, :]), ACT.Exp).then_inc(sig["r_ex"], 1)
                if slot == 13:
                    act.wait_ge(sig["r_wTps"], q + 1)
                    wait(act, "w_out", 16 * q)
                    act.activation(r_wT[:, :], pq[0:E, :], ACT.Copy).then_inc(sig["r_wT"], 1)

            def rwkv_step(m, slot):
                if slot == 3:
                    act.wait_ge(sig["t_tr"], m + 1)
                    act.activation(t_h[:, 1:1 + S], pu[:, :], ACT.Identity, bias=vec[:, LN1_B:LN1_B + 1],
                                   scale=vec[:, LN1_W:LN1_W + 1]).then_inc(sig["t_h"], 1)
                if slot == 6:
                    act.wait_ge(sig["t_kps"], m + 1)
                    act.activation(t_k[:, :], pv[:, :], ACT.Copy).then_inc(sig["t_k"], 1)
                    act.wait_ge(sig["t_vps"], m + 1)
                    act.activation(t_v[:, :], pu[:, :], ACT.Copy).then_inc(sig["t_v"], 1)
                    act.wait_ge(sig["t_rps"], m + 1)
                    act.activation(t_r[:, :], pv[:, :], ACT.Tanh, scale=0.5).then_inc(sig["t_r"], 1)
                if slot == 7:
                    act.wait_ge(sig["t_a0"], m + 1)
                    act.wait_ge(sig["t_a1"], m + 1)
                    act.activation(wide(t_ea[:, :, :]), wide(t_ea[:, :, :]), ACT.Exp).then_inc(sig["t_expa"], 1)
                    act.wait_ge(sig["t_b0"], m + 1)
                    act.wait_ge(sig["t_b1"], m + 1)
                    act.activation(wide(t_eb[:, :, :]), wide(t_eb[:, :, :]), ACT.Exp).then_inc(sig["t_expb"], 1)
                if slot == 14:
                    act.wait_ge(sig["f_tr"], m + 1)
                    act.activation(t_h[:, 1:1 + S], pu[:, :], ACT.Identity, bias=vec[:, LN2_B:LN2_B + 1],
                                   scale=vec[:, LN2_W:LN2_W + 1]).then_inc(sig["f_h"], 1)
                if slot == 16:
                    relu(m, 0, pv)
                    act.wait_ge(sig["f_rec"], m + 1)
                    act.activation(t_tr[:, :], pu[:, :], ACT.Tanh, scale=0.5).then_inc(sig["f_tr2"], 1)
                if slot == 17:
                    relu(m, 1, pv)
                    relu(m, 2, pu)
                    relu(m, 3, pv)

            def relu(m, j, ps):
                act.wait_ge(sig["f_key"], FB * m + j + 1)
                wait(act, "f_kk", FB * m + j - 1)
                act.activation(t_rk[:, j % 2, :], ps[:, :], ACT.Relu).then_inc(sig["f_rk"], 1)

            def out_copy(g):
                act.wait_ge(sig["m_y"], done(UNITS * (g + 1)))
                act.activation(m_y[:, :], py[:, :], ACT.Copy).then_inc(sig["m_ys"], 1)

            def iteration(g=None, bb=None, att=None, rwkv=None, pro=None, pb_=None):
                for slot in range(UNITS + 1):
                    if g is not None and slot < UNITS:
                        unit(g, slot)
                    if att is not None:
                        att_step(att, slot)
                    if rwkv is not None:
                        rwkv_step(rwkv, slot)
                    if pro is not None:
                        pro_step(pro, pb_, slot)
                if g is not None:
                    out_copy(g)

            iteration(att=0)
            iteration(att=1, pro=0, pb_=0)
            with act.Fori(0, B - 2) as g:
                iteration(g, g, att=g + 2, pro=g + 1, pb_=g + 1)
            iteration(B - 2, B - 2, rwkv=0, pro=B - 1, pb_=B - 1)
            iteration(B - 1, B - 1, rwkv=1, pro=B, pb_=0)
            with act.Fori(B, 2 * B - 2) as g:
                iteration(g, g - B, rwkv=g - (B - 2), pro=g + 1, pb_=g - (B - 1))
            iteration(2 * B - 2, B - 2, pro=2 * B - 1, pb_=B - 1)
            iteration(2 * B - 1, B - 1)

        @block.tensor
        def _(pe):
            pe.wait_ge(sig["c_pool"], 11)
            pe.wait_ge(sig["in_am"], 16)
            pe.matmul(pv[:, 0:D], am[:, 0, :], am[:, 1, :], start=True, stop=True).then_inc(sig["c_qkm_ps"], 1)

            def turn(ps, src, signal):
                for t in range(T):
                    ins = pe.transpose(ps[:, P * t:P * (t + 1)], src[:, t, :], ident[:, :])
                ins.then_inc(sig[signal], 1)

            def unit(g, bb, p):
                k = UNITS * g + p
                if p == 0:
                    pe.wait_ge(sig["m_xT"], g + 1)
                pe.wait_ge(sig["m_v"], done(k) if p == 0 else done(k - 1))
                up = w1[:, p, :] if p < PAIRS else mt[:, M_S1, :]
                gate = w3[:, p, :] if p < PAIRS else mt[:, M_S3, :]
                pe.matmul(pa[p % 2][:, :], up, m_xT[:, bb, :], start=True, stop=True).then_inc(sig["m_a"], 1)
                pe.matmul(pb[p % 2][:, :], gate, m_xT[:, bb, :], start=True, stop=True).then_inc(sig["m_b"], 1)

            def out_product(g, p):
                k = UNITS * g + p
                if p == 0:
                    pe.wait_ge(sig["m_x"], done(g))
                pe.wait_ge(sig["m_h"], done(k + 1))
                down = w2[:, p, :] if p < PAIRS else mt[:, M_S2, :]
                pe.matmul(py[:, :], down, m_h[:, p % 3, :], start=(p == 0), stop=(p == UNITS - 1)).then_inc(sig["m_y"], 1)

            def out_turn(g):
                pe.wait_ge(sig["m_ys"], g + 1)
                for t in range(T):
                    ins = pe.transpose(py[:, P * t:P * (t + 1)], m_y[:, P * t:P * (t + 1)], ident[:, :])
                ins.then_inc(sig["m_yT"], 1)

            def att_step(n, slot):
                if slot == 2:
                    pe.wait_ge(sig["a_xn"], n + 1)
                    turn(pu, a_xn, "a_tr")
                if slot == 4:
                    pe.wait_ge(sig["c_qkm"], 1)
                    pe.wait_ge(sig["a_xT"], n + 1)
                    pe.matmul(pv[:, :], qk_m[:, :], a_xT[:, :], start=True, stop=True).then_inc(sig["a_gps"], 1)
                    for t in range(T):
                        ins = pe.matmul(pu[:, P * t:P * (t + 1)], a_xT[:, P * t:P * (t + 1)], am[:, 2, :],
                                        start=True, stop=True)
                    ins.then_inc(sig["a_vps"], 1)
                if slot == 6:
                    pe.wait_ge(sig["a_g"], n + 1)
                    scores(n, (0, 1), (0, P))
                if slot == 8:
                    pe.wait_ge(sig["a_v"], n + 1)
                    probs(n, 0, 3)
                    scores(n, (2,), (0,))
                if slot == 10:
                    values(n, 0, (0, 1), (0, P))
                if slot == 11:
                    probs(n, 1, 3)
                    scores(n, (3,), (0,))
                if slot == 13:
                    values(n, 1, (2,), (0,))
                if slot == 14:
                    probs(n, 2, 4)
                if slot == 15:
                    values(n, 2, (3,), (0,))

            def scores(n, tiles, at):
                for t, o in zip(tiles, at):
                    q = slice(P * t, P * (t + 1))
                    pe.matmul(pv[:, o:o + P * (t + 1)], a_g[:, q], a_xT[:, 0:P * (t + 1)], start=True, stop=False)
                    ins = pe.matmul(pv[:, o + P * t:o + P * (t + 1)], ident_b[:, :], causal_b[:, :],
                                    start=False, stop=True)
                ins.then_inc(sig["a_s"], 1)

            def probs(n, i, blocks):
                pe.wait_ge(sig["a_exp"], 3 * n + i + 1)
                wait(pe, "a_add", 3 * n + i)
                for j in range(blocks):
                    ins = pe.transpose(pu[:, P * j:P * (j + 1)], a_p[:, P * j:P * (j + 1)], ident[:, :])
                ins.then_inc(sig["a_pT"], 1)

            def values(n, i, tiles, at):
                pe.wait_ge(sig["a_pTs"], 3 * n + i + 1)
                for t, o in zip(tiles, at):
                    for j in range(t + 1):
                        ins = pe.matmul(pu[:, P * t:P * (t + 1)], a_pT[:, o + P * j:o + P * (j + 1)], a_v[:, j, :],
                                        start=(j == 0), stop=(j == t))
                ins.then_inc(sig["a_o"], 1)

            def pro_step(q, slot):
                if slot == 3:
                    pe.wait_ge(sig["r_xn"], q + 1)
                    wait(pe, "r_wT", q)
                    turn(pq, r_xn, "r_tr")
                if slot == 5:
                    pe.wait_ge(sig["m_xT"], q + 1)
                    for t in range(T):
                        ins = pe.matmul(pq[:, E * t:E * (t + 1)], r_xT[:, P * t:P * (t + 1)], wg[:, :],
                                        start=True, stop=True)
                    ins.then_inc(sig["r_lgps"], 1)
                if slot == 10:
                    pe.wait_ge(sig["r_sel"], q + 1)
                    for t in range(T):
                        later = T - t
                        pe.matmul(pq[:, E * (t + 1):E * (T + 1)].rearrange("p (a e) -> p a e", a=later),
                                  ones_b[:, :], r_sel[:, t:t + 1, :].broadcast_to([P, later, E]),
                                  start=(t == 0), stop=False, skip_group_check=True)
                        ins = pe.matmul(pq[:, E * t:E * (t + 1)], tri_b[:, :], r_sel[:, t, :],
                                        start=False, stop=(t == T - 1), skip_group_check=True)
                    ins.then_inc(sig["r_cnt"], 1)
                if slot == 12:
                    pe.wait_ge(sig["r_w"], q + 1)
                    pe.wait_ge(sig["r_carry"], q + 1)
                    for t in range(T):
                        ins = pe.transpose(pq[0:E, P * t:P * (t + 1)], r_w[:, t, :], ident[:, :])
                    ins.then_inc(sig["r_wTps"], 1)

            def rwkv_step(m, slot):
                if slot == 2:
                    pe.wait_ge(sig["t_hn"], m + 1)
                    turn(pu, t_hn, "t_tr")
                if slot == 5:
                    pe.wait_ge(sig["t_xk"], 3 * m + 3)
                    pe.matmul(pv[:, :], mt[:, M_K, :], t_xk[:, :], start=True, stop=True).then_inc(sig["t_kps"], 1)
                    pe.matmul(pu[:, :], mt[:, M_V, :], t_xv[:, :], start=True, stop=True).then_inc(sig["t_vps"], 1)
                if slot == 6:
                    pe.wait_ge(sig["t_k"], m + 1)
                    pe.matmul(pv[:, :], mt[:, M_R, :], t_xr[:, :], start=True, stop=True).then_inc(sig["t_rps"], 1)
                if slot == 11:
                    pe.wait_ge(sig["t_rw"], m + 1)
                    for t in range(T):
                        ins = pe.matmul(pu[:, P * t:P * (t + 1)], t_n1[:, P * t:P * (t + 1)], mt[:, M_O, :],
                                        start=True, stop=True)
                    ins.then_inc(sig["t_ops"], 1)
                if slot == 13:
                    pe.wait_ge(sig["f_hn"], m + 1)
                    turn(pu, t_hn, "f_tr")
                if slot == 15:
                    pe.wait_ge(sig["f_xk"], 2 * m + 2)
                    key(m, 0, pv)
                    for t in range(T):
                        ins = pe.matmul(pu[:, P * t:P * (t + 1)], t_xr[:, P * t:P * (t + 1)], mt[:, M_REC, :],
                                        start=True, stop=True)
                    ins.then_inc(sig["f_rec"], 1)
                if slot == 16:
                    pe.wait_ge(sig["f_rk"], FB * m + 1)
                    key(m, 1, pv)
                    pe.wait_ge(sig["f_tr2"], m + 1)
                    key(m, 2, pu)
                if slot == 17:
                    pe.wait_ge(sig["f_rk"], FB * m + 2)
                    key(m, 3, pv)
                if slot == 18:
                    pe.wait_ge(sig["f_kk"], FB * m + FB)
                    for t in range(T):
                        for j in range(FB):
                            ins = pe.matmul(pu[:, P * t:P * (t + 1)], t_kk[:, j, P * t:P * (t + 1)],
                                            mt[:, M_VAL + j, :], start=(j == 0), stop=(j == FB - 1))
                    ins.then_inc(sig["f_kv"], 1)

            def key(m, j, ps):
                pe.matmul(ps[:, :], mt[:, M_KEY + j, :], t_xk[:, :], start=True, stop=True).then_inc(sig["f_key"], 1)

            def iteration(g=None, bb=None, att=None, rwkv=None, pro=None, pb_=None):
                for slot in range(UNITS + 2):
                    if g is not None and slot < UNITS:
                        unit(g, bb, slot)
                    if g is not None and slot >= 2:
                        out_product(g, slot - 2)
                    if att is not None:
                        att_step(att, slot)
                    if rwkv is not None:
                        rwkv_step(rwkv, slot)
                    if pro is not None:
                        pro_step(pro, slot)
                if g is not None:
                    out_turn(g)

            iteration(att=0)
            pe.wait_ge(sig["in_wg"], 16)
            iteration(att=1, pro=0, pb_=0)
            for name in ("in_w1", "in_w3", "in_w2", "in_mt"):
                pe.wait_ge(sig[name], 16)
            with pe.Fori(0, B - 2) as g:
                iteration(g, g, att=g + 2, pro=g + 1, pb_=g + 1)
            iteration(B - 2, B - 2, rwkv=0, pro=B - 1, pb_=B - 1)
            iteration(B - 1, B - 1, rwkv=1, pro=B, pb_=0)
            with pe.Fori(B, 2 * B - 2) as g:
                iteration(g, g - B, rwkv=g - (B - 2), pro=g + 1, pb_=g - (B - 1))
            iteration(2 * B - 2, B - 2, pro=2 * B - 1, pb_=B - 1)
            iteration(2 * B - 1, B - 1)

        @block.vector
        def _(dve):
            for ap, value in ((r_p[:, :, E:E + TOP_K], -1.0), (r_carry[:, :], 0.0), (t_h[:, 0:1], 0.0),
                              (t_pp[:, 0:1], NEVER), (t_aa[:, 0:1], 0.0), (t_bb[:, 0:1], 0.0)):
                dve.memset(ap, value).then_inc(sig["c_dve"], 1)
            dve.wait_ge(sig["c_dve"], 6)
            dve.wait_ge(sig["c_dec0"], 1)
            dve.tensor_scalar(decay[:, :], decay[:, :], -1.0, None, ALU.mult).then_inc(sig["c_dec"], 1)

            def constants_set():
                dve.wait_ge(sig["c_dve"], 6)

            def row_stats(src, st, mv, n, s_st, s_mv):
                for t in range(T):
                    ins = dve.bn_stats(st[:, t, :], src[:, t, :])
                ins.then_inc(sig[s_st], 1)
                dve.wait_ge(sig[s_st], n + 1)
                dve.sem_inc(sig["stats_seen"], 1)
                for t in range(T):
                    ins = dve.bn_aggr(mv[:, t, :], st[:, t, :])
                ins.then_inc(sig[s_mv], 1)
                dve.wait_ge(sig[s_mv], n + 1)

            def normalise(dst, src, mv, rs, signal):
                for t in range(T):
                    ins = dve.tensor_scalar(dst[:, t, :], src[:, t, :], mv[:, t, 0:1], rs[:, t:t + 1],
                                            ALU.subtract, ALU.mult)
                ins.then_inc(sig[signal], 1)

            def unit(g, p):
                k = UNITS * g + p
                r = p % 2
                dve.wait_ge(sig["m_th"], k + 1)
                dve.scalar_tensor_tensor(out=m_u[:, r, :], in0=m_th[:, r, :], scalar=1.0, in1=pa[r][:, :],
                                         op0=ALU.add, op1=ALU.mult).then_inc(sig["m_u"], 1)
                dve.wait_ge(sig["m_b"], k + 1)
                dve.wait_ge(sig["m_u"], done(k + 1))
                dve.wait_ge(sig["m_h"], done(k) if p == 0 else done(k - 1))
                dve.tensor_tensor(m_v[:, r, :], m_u[:, r, :], pb[r][:, :], ALU.mult).then_inc(sig["m_v"], 1)

            def add_out(g, bb):
                dve.wait_ge(sig["m_yT"], g + 1)
                dve.tensor_tensor(wide(chunk(bb)), wide(chunk(bb)), py[:, :], ALU.add).then_inc(sig["m_x"], 1)

            def att_step(n, slot):
                if slot == 0:
                    if isinstance(n, int):
                        dve.wait_ge(sig["in_x0" if n == 0 else "in_x1"], 16)
                    row_stats(chunk(n), a_st, a_mv, n, "a_stats", "a_mvs")
                    dve.tensor_scalar(a_ve[:, 0:T], a_mv[:, :, 1], EPS, None, ALU.add).then_inc(sig["a_vedone"], 1)
                if slot == 1:
                    dve.wait_ge(sig["a_rstd"], n + 1)
                    normalise(a_xn, chunk(n), a_mv, a_rs, "a_xn")
                if slot == 7:
                    row_max(n, 0, (0, 1), (0, P))
                if slot == 9:
                    row_max(n, 1, (2,), (0,))
                if slot == 10:
                    add_att(n, 0, (0, 1))
                if slot == 12:
                    row_max(n, 2, (3,), (0,))
                if slot == 13:
                    add_att(n, 1, (2,))
                if slot == 15:
                    add_att(n, 2, (3,))

            def row_max(n, i, tiles, at):
                dve.wait_ge(sig["a_s"], 3 * n + i + 1)
                for t, o in zip(tiles, at):
                    ins = dve.tensor_reduce(a_mx[:, t:t + 1], pv[:, o:o + P * (t + 1)], AX_X, ALU.max)
                ins.then_inc(sig["a_mx"], 1)
                dve.wait_ge(sig["a_mx"], 3 * n + i + 1)
                a, b = tiles[0], tiles[-1] + 1
                dve.tensor_scalar(a_nm[:, a:b], a_mx[:, a:b], -SCALE, None, ALU.mult).then_inc(sig["a_nm"], 1)

            def add_att(n, i, tiles):
                a, b = tiles[0], tiles[-1] + 1
                dve.wait_ge(sig["a_exp"], 3 * n + i + 1)
                dve.reciprocal(a_ri[:, a:b], a_sum[:, a:b]).then_inc(sig["a_ri"], 1)
                dve.wait_ge(sig["a_ri"], 3 * n + i + 1)
                dve.wait_ge(sig["a_o"], 3 * n + i + 1)
                for t in tiles:
                    ins = dve.scalar_tensor_tensor(out=chunk(n)[:, t, :], in0=pu[:, P * t:P * (t + 1)],
                                                   scalar=a_ri[:, t:t + 1], in1=chunk(n)[:, t, :],
                                                   op0=ALU.mult, op1=ALU.add)
                ins.then_inc(sig["a_add"], 1)

            def pro_step(q, c, slot, layer):
                if slot == 1:
                    if layer == 0:
                        dve.wait_ge(sig["a_add"], 3 * q + 3)
                    else:
                        dve.wait_ge(sig["f_x"], 2 * (q - B) + 2)
                    row_stats(chunk(c), r_st, r_mv, q, "r_stats", "r_mvs")
                    dve.tensor_scalar(r_ve[:, :], r_mv[:, :, 1], EPS, None, ALU.add).then_inc(sig["r_vedone"], 1)
                if slot == 2:
                    dve.wait_ge(sig["r_rstd"], q + 1)
                    normalise(r_xn, chunk(c), r_mv, r_rs, "r_xn")
                if slot == 6:
                    dve.wait_ge(sig["r_lgps"], q + 1)
                    lg = pq[:, 0:T * E].rearrange("p (t e) -> p t e", t=T)
                    dve.tensor_reduce(r_mx[:, :], lg, AX_X, ALU.max).then_inc(sig["r_mx"], 1)
                    dve.wait_ge(sig["r_mx"], q + 1)
                    dve.tensor_tensor(r_lg[:, :, :], lg, r_mx[:, :].unsqueeze(2).broadcast_to([P, T, E]),
                                      ALU.subtract).then_inc(sig["r_lg"], 1)
                if slot == 8:
                    dve.wait_ge(sig["r_ex"], q + 1)
                    dve.tensor_reduce(r_sum[:, :], r_ex[:, :, :], AX_X, ALU.add).then_inc(sig["r_sum"], 1)
                    dve.wait_ge(sig["r_sum"], q + 1)
                    dve.reciprocal(r_ri[:, :], r_sum[:, :]).then_inc(sig["r_ri"], 1)
                    dve.wait_ge(sig["r_ri"], q + 1)
                    dve.scalar_tensor_tensor(out=r_p[:, :, 0:E], in0=r_ex[:, :, :], scalar=0.5,
                                             in1=r_ri[:, :].unsqueeze(2).broadcast_to([P, T, E]),
                                             op0=ALU.mult, op1=ALU.mult).then_inc(sig["r_p"], 1)
                    constants_set()
                    dve.wait_ge(sig["r_p"], q + 1)
                    for t in range(T):
                        ins = dve.max(r_top[:, t, :], r_p[:, t, :])
                    ins.then_inc(sig["r_top"], 1)
                if slot == 9:
                    dve.wait_ge(sig["r_top"], q + 1)
                    dve.memset(r_top[:, :, TOP_K:8], -1.0).then_inc(sig["r_pad"], 1)
                    constants_set()
                    dve.wait_ge(sig["r_pad"], q + 1)
                    for t in range(T):
                        ins = dve.match_replace(r_rep[:, t, :], r_top[:, t, :], r_p[:, t, :], -2.0)
                    ins.then_inc(sig["r_rep"], 1)
                    dve.wait_ge(sig["r_rep"], q + 1)
                    dve.tensor_scalar(r_sel[:, :, :], r_rep[:, :, 0:E], 0.0, None, ALU.is_lt).then_inc(sig["r_sel"], 1)
                    dve.wait_ge(sig["r_sel"], q + 1)
                    dve.tensor_tensor(r_ws[:, :, :], r_sel[:, :, :], r_p[:, :, 0:E], ALU.mult).then_inc(sig["r_ws"], 1)
                if slot == 11:
                    dve.wait_ge(sig["r_cnt"], q + 1)
                    wait(dve, "r_carry", q)
                    dve.tensor_tensor(r_pos[:, :, :], pq[:, 0:T * E].rearrange("p (t e) -> p t e", t=T),
                                      r_carry[:, :].unsqueeze(1).broadcast_to([P, T, E]), ALU.add).then_inc(sig["r_pos"], 1)
                    dve.wait_ge(sig["r_pos"], q + 1)
                    dve.wait_ge(sig["r_ws"], q + 1)
                    dve.scalar_tensor_tensor(out=wide(r_w[:, :, :]), in0=wide(r_pos[:, :, :]), scalar=float(CAPACITY),
                                             in1=wide(r_ws[:, :, :]), op0=ALU.is_le, op1=ALU.mult).then_inc(sig["r_w"], 1)
                    if isinstance(q, int) and q == B - 1:
                        dve.memset(r_carry[:, :], 0.0).then_inc(sig["r_carry"], 1)
                    else:
                        dve.tensor_tensor(r_carry[:, :], pq[:, T * E:(T + 1) * E], r_carry[:, :],
                                          ALU.add).then_inc(sig["r_carry"], 1)

            def rwkv_step(m, slot):
                if slot == 0:
                    dve.wait_ge(sig["m_x"], done(m + 1))
                    row_stats(chunk(m), a_st, a_mv, m, "t_stats", "t_mvs")
                    dve.tensor_scalar(a_ve[:, 0:T], a_mv[:, :, 1], EPS, None, ALU.add).then_inc(sig["t_ve"], 1)
                    dve.tensor_scalar(a_ve[:, T:2 * T], a_mv[:, :, 1], 1.0 + EPS, EPS * EPS, ALU.mult,
                                      ALU.add).then_inc(sig["t_ve"], 1)
                if slot == 1:
                    dve.wait_ge(sig["t_rstd"], m + 1)
                    normalise(t_hn, chunk(m), a_mv, a_rs[:, T:2 * T], "t_hn")
                    normalise(t_u, chunk(m), a_mv, a_rs[:, 0:T], "t_u")
                if slot == 4:
                    dve.wait_ge(sig["t_d"], m + 1)
                    for dst, c in ((t_xk, MIX_K), (t_xv, MIX_V), (t_xr, MIX_R)):
                        dve.scalar_tensor_tensor(out=dst[:, :], in0=t_d[:, :], scalar=vec[:, c:c + 1], in1=t_h[:, 0:S],
                                                 op0=ALU.mult, op1=ALU.add).then_inc(sig["t_xk"], 1)
                if slot == 6:
                    dve.wait_ge(sig["t_k"], m + 1)
                    dve.tensor_tensor_scan(out=t_pp[:, 1:1 + S], data0=decay[:, 0:1].to_broadcast([P, S]),
                                           data1=t_k[:, :], initial=NEVER, op0=ALU.add, op1=ALU.max)\
                       .then_inc(sig["t_pp"], 1)
                    dve.wait_ge(sig["t_pp"], m + 1)
                    dve.scalar_tensor_tensor(out=t_qq[:, :], in0=t_k[:, :], scalar=vec[:, FIRST:FIRST + 1],
                                             in1=t_pp[:, 0:S], op0=ALU.add, op1=ALU.max).then_inc(sig["t_qq"], 1)
                    dve.scalar_tensor_tensor(out=t_ea[:, 0, :], in0=t_pp[:, 0:S], scalar=decay[:, 0:1],
                                             in1=t_pp[:, 1:1 + S], op0=ALU.add, op1=ALU.subtract).then_inc(sig["t_a0"], 1)
                    dve.wait_ge(sig["t_qq"], m + 1)
                    dve.scalar_tensor_tensor(out=t_eb[:, 1, :], in0=t_k[:, :], scalar=vec[:, FIRST:FIRST + 1],
                                             in1=t_qq[:, :], op0=ALU.add, op1=ALU.subtract).then_inc(sig["t_b1"], 1)
                if slot == 8:
                    dve.wait_ge(sig["t_ev"], m + 1)
                    dve.tensor_tensor_scan(out=t_aa[:, 1:1 + S], data0=t_ea[:, 0, :], data1=t_ev[:, :], initial=0.0,
                                           op0=ALU.mult, op1=ALU.add).then_inc(sig["t_aa"], 1)
                    dve.tensor_tensor_scan(out=t_bb[:, 1:1 + S], data0=t_ea[:, 0, :], data1=t_ea[:, 1, :], initial=0.0,
                                           op0=ALU.mult, op1=ALU.add).then_inc(sig["t_bb"], 1)
                    dve.wait_ge(sig["t_expb"], m + 1)
                    dve.wait_ge(sig["t_aa"], m + 1)
                    dve.tensor_tensor(t_n1[:, :], t_eb[:, 0, :], t_aa[:, 0:S], ALU.mult).then_inc(sig["t_n1"], 1)
                    dve.wait_ge(sig["t_bb"], m + 1)
                    dve.tensor_tensor(t_d1[:, :], t_eb[:, 0, :], t_bb[:, 0:S], ALU.mult).then_inc(sig["t_d1"], 1)
                if slot == 9:
                    dve.wait_ge(sig["t_d1"], m + 1)
                    dve.tensor_tensor(t_d1[:, :], t_d1[:, :], t_eb[:, 1, :], ALU.add).then_inc(sig["t_den"], 1)
                    dve.wait_ge(sig["t_n2"], m + 1)
                    dve.wait_ge(sig["t_n1"], m + 1)
                    dve.tensor_tensor(t_n1[:, :], t_n1[:, :], t_n2[:, :], ALU.add).then_inc(sig["t_num"], 1)
                    dve.wait_ge(sig["t_den"], m + 1)
                    invert(0)
                if slot == 10:
                    for i in range(1, T):
                        invert(i)
                    dve.wait_ge(sig["t_ri"], T * m + T)
                    dve.wait_ge(sig["t_num"], m + 1)
                    dve.tensor_tensor(t_ri[:, :], t_n1[:, :], t_ri[:, :], ALU.mult).then_inc(sig["t_y"], 1)
                    dve.wait_ge(sig["t_y"], m + 1)
                    dve.wait_ge(sig["t_r"], m + 1)
                    dve.scalar_tensor_tensor(out=t_n1[:, :], in0=t_r[:, :], scalar=1.0, in1=t_ri[:, :],
                                             op0=ALU.add, op1=ALU.mult).then_inc(sig["t_rw"], 1)
                if slot == 12:
                    dve.wait_ge(sig["t_ops"], m + 1)
                    dve.wait_ge(sig["t_u"], m + 1)
                    dve.scalar_tensor_tensor(out=wide(t_u2[:, :, :]), in0=pu[:, :], scalar=0.5,
                                             in1=wide(t_u[:, :, :]), op0=ALU.mult, op1=ALU.add).then_inc(sig["t_u2"], 1)
                    dve.wait_ge(sig["t_u2"], m + 1)
                    row_stats(t_u2, a_st, a_mv, m, "f_stats", "f_mvs")
                    dve.tensor_scalar(a_ve[:, 0:T], a_mv[:, :, 1], EPS, None, ALU.add).then_inc(sig["f_ve"], 1)
                if slot == 13:
                    dve.wait_ge(sig["f_rstd"], m + 1)
                    normalise(t_hn, t_u2, a_mv, a_rs, "f_hn")
                    dve.tensor_tensor(wide(chunk(m)), wide(chunk(m)), wide(t_u2[:, :, :]), ALU.add)\
                       .then_inc(sig["f_x"], 1)
                if slot == 15:
                    dve.wait_ge(sig["f_d"], m + 1)
                    for dst, c in ((t_xk, FMIX_K), (t_xr, FMIX_R)):
                        dve.scalar_tensor_tensor(out=dst[:, :], in0=t_d[:, :], scalar=vec[:, c:c + 1], in1=t_h[:, 0:S],
                                                 op0=ALU.mult, op1=ALU.add).then_inc(sig["f_xk"], 1)
                if slot == 18:
                    dve.wait_ge(sig["f_tr2"], m + 1)
                    dve.wait_ge(sig["f_kv"], m + 1)
                    dve.scalar_tensor_tensor(out=t_g[:, :], in0=t_tr[:, :], scalar=1.0, in1=pu[:, :],
                                             op0=ALU.add, op1=ALU.mult).then_inc(sig["f_g"], 1)
                    dve.wait_ge(sig["f_g"], m + 1)
                    dve.wait_ge(sig["f_x"], 2 * m + 1)
                    dve.scalar_tensor_tensor(out=wide(chunk(m)), in0=t_g[:, :], scalar=0.5, in1=wide(chunk(m)),
                                             op0=ALU.mult, op1=ALU.add).then_inc(sig["f_x"], 1)

            def invert(i):
                part = slice(P * i, P * (i + 1))
                dve.reciprocal(t_ri[:, part], t_d1[:, part]).then_inc(sig["t_ri"], 1)

            def iteration(g=None, bb=None, att=None, rwkv=None, pro=None, pb_=None, layer=0):
                for slot in range(UNITS + 2):
                    if g is not None and slot < UNITS:
                        unit(g, slot)
                    if att is not None:
                        att_step(att, slot)
                    if rwkv is not None:
                        rwkv_step(rwkv, slot)
                    if pro is not None:
                        pro_step(pro, pb_, slot, layer)
                if g is not None:
                    add_out(g, bb)

            iteration(att=0)
            iteration(att=1, pro=0, pb_=0)
            dve.wait_ge(sig["in_xr"], 16 * (B - 2))
            with dve.Fori(0, B - 2) as g:
                iteration(g, g, att=g + 2, pro=g + 1, pb_=g + 1)
            dve.wait_ge(sig["in_vec"], 16)
            dve.wait_ge(sig["c_dec"], 1)
            iteration(B - 2, B - 2, rwkv=0, pro=B - 1, pb_=B - 1)
            iteration(B - 1, B - 1, rwkv=1, pro=B, pb_=0, layer=1)
            with dve.Fori(B, 2 * B - 2) as g:
                iteration(g, g - B, rwkv=g - (B - 2), pro=g + 1, pb_=g - (B - 1), layer=1)
            iteration(2 * B - 2, B - 2, pro=2 * B - 1, pb_=B - 1, layer=1)
            iteration(2 * B - 1, B - 1)


def kernel(**inputs):
    import numpy as np
    import concourse.bacc as _bacc
    from concourse.bass_utils import run_bass_kernel_spmd as _run

    def get(name):
        return np.asarray(inputs["L0_" + name])

    def packed(blocks):
        return np.ascontiguousarray(np.stack(blocks, axis=1))

    key = get("attn_b_Wkey").T
    val = get("attn_b_Wval").T
    arrays = {
        "x": np.ascontiguousarray(get("attn_a_embeddings")),
        "att_mats": packed([get("attn_a_W_Q").T, get("attn_a_W_K").T, get("attn_a_W_V")]),
        "mats": packed(
            [get("attn_b_" + n).T for n in ("Wk", "Wv", "Wr", "Wo", "Wrec")]
            + [get("ffn_" + n) for n in ("Ws1", "Ws3", "Ws2")]
            + [key[:, P * j:P * (j + 1)] for j in range(FB)]
            + [val[P * j:P * (j + 1), :] for j in range(FB)]),
        "vecs": packed([get("attn_b_" + n).reshape(-1) for n in (
            "ln1_w", "ln1_b", "ln2_w", "ln2_b", "att_tmk", "att_tmv", "att_tmr", "time_decay", "time_first",
            "ffn_tmk", "ffn_tmr")]),
        "w_gate": np.ascontiguousarray(get("ffn_Wg")),
        "w1": np.ascontiguousarray(get("ffn_W1").transpose(1, 0, 2).reshape(D, PAIRS, P)),
        "w3": np.ascontiguousarray(get("ffn_W3").transpose(1, 0, 2).reshape(D, PAIRS, P)),
        "w2": np.ascontiguousarray(get("ffn_W2").reshape(PAIRS, P, D).transpose(1, 0, 2)),
    }
    nc = _bacc.Bacc("TRN2", target_bir_lowering=False, num_devices=1)
    args = [nc.dram_tensor("in_" + n, a.shape, mybir.dt.from_np(a.dtype), kind="ExternalInput").ap() for n, a in arrays.items()]
    args.append(nc.dram_tensor("x_out", (B, S, D), F32, kind="ExternalOutput").ap())
    hybrid_kernel(nc, *args)
    r = _run(nc, [{"in_" + n: a for n, a in arrays.items()}], core_ids=[0])
    return r.results[0]["x_out"]
```

```python
from contextlib import ExitStack

import concourse.bass as bass
from concourse import mybir

ALU = mybir.AluOpType
ACT = mybir.ActivationFunctionType
AX_X = mybir.AxisListType.X
F32 = mybir.dt.float32
F32R = mybir.dt.float32r
BF16 = mybir.dt.bfloat16

P = 128
B = 8
S = 512
D = 128
T = S // P
E = 32
H = 64
TOP_K = 4
CAPACITY = 4 * (B * S * TOP_K) // E
PAIRS = E * H // P
UNITS = PAIRS + 1
GROUPS = 4
GP = PAIRS // GROUPS
GRING = 2
SILU_FROM = B - 2
LAG = 3
EXP_UNIT = 10
FB = 4
EPS = 1e-5
SCALE = 1.0 / float(D) ** 0.5
MASKED = -1.0e30
NEVER = -1.0e38
BASE = 1

LN1_W, LN1_B, LN2_W, LN2_B, MIX_K, MIX_V, MIX_R, DECAY, FIRST, FMIX_K, FMIX_R = range(11)
M_K, M_V, M_R, M_O, M_REC, M_S1, M_S3, M_S2, M_KEY, M_VAL = 0, 1, 2, 3, 4, 5, 6, 7, 8, 12
N_MATS = 16


def hybrid_kernel(nc, x_in, att_mats, mats, vecs, w_gate, w1_in, w3_in, w2_in, x_out):
    with ExitStack() as ctx:
        def sb(name, shape, dt=F32):
            return ctx.enter_context(nc.sbuf_tensor(name, shape, dt))

        def bank(name, dt=F32):
            return ctx.enter_context(nc.psum_tensor(name, [P, 512], dt))

        def sem(name):
            return ctx.enter_context(nc.semaphore(name))

        x_sb = sb("x_sb", [P, B, T, D])
        am = sb("am", [P, 3, D])
        mt = sb("mt", [P, N_MATS, D])
        vec = sb("vec", [P, 11])
        wg = sb("wg", [P, E])
        w1h = sb("w1h", [P, UNITS, P], F32R)
        w1l = sb("w1l", [P, UNITS, P], F32R)
        w3h = sb("w3h", [P, UNITS, P], F32R)
        w3l = sb("w3l", [P, UNITS, P], F32R)
        w2 = sb("w2", [P, PAIRS, P])
        qk_m = sb("qk_m", [P, D])
        ident = sb("ident", [P, P])
        ident_b = sb("ident_b", [P, P], BF16)
        causal_b = sb("causal_b", [P, P], BF16)
        tri_b = sb("tri_b", [P, P], BF16)
        ones_b = sb("ones_b", [P, P], BF16)
        minus_half = sb("minus_half", [P, 2 * T])
        one = sb("one", [P, 1])
        decay = sb("decay", [P, 1])

        a_st = sb("a_st", [P, T, 6])
        a_mv = sb("a_mv", [P, T, 2])
        a_ve = sb("a_ve", [P, T])
        a_rs = sb("a_rs", [P, T])
        a_xn = sb("a_xn", [P, T, D])
        a_xT = sb("a_xT", [P, 1 + S])
        a_g = sb("a_g", [P, S])
        a_v = sb("a_v", [P, T, D])
        a_p = sb("a_p", [P, S])
        a_pT = sb("a_pT", [P, S])
        a_mx = sb("a_mx", [P, T])
        a_nm = sb("a_nm", [P, T])
        a_sum = sb("a_sum", [P, T])
        a_ri = sb("a_ri", [P, T])

        r_st = sb("r_st", [P, T, 6])
        r_mv = sb("r_mv", [P, T, 2])
        r_ve = sb("r_ve", [P, T])
        r_rs = sb("r_rs", [P, T])
        r_xn = sb("r_xn", [P, T, D])
        r_xT = sb("r_xT", [P, S])
        r_mx = sb("r_mx", [P, T])
        r_lg = sb("r_lg", [P, T, E])
        r_ex = sb("r_ex", [P, T, E])
        r_sum = sb("r_sum", [P, T])
        r_ri = sb("r_ri", [P, T])
        r_p = sb("r_p", [P, T, E + TOP_K])
        r_top = sb("r_top", [P, T, 8])
        r_rep = sb("r_rep", [P, T, E + TOP_K])
        r_sel = sb("r_sel", [P, T, E], BF16)
        r_ws = sb("r_ws", [P, T, E])
        r_pos = sb("r_pos", [P, T, E])
        r_w = sb("r_w", [P, T, E])
        r_carry = sb("r_carry", [P, E])
        r_wT = sb("r_wT", [E, S])

        m_xh = sb("m_xh", [P, 2, S], F32R)
        m_xl = sb("m_xl", [P, 2, S], F32R)
        m_wb = sb("m_wb", [P, GRING * GP, S])
        w_stage = m_wb[:, :, :].rearrange("p a (b c) -> p (a b) c", c=P)
        m_th = sb("m_th", [P, 2, S])
        m_u = sb("m_u", [P, 2, S])
        m_v = sb("m_v", [P, 2, S])
        m_h = sb("m_h", [P, 5, S])
        m_y = sb("m_y", [P, S])

        t_u = sb("t_u", [P, T, D])
        t_hn = sb("t_hn", [P, T, D])
        t_h = sb("t_h", [P, 1 + S])
        t_d = sb("t_d", [P, S])
        t_xk = sb("t_xk", [P, S])
        t_xv = sb("t_xv", [P, S])
        t_xr = sb("t_xr", [P, S])
        t_k = sb("t_k", [P, S])
        t_v = sb("t_v", [P, S])
        t_r = sb("t_r", [P, S])
        t_pp = sb("t_pp", [P, 1 + S])
        t_aa = sb("t_aa", [P, 1 + S])
        t_bb = sb("t_bb", [P, 1 + S])
        t_qq = sb("t_qq", [P, S])
        t_ea = sb("t_ea", [P, 2, S])
        t_eb = sb("t_eb", [P, 2, S])
        t_ev = sb("t_ev", [P, S])
        t_n1 = sb("t_n1", [P, S])
        t_n2 = sb("t_n2", [P, S])
        t_d1 = sb("t_d1", [P, S])
        t_ri = sb("t_ri", [P, S])
        t_u2 = sb("t_u2", [P, T, D])
        f_kk = sb("f_kk", [P, FB, S])
        f_tr = sb("f_tr", [P, S])
        f_g = sb("f_g", [P, S])
        f_hn, f_h, f_d, f_xk, f_xr = a_xn, a_xT, a_g, a_p, a_pT
        t_st, t_mv = sb("t_st", [P, T, 6]), sb("t_mv", [P, T, 2])
        t_ve, t_rs = sb("t_ve", [P, 2 * T]), sb("t_rs", [P, 2 * T])

        pa = [bank("pa0"), bank("pa1")]
        pb = [bank("pb0"), bank("pb1")]
        py = bank("py")
        pq = bank("pq")
        pu, pv = bank("pu"), bank("pv")

        w_scratch = nc.dram_tensor("w_scratch", [2 * B, GROUPS, GP, 2, S], F32, kind="Internal").ap()

        names = (
            "in_x0 in_x1 in_xr in_am in_vec in_wg in_w1 in_w3 in_w2 in_mt c_pool c_dve c_dec0 c_dec c_qkm_ps c_qkm "
            "a_stats a_mvs a_vedone a_rstd a_xn a_tr a_xT a_gps a_vps a_g a_v a_s a_mx a_nm a_exp a_pT a_pTs a_o a_ri a_add "
            "r_stats r_mvs r_vedone r_rstd r_xn r_tr r_xT m_xh m_xl r_lgps r_mx r_lg r_ex r_sum r_ri r_p r_top r_pad r_rep "
            "r_sel r_ws r_cnt r_pos r_w r_carry r_wTps r_wT w_out "
            "c_wh c_wl m_a m_b m_th m_u m_ue m_v m_h m_y m_ys m_yT m_x "
            "t_stats t_mvs t_ve t_rstd t_hn t_tr t_h t_d t_xk t_kps t_vps t_rps t_k t_v t_r t_pp t_a0 t_a1 t_qq t_b0 t_b1 "
            "t_expa t_expb t_ev t_n2 t_aa t_bb t_n1 t_d1 t_den t_num t_ri t_y t_rw t_ops t_u t_u2 t_xu "
            "f_stats f_mvs f_ve f_rstd f_hn f_tr f_h f_d f_xk f_key f_rk f_kk f_rec f_zero f_tr2 f_kv f_g f_x "
            "out_done stats_seen"
        ).split()
        sig = {n: sem("s_" + n) for n in names}
        wb_in = [sem(f"s_wb_in{j}") for j in range(GROUPS)]

        def wait(eng, name, value):
            if not (isinstance(value, int) and value <= 0):
                eng.wait_ge(sig[name], value)

        def done(n):
            return n + BASE

        block = ctx.enter_context(nc.Block())
        xv = x_in.rearrange("b (t p) d -> b p t d", p=P)
        ov = x_out.rearrange("b (t p) d -> b p t d", p=P)

        def layer_of(q):
            return (0 if q < B else 1) if isinstance(q, int) else (0 if q.max_val < B else 1)

        def sequence(q):
            return q if layer_of(q) == 0 else q - B

        def sequence_before(g):
            if isinstance(g, int):
                return (g - 1) % B
            return sequence(g) - 1

        def hidden_slot(p):
            return p % 4 if p < PAIRS else 4

        def chunk(c):
            return x_sb[:, c, :, :]

        def router_bank(cmix):
            return pq if cmix is None else pv

        def wide(ap):
            return ap.rearrange("p t d -> p (t d)")

        @block.sync
        def _(sp):
            sp.dma_start(chunk(0), xv[0]).then_inc(sig["in_x0"], 16)
            sp.dma_start(w_stage[:, 0:PAIRS, :], w1_in).then_inc(sig["in_w1"], 16)
            sp.dma_start(w_stage[:, PAIRS:2 * PAIRS, :], w3_in).then_inc(sig["in_w3"], 16)
            sp.dma_start(chunk(1), xv[1]).then_inc(sig["in_x1"], 16)
            sp.dma_start(wg[:, :], w_gate).then_inc(sig["in_wg"], 16)
            sp.dma_start(mt[:, :, :], mats).then_inc(sig["in_mt"], 16)
            sp.dma_start(w2[:, :, :], w2_in).then_inc(sig["in_w2"], 16)
            for c in range(2, B):
                sp.dma_start(chunk(c), xv[c]).then_inc(sig["in_xr"], 16)
            for name in ("m_v", "m_h", "m_y", "m_x"):
                sp.sem_inc(sig[name], BASE)

            def spread_weights(q):
                sp.wait_ge(sig["r_wT"], q + 1)
                sp.dma_start(w_scratch[q].rearrange("j a h s -> (j a h) s"), r_wT[:, :]).then_inc(sig["w_out"], 16)
                sp.wait_ge(sig["w_out"], 16 * q + 16)
                for j in range(GROUPS):
                    if j >= GRING:
                        sp.wait_ge(sig["m_h"], done(UNITS * q + GP * (j - GRING + 1)))
                    elif isinstance(q, int) and q == 0:
                        sp.wait_ge(sig["c_wl"], 2)
                    else:
                        sp.wait_ge(sig["m_h"], done(UNITS * (q - 1) + GP * (GROUPS - GRING + j + 1)))
                    at = GP * (j % GRING)
                    for h in range(2):
                        sp.dma_start(m_wb[H * h:H * (h + 1), at:at + GP, :],
                                     w_scratch[q, j, :, h, :].partition_broadcast(H)).then_inc(wb_in[j], 16)

            def store(c):
                sp.wait_ge(sig["m_x"], done(B + c + 1))
                sp.dma_start(ov[c], chunk(c)).then_inc(sig["out_done"], 16)

            spread_weights(0)
            with sp.Fori(1, B + 2) as q:
                spread_weights(q)
            with sp.Fori(B + 2, 2 * B) as q:
                spread_weights(q)
                store(q - (B + 2))
            store(B - 2)
            store(B - 1)
            sp.wait_ge(sig["out_done"], 16 * B)

        @block.gpsimd
        def _(pool):
            pool.memset(ident[:, :], 0.0).then_inc(sig["c_pool"], 1)
            pool.memset(ident_b[:, :], 0.0).then_inc(sig["c_pool"], 1)
            pool.memset(causal_b[:, :], 0.0).then_inc(sig["c_pool"], 1)
            pool.memset(tri_b[:, :], 1.0).then_inc(sig["c_pool"], 1)
            pool.memset(ones_b[:, :], 1.0).then_inc(sig["c_pool"], 1)
            pool.memset(minus_half[:, :], -0.5).then_inc(sig["c_pool"], 1)
            pool.memset(one[:, :], 1.0).then_inc(sig["c_pool"], 1)
            pool.wait_ge(sig["c_pool"], 7)
            for m in (ident, ident_b):
                pool.affine_select(out=m[:, :], in_=m[:, :], compare_op=ALU.not_equal, fill=1.0, base=0,
                                   pattern=[[-1, P]], channel_multiplier=1).then_inc(sig["c_pool"], 1)
            pool.affine_select(out=causal_b[:, :], in_=causal_b[:, :], compare_op=ALU.is_ge, fill=MASKED, base=0,
                               pattern=[[-1, P]], channel_multiplier=1).then_inc(sig["c_pool"], 1)
            pool.affine_select(out=tri_b[:, :], in_=tri_b[:, :], compare_op=ALU.is_ge, fill=0.0, base=0,
                               pattern=[[1, P]], channel_multiplier=-1).then_inc(sig["c_pool"], 1)

            def rsqrt(out, in_, ready, n, signal):
                pool.wait_ge(sig[ready], n)
                pool.tensor_tensor(out, in_, minus_half[:, 0:out.shape[1]], ALU.pow).then_inc(sig[signal], 1)

            def unit(g, p):
                k = UNITS * g + p
                if p < PAIRS and p % GP == 0:
                    pool.wait_ge(wb_in[p // GP], 32 * g + 32)
                pool.wait_ge(sig["m_v"], done(k + 1))
                wait(pool, "m_y", done(k - 3))
                if p < PAIRS:
                    pool.tensor_tensor(m_h[:, hidden_slot(p), :], m_v[:, p % 2, :], m_wb[:, p % (GRING * GP), :], ALU.mult).then_inc(sig["m_h"], 1)
                else:
                    pool.tensor_tensor(m_h[:, hidden_slot(p), :], m_v[:, p % 2, :], one[:, 0:1].to_broadcast([P, S]),
                                       ALU.mult).then_inc(sig["m_h"], 1)

            def split_weights(blocks, high, low, src, loaded):
                pool.wait_ge(sig[loaded[0]], 16)
                pool.wait_ge(sig["c_wh"], loaded[1])
                pool.tensor_tensor(low[:, blocks, :], src, high[:, blocks, :].bitcast(F32),
                                   ALU.subtract).then_inc(sig["c_wl"], 1)

            def pro_step(q, slot):
                if slot == 1:
                    rsqrt(r_rs[:, :], r_ve[:, :], "r_vedone", q + 1, "r_rstd")
                if slot == 6:
                    pool.wait_ge(sig["r_xT"], q + 1)
                    pool.wait_ge(sig["m_xh"], q + 1)
                    pool.tensor_tensor(m_xl[:, q % 2, :], r_xT[:, :], m_xh[:, q % 2, :].bitcast(F32),
                                       ALU.subtract).then_inc(sig["m_xl"], 1)

            def time_step(m, slot):
                if slot == 0:
                    rsqrt(t_rs[:, :], t_ve[:, :], "t_ve", 2 * m + 2, "t_rstd")
                if slot == 5:
                    pool.wait_ge(sig["t_h"], m + 1)
                    pool.tensor_tensor(t_d[:, :], t_h[:, 1:1 + S], t_h[:, 0:S], ALU.subtract).then_inc(sig["t_d"], 1)
                if slot == 9:
                    pool.wait_ge(sig["t_pp"], m + 1)
                    pool.tensor_tensor(t_ea[:, 1, :], t_k[:, :], t_pp[:, 1:1 + S], ALU.subtract).then_inc(sig["t_a1"], 1)
                    pool.wait_ge(sig["t_qq"], m + 1)
                    pool.tensor_tensor(t_eb[:, 0, :], t_pp[:, 0:S], t_qq[:, :], ALU.subtract).then_inc(sig["t_b0"], 1)
                if slot == 10:
                    pool.wait_ge(sig["t_expa"], m + 1)
                    pool.tensor_tensor(t_ev[:, :], t_ea[:, 1, :], t_v[:, :], ALU.mult).then_inc(sig["t_ev"], 1)
                    pool.wait_ge(sig["t_expb"], m + 1)
                    pool.tensor_tensor(t_n2[:, :], t_eb[:, 1, :], t_v[:, :], ALU.mult).then_inc(sig["t_n2"], 1)

            def channel_step(m, slot):
                if slot == 4:
                    rsqrt(a_rs[:, :], a_ve[:, :], "f_ve", m + 1, "f_rstd")
                if slot == 10:
                    pool.wait_ge(sig["f_h"], m + 1)
                    pool.tensor_tensor(f_d[:, :], f_h[:, 1:1 + S], f_h[:, 0:S], ALU.subtract).then_inc(sig["f_d"], 1)

            def iteration(g=None, att=None, tmix=None, cmix=None, pro=None):
                for slot in range(UNITS + 1):
                    if g is not None and slot < UNITS:
                        unit(g, slot)
                    if att is not None and slot == 0:
                        rsqrt(a_rs[:, :], a_ve[:, :], "a_vedone", att + 1, "a_rstd")
                    if cmix is not None:
                        channel_step(cmix, slot)
                    if tmix is not None:
                        time_step(tmix, slot)
                    if pro is not None:
                        pro_step(pro, slot)

            iteration(att=0)
            split_weights(slice(0, PAIRS), w1h, w1l, w_stage[:, 0:PAIRS, :], ("in_w1", 1))
            split_weights(slice(0, PAIRS), w3h, w3l, w_stage[:, PAIRS:2 * PAIRS, :], ("in_w3", 2))
            split_weights(slice(PAIRS, UNITS), w1h, w1l, mt[:, M_S1:M_S1 + 1, :], ("in_mt", 3))
            split_weights(slice(PAIRS, UNITS), w3h, w3l, mt[:, M_S3:M_S3 + 1, :], ("in_mt", 4))
            iteration(att=1, pro=0)
            iteration(0, att=2, pro=1)
            with pool.Fori(1, B - 3) as g:
                iteration(g, att=g + 2, pro=g + 1)
            iteration(B - 3, att=B - 1, tmix=0, pro=B - 2)
            iteration(B - 2, tmix=1, cmix=0, pro=B - 1)
            iteration(B - 1, tmix=2, cmix=1, pro=B)
            iteration(B, tmix=3, cmix=2, pro=B + 1)
            with pool.Fori(B + 1, 2 * B - 3) as g:
                iteration(g, tmix=g - (B - 3), cmix=g - (B - 2), pro=g + 1)
            iteration(2 * B - 3, cmix=B - 1, pro=2 * B - 2)
            iteration(2 * B - 2, pro=2 * B - 1)
            iteration(2 * B - 1)
        @block.scalar
        def _(act):
            act.dma_start(am[:, :, :], att_mats).then_inc(sig["in_am"], 16)
            act.dma_start(vec[:, :], vecs).then_inc(sig["in_vec"], 16)
            act.wait_ge(sig["in_vec"], 16)
            act.activation(decay[:, :], vec[:, DECAY:DECAY + 1], ACT.Exp).then_inc(sig["c_dec0"], 1)
            act.wait_ge(sig["c_qkm_ps"], 1)
            act.activation(qk_m[:, :], pv[:, 0:D], ACT.Copy).then_inc(sig["c_qkm"], 1)

            def unit(g, p, silu):
                act.wait_ge(sig["m_a"], UNITS * g + p + 1)
                if silu and p != EXP_UNIT:
                    ins = act.activation(m_th[:, p % 2, :], pa[p % 2][:, :], ACT.Silu)
                else:
                    ins = act.activation(m_th[:, p % 2, :], pa[p % 2][:, :], ACT.Tanh, scale=0.5)
                ins.then_inc(sig["m_th"], 1)

            def att_step(n, slot):
                if slot == 3:
                    act.wait_ge(sig["a_tr"], n + 1)
                    act.activation(a_xT[:, 0:S], pu[:, :], ACT.Copy).then_inc(sig["a_xT"], 1)
                if slot == 5:
                    act.wait_ge(sig["a_gps"], n + 1)
                    act.activation(a_g[:, :], pv[:, :], ACT.Copy).then_inc(sig["a_g"], 1)
                    act.wait_ge(sig["a_vps"], n + 1)
                    act.activation(wide(a_v[:, :, :]), pu[:, :], ACT.Copy).then_inc(sig["a_v"], 1)
                if slot == 8:
                    att_exp(n, 0, (0, 1), (0, P))
                if slot == 10:
                    turn_probs(n, 0, 3)
                    att_exp(n, 1, (2,), (0,))
                if slot == 13:
                    turn_probs(n, 1, 3)
                    att_exp(n, 2, (3,), (0,))
                if slot == 15:
                    turn_probs(n, 2, 4)

            def att_exp(n, i, tiles, at):
                act.wait_ge(sig["a_nm"], 3 * n + i + 1)
                wait(act, "a_pT", 3 * n + i)
                for t, o in zip(tiles, at):
                    ins = act.activation(a_p[:, o:o + P * (t + 1)], pv[:, o:o + P * (t + 1)], ACT.Exp,
                                         bias=a_nm[:, t:t + 1], scale=SCALE, accum_out=a_sum[:, t:t + 1])
                ins.then_inc(sig["a_exp"], 1)

            def turn_probs(n, i, blocks):
                act.wait_ge(sig["a_pT"], 3 * n + i + 1)
                act.activation(a_pT[:, 0:P * blocks], pu[:, 0:P * blocks], ACT.Copy).then_inc(sig["a_pTs"], 1)

            def pro_step(q, slot, cmix):
                if slot == 6:
                    act.wait_ge(sig["r_tr"], q + 1)
                    act.activation(r_xT[:, :], router_bank(cmix)[:, :], ACT.Copy).then_inc(sig["r_xT"], 1)
                    act.activation(m_xh[:, q % 2, :], router_bank(cmix)[:, :], ACT.Copy).then_inc(sig["m_xh"], 1)
                if slot == 9:
                    act.wait_ge(sig["r_lg"], q + 1)
                    act.activation(wide(r_ex[:, :, :]), wide(r_lg[:, :, :]), ACT.Exp).then_inc(sig["r_ex"], 1)
                if slot == 15:
                    act.wait_ge(sig["r_wTps"], q + 1)
                    wait(act, "w_out", 16 * q)
                    act.activation(r_wT[:, :], pq[0:E, :], ACT.Copy).then_inc(sig["r_wT"], 1)

            def time_step(m, slot):
                if slot == 4:
                    act.wait_ge(sig["t_tr"], m + 1)
                    act.activation(t_h[:, 1:1 + S], pq[:, :], ACT.Identity, bias=vec[:, LN1_B:LN1_B + 1],
                                   scale=vec[:, LN1_W:LN1_W + 1]).then_inc(sig["t_h"], 1)
                if slot == 8:
                    act.wait_ge(sig["t_kps"], m + 1)
                    act.activation(t_k[:, :], pq[:, :], ACT.Copy).then_inc(sig["t_k"], 1)
                if slot == 9:
                    act.wait_ge(sig["t_vps"], m + 1)
                    act.activation(t_v[:, :], pq[:, :], ACT.Copy).then_inc(sig["t_v"], 1)
                if slot == 10:
                    act.wait_ge(sig["t_rps"], m + 1)
                    act.activation(t_r[:, :], pq[:, :], ACT.Tanh, scale=0.5).then_inc(sig["t_r"], 1)
                    act.wait_ge(sig["t_a0"], m + 1)
                    act.wait_ge(sig["t_a1"], m + 1)
                    act.activation(wide(t_ea[:, :, :]), wide(t_ea[:, :, :]), ACT.Exp).then_inc(sig["t_expa"], 1)
                    act.wait_ge(sig["t_b0"], m + 1)
                    act.wait_ge(sig["t_b1"], m + 1)
                    act.activation(wide(t_eb[:, :, :]), wide(t_eb[:, :, :]), ACT.Exp).then_inc(sig["t_expb"], 1)

            def channel_step(m, slot):
                if slot == 9:
                    act.wait_ge(sig["f_tr"], m + 1)
                    act.activation(f_h[:, 1:1 + S], pu[:, :], ACT.Identity, bias=vec[:, LN2_B:LN2_B + 1],
                                   scale=vec[:, LN2_W:LN2_W + 1]).then_inc(sig["f_h"], 1)
                if slot == 11:
                    relu_square(m, 0, pv)
                    act.wait_ge(sig["f_rec"], m + 1)
                    act.activation(f_tr[:, :], pu[:, :], ACT.Tanh, scale=0.5).then_inc(sig["f_tr2"], 1)
                if slot == 12:
                    relu_square(m, 1, pv)
                if slot == 13:
                    relu_square(m, 2, pu)
                if slot == 14:
                    relu_square(m, 3, pv)

            def relu_square(m, j, ps):
                act.wait_ge(sig["f_key"], FB * m + j + 1)
                act.activation(f_kk[:, j, :], ps[:, :], ACT.Relu).then_inc(sig["f_rk"], 1)
                act.wait_ge(sig["f_rk"], FB * m + j + 1)
                act.activation(f_kk[:, j, :], f_kk[:, j, :], ACT.Square).then_inc(sig["f_kk"], 1)

            def out_copy(g):
                if g is None or (isinstance(g, int) and g == 0):
                    return
                act.wait_ge(sig["m_y"], done(UNITS * g))
                act.activation(m_y[:, :], py[:, :], ACT.Copy).then_inc(sig["m_ys"], 1)

            def iteration(g=None, att=None, tmix=None, cmix=None, pro=None, silu=False):
                for slot in range(UNITS + 1):
                    if g is not None and slot < UNITS:
                        unit(g, slot, silu)
                    if slot == LAG - 1:
                        out_copy(g)
                    if att is not None:
                        att_step(att, slot)
                    if cmix is not None:
                        channel_step(cmix, slot)
                    if pro is not None:
                        pro_step(pro, slot, cmix)
                    if tmix is not None:
                        time_step(tmix, slot)

            iteration(att=0)
            iteration(att=1, pro=0)
            iteration(0, att=2, pro=1)
            with act.Fori(1, B - 3) as g:
                iteration(g, att=g + 2, pro=g + 1)
            iteration(B - 3, att=B - 1, tmix=0, pro=B - 2)
            iteration(B - 2, tmix=1, cmix=0, pro=B - 1, silu=True)
            iteration(B - 1, tmix=2, cmix=1, pro=B, silu=True)
            iteration(B, tmix=3, cmix=2, pro=B + 1, silu=True)
            with act.Fori(B + 1, 2 * B - 3) as g:
                iteration(g, tmix=g - (B - 3), cmix=g - (B - 2), pro=g + 1, silu=True)
            iteration(2 * B - 3, cmix=B - 1, pro=2 * B - 2, silu=True)
            iteration(2 * B - 2, pro=2 * B - 1, silu=True)
            iteration(2 * B - 1, silu=True)
            out_copy(2 * B)

        @block.tensor
        def _(pe):
            pe.wait_ge(sig["c_pool"], 11)
            pe.wait_ge(sig["in_am"], 16)
            pe.matmul(pv[:, 0:D], am[:, 0, :], am[:, 1, :], start=True, stop=True).then_inc(sig["c_qkm_ps"], 1)

            def turn(ps, src, signal):
                for t in range(T):
                    ins = pe.transpose(ps[:, P * t:P * (t + 1)], src[:, t, :], ident[:, :])
                ins.then_inc(sig[signal], 1)

            def unit(g, p):
                k = UNITS * g + p
                if p == 0:
                    pe.wait_ge(sig["m_xl"], g + 1)
                    pe.wait_ge(sig["m_xh"], g + 1)
                pe.wait_ge(sig["m_v"], done(k) if p == 0 else done(k - 1))
                up(pa[p % 2], w1h, w1l, g, p).then_inc(sig["m_a"], 1)
                up(pb[p % 2], w3h, w3l, g, p).then_inc(sig["m_b"], 1)

            def up(ps, high, low, g, p):
                xh, xl = m_xh[:, g % 2, :], m_xl[:, g % 2, :]
                pe.matmul(ps[:, :], high[:, p, :], xh, start=True, stop=False)
                pe.matmul(ps[:, :], high[:, p, :], xl, start=False, stop=False)
                return pe.matmul(ps[:, :], low[:, p, :], xh, start=False, stop=True)

            def out_product(g, p):
                k = UNITS * g + p
                if p == 0:
                    wait(pe, "m_ys", g)
                pe.wait_ge(sig["m_h"], done(k + 1))
                down = w2[:, p, :] if p < PAIRS else mt[:, M_S2, :]
                pe.matmul(py[:, :], down, m_h[:, hidden_slot(p), :], start=(p == 0),
                          stop=(p == UNITS - 1)).then_inc(sig["m_y"], 1)

            def out_step(g, slot):
                if slot >= LAG:
                    out_product(g, slot - LAG)
                elif not (isinstance(g, int) and g == 0):
                    out_product(g - 1, UNITS - LAG + slot)
                if slot == LAG + 1 and not (isinstance(g, int) and g == 0):
                    out_turn(g)

            def out_turn(g):
                pe.wait_ge(sig["m_ys"], g)
                for t in range(T):
                    ins = pe.transpose(pv[:, P * t:P * (t + 1)], m_y[:, P * t:P * (t + 1)], ident[:, :])
                ins.then_inc(sig["m_yT"], 1)

            def att_step(n, slot, n_chunk):
                if slot == 3:
                    pe.wait_ge(sig["a_xn"], n + 1)
                    turn(pu, a_xn, "a_tr")
                if slot == 5:
                    pe.wait_ge(sig["c_qkm"], 1)
                    pe.wait_ge(sig["a_xT"], n + 1)
                    if n_chunk is not None:
                        wait(pe, "m_x", done(n_chunk) if not isinstance(n_chunk, int) or n_chunk else 0)
                    pe.matmul(pv[:, :], qk_m[:, :], a_xT[:, 0:S], start=True, stop=True).then_inc(sig["a_gps"], 1)
                    for t in range(T):
                        ins = pe.matmul(pu[:, P * t:P * (t + 1)], a_xT[:, P * t:P * (t + 1)], am[:, 2, :],
                                        start=True, stop=True)
                    ins.then_inc(sig["a_vps"], 1)
                if slot == 7:
                    pe.wait_ge(sig["a_g"], n + 1)
                    scores(n, (0, 1), (0, P))
                if slot == 9:
                    pe.wait_ge(sig["a_v"], n + 1)
                    probs(n, 0, 3)
                    scores(n, (2,), (0,))
                if slot == 11:
                    values(n, 0, (0, 1), (0, P))
                if slot == 12:
                    probs(n, 1, 3)
                    scores(n, (3,), (0,))
                if slot == 14:
                    values(n, 1, (2,), (0,))
                if slot == 15:
                    probs(n, 2, 4)
                if slot == 16:
                    values(n, 2, (3,), (0,))

            def scores(n, tiles, at):
                for t, o in zip(tiles, at):
                    q = slice(P * t, P * (t + 1))
                    pe.matmul(pv[:, o:o + P * (t + 1)], a_g[:, q], a_xT[:, 0:P * (t + 1)], start=True, stop=False)
                    ins = pe.matmul(pv[:, o + P * t:o + P * (t + 1)], ident_b[:, :], causal_b[:, :],
                                    start=False, stop=True)
                ins.then_inc(sig["a_s"], 1)

            def probs(n, i, blocks):
                pe.wait_ge(sig["a_exp"], 3 * n + i + 1)
                wait(pe, "a_add", 3 * n + i)
                for j in range(blocks):
                    ins = pe.transpose(pu[:, P * j:P * (j + 1)], a_p[:, P * j:P * (j + 1)], ident[:, :])
                ins.then_inc(sig["a_pT"], 1)

            def values(n, i, tiles, at):
                pe.wait_ge(sig["a_pTs"], 3 * n + i + 1)
                for t, o in zip(tiles, at):
                    for j in range(t + 1):
                        ins = pe.matmul(pu[:, P * t:P * (t + 1)], a_pT[:, o + P * j:o + P * (j + 1)], a_v[:, j, :],
                                        start=(j == 0), stop=(j == t))
                ins.then_inc(sig["a_o"], 1)

            def pro_step(q, slot, tmix, cmix):
                ps = router_bank(cmix)
                if slot == 6:
                    pe.wait_ge(sig["r_xn"], q + 1)
                    if cmix is not None:
                        pe.wait_ge(sig["m_x"], done(q - 1))
                    elif tmix is not None:
                        pe.wait_ge(sig["t_h"], tmix + 1)
                    else:
                        wait(pe, "r_wT", q)
                    turn(ps, r_xn, "r_tr")
                if slot == 8:
                    pe.wait_ge(sig["m_xh"], q + 1)
                    for t in range(T):
                        ins = pe.matmul(ps[:, E * t:E * (t + 1)], r_xT[:, P * t:P * (t + 1)], wg[:, :],
                                        start=True, stop=True)
                    ins.then_inc(sig["r_lgps"], 1)
                if slot == 13:
                    pe.wait_ge(sig["r_sel"], q + 1)
                    if tmix is not None:
                        pe.wait_ge(sig["t_r"], tmix + 1)
                    for t in range(T):
                        later = T - t
                        pe.matmul(pq[:, E * (t + 1):E * (T + 1)].rearrange("p (a e) -> p a e", a=later),
                                  ones_b[:, :], r_sel[:, t:t + 1, :].broadcast_to([P, later, E]),
                                  start=(t == 0), stop=False, skip_group_check=True)
                        ins = pe.matmul(pq[:, E * t:E * (t + 1)], tri_b[:, :], r_sel[:, t, :],
                                        start=False, stop=(t == T - 1), skip_group_check=True)
                    ins.then_inc(sig["r_cnt"], 1)
                if slot == 15:
                    pe.wait_ge(sig["r_w"], q + 1)
                    pe.wait_ge(sig["r_carry"], q + 1)
                    for t in range(T):
                        ins = pe.transpose(pq[0:E, P * t:P * (t + 1)], r_w[:, t, :], ident[:, :])
                    ins.then_inc(sig["r_wTps"], 1)

            def time_step(m, slot, q, cmix):
                if slot == 4:
                    pe.wait_ge(sig["t_hn"], m + 1)
                    pe.wait_ge(sig["r_wT"], q)
                    wait(pe, "t_u2", m)
                    turn(pq, t_hn, "t_tr")
                if slot == 8:
                    pe.wait_ge(sig["t_xk"], 3 * m + 3)
                    if cmix is None:
                        pe.wait_ge(sig["r_lg"], q + 1)
                    pe.matmul(pq[:, :], mt[:, M_K, :], t_xk[:, :], start=True, stop=True).then_inc(sig["t_kps"], 1)
                if slot == 9:
                    pe.wait_ge(sig["t_k"], m + 1)
                    pe.matmul(pq[:, :], mt[:, M_V, :], t_xv[:, :], start=True, stop=True).then_inc(sig["t_vps"], 1)
                if slot == 10:
                    pe.wait_ge(sig["t_v"], m + 1)
                    pe.matmul(pq[:, :], mt[:, M_R, :], t_xr[:, :], start=True, stop=True).then_inc(sig["t_rps"], 1)
            def channel_step(m, slot, q):
                if slot == 1:
                    pe.wait_ge(sig["t_rw"], m + 1)
                    pe.wait_ge(sig["r_wT"], q)
                    for t in range(T):
                        ins = pe.matmul(pq[:, P * t:P * (t + 1)], t_n1[:, P * t:P * (t + 1)], mt[:, M_O, :],
                                        start=True, stop=True)
                    ins.then_inc(sig["t_ops"], 1)
                if slot == 9:
                    pe.wait_ge(sig["f_hn"], m + 1)
                    turn(pu, f_hn, "f_tr")
                if slot == 11:
                    pe.wait_ge(sig["f_xk"], 2 * m + 2)
                    key(m, 0, pv)
                    for t in range(T):
                        ins = pe.matmul(pu[:, P * t:P * (t + 1)], f_xr[:, P * t:P * (t + 1)], mt[:, M_REC, :],
                                        start=True, stop=True)
                    ins.then_inc(sig["f_rec"], 1)
                if slot == 12:
                    pe.wait_ge(sig["f_rk"], FB * m + 1)
                    key(m, 1, pv)
                if slot == 13:
                    pe.wait_ge(sig["f_tr2"], m + 1)
                    key(m, 2, pu)
                if slot == 14:
                    pe.wait_ge(sig["f_rk"], FB * m + 2)
                    key(m, 3, pv)
                if slot == 16:
                    pe.wait_ge(sig["f_kk"], FB * m + FB)
                    for t in range(T):
                        for j in range(FB):
                            ins = pe.matmul(pu[:, P * t:P * (t + 1)], f_kk[:, j, P * t:P * (t + 1)],
                                            mt[:, M_VAL + j, :], start=(j == 0), stop=(j == FB - 1))
                    ins.then_inc(sig["f_kv"], 1)

            def key(m, j, ps):
                pe.matmul(ps[:, :], mt[:, M_KEY + j, :], f_xk[:, :], start=True, stop=True).then_inc(sig["f_key"], 1)

            def iteration(g=None, att=None, tmix=None, cmix=None, pro=None):
                for slot in range(UNITS):
                    if g is not None:
                        unit(g, slot)
                        out_step(g, slot)
                    if att is not None:
                        att_step(att, slot, g)
                    if cmix is not None:
                        channel_step(cmix, slot, cmix + B - 1)
                    if pro is not None:
                        pro_step(pro, slot, tmix, cmix)
                    if tmix is not None:
                        time_step(tmix, slot, pro, cmix)

            iteration(att=0)
            pe.wait_ge(sig["in_wg"], 16)
            iteration(att=1, pro=0)
            for name in ("in_w2", "in_mt"):
                pe.wait_ge(sig[name], 16)
            pe.wait_ge(sig["c_wl"], 4)
            pe.wait_ge(sig["c_wh"], 4)
            iteration(0, att=2, pro=1)
            with pe.Fori(1, B - 3) as g:
                iteration(g, att=g + 2, pro=g + 1)
            iteration(B - 3, att=B - 1, tmix=0, pro=B - 2)
            iteration(B - 2, tmix=1, cmix=0, pro=B - 1)
            iteration(B - 1, tmix=2, cmix=1, pro=B)
            iteration(B, tmix=3, cmix=2, pro=B + 1)
            with pe.Fori(B + 1, 2 * B - 3) as g:
                iteration(g, tmix=g - (B - 3), cmix=g - (B - 2), pro=g + 1)
            iteration(2 * B - 3, cmix=B - 1, pro=2 * B - 2)
            iteration(2 * B - 2, pro=2 * B - 1)
            iteration(2 * B - 1)
            for p in range(UNITS - LAG, UNITS):
                out_product(2 * B - 1, p)
            out_turn(2 * B)

        @block.vector
        def _(dve):
            for ap, value in ((r_p[:, :, E:E + TOP_K], -1.0), (r_carry[:, :], 0.0), (t_h[:, 0:1], 0.0),
                              (t_pp[:, 0:1], NEVER), (t_aa[:, 0:1], 0.0), (t_bb[:, 0:1], 0.0)):
                dve.memset(ap, value).then_inc(sig["c_dve"], 1)
            dve.wait_ge(sig["c_dve"], 6)
            dve.wait_ge(sig["c_dec0"], 1)
            dve.tensor_scalar(decay[:, :], decay[:, :], -1.0, None, ALU.mult).then_inc(sig["c_dec"], 1)

            def constants_set():
                dve.wait_ge(sig["c_dve"], 6)

            def row_stats(src, st, mv, n, s_st, s_mv):
                for t in range(T):
                    ins = dve.bn_stats(st[:, t, :], src[:, t, :])
                ins.then_inc(sig[s_st], 1)
                dve.wait_ge(sig[s_st], n + 1)
                dve.sem_inc(sig["stats_seen"], 1)
                for t in range(T):
                    ins = dve.bn_aggr(mv[:, t, :], st[:, t, :])
                ins.then_inc(sig[s_mv], 1)
                dve.wait_ge(sig[s_mv], n + 1)

            def normalise(dst, src, mv, rs, signal):
                for t in range(T):
                    ins = dve.tensor_scalar(dst[:, t, :], src[:, t, :], mv[:, t, 0:1], rs[:, t:t + 1],
                                            ALU.subtract, ALU.mult)
                ins.then_inc(sig[signal], 1)

            def unit(g, p, silu):
                k = UNITS * g + p
                r = p % 2
                dve.wait_ge(sig["m_th"], k + 1)
                if silu and p != EXP_UNIT:
                    dve.wait_ge(sig["m_b"], k + 1)
                    dve.wait_ge(sig["m_h"], done(k) if p == 0 else done(k - 1))
                    dve.tensor_tensor(m_v[:, r, :], m_th[:, r, :], pb[r][:, :], ALU.mult).then_inc(sig["m_v"], 1)
                    return
                through, count = ("m_ue", g - SILU_FROM + 1) if silu else ("m_u", k + 1)
                dve.scalar_tensor_tensor(out=m_u[:, r, :], in0=m_th[:, r, :], scalar=1.0, in1=pa[r][:, :],
                                         op0=ALU.add, op1=ALU.mult).then_inc(sig[through], 1)
                dve.wait_ge(sig["m_b"], k + 1)
                dve.wait_ge(sig[through], count)
                dve.wait_ge(sig["m_h"], done(k) if p == 0 else done(k - 1))
                dve.scalar_tensor_tensor(out=m_v[:, r, :], in0=m_u[:, r, :], scalar=0.5, in1=pb[r][:, :],
                                         op0=ALU.mult, op1=ALU.mult).then_inc(sig["m_v"], 1)

            def add_out(g):
                if g is None or (isinstance(g, int) and g == 0):
                    return
                c = sequence_before(g)
                dve.wait_ge(sig["m_yT"], g)
                dve.tensor_tensor(wide(chunk(c)), wide(chunk(c)), pv[:, :], ALU.add).then_inc(sig["m_x"], 1)

            def att_step(n, slot):
                if slot == 0:
                    if isinstance(n, int):
                        dve.wait_ge(sig["in_x0" if n == 0 else "in_x1"], 16)
                    row_stats(chunk(n), a_st, a_mv, n, "a_stats", "a_mvs")
                    dve.tensor_scalar(a_ve[:, 0:T], a_mv[:, :, 1], EPS, None, ALU.add).then_inc(sig["a_vedone"], 1)
                if slot == 2:
                    dve.wait_ge(sig["a_rstd"], n + 1)
                    normalise(a_xn, chunk(n), a_mv, a_rs, "a_xn")
                if slot == 6 and isinstance(n, int) and n == 0:
                    for k, (src, blocks, high, loaded) in enumerate((
                            (w_stage[:, 0:PAIRS, :], slice(0, PAIRS), w1h, "in_w1"),
                            (w_stage[:, PAIRS:2 * PAIRS, :], slice(0, PAIRS), w3h, "in_w3"),
                            (mt[:, M_S1:M_S1 + 1, :], slice(PAIRS, UNITS), w1h, "in_mt"),
                            (mt[:, M_S3:M_S3 + 1, :], slice(PAIRS, UNITS), w3h, "in_mt"))):
                        dve.wait_ge(sig[loaded], 16)
                        dve.tensor_copy(high[:, blocks, :], src).then_inc(sig["c_wh"], 1)
                if slot == 8:
                    row_max(n, 0, (0, 1), (0, P))
                if slot == 10:
                    row_max(n, 1, (2,), (0,))
                if slot == 11:
                    add_att(n, 0, (0, 1))
                if slot == 13:
                    row_max(n, 2, (3,), (0,))
                if slot == 14:
                    add_att(n, 1, (2,))
                if slot == 16:
                    add_att(n, 2, (3,))

            def row_max(n, i, tiles, at):
                dve.wait_ge(sig["a_s"], 3 * n + i + 1)
                for t, o in zip(tiles, at):
                    ins = dve.tensor_reduce(a_mx[:, t:t + 1], pv[:, o:o + P * (t + 1)], AX_X, ALU.max)
                ins.then_inc(sig["a_mx"], 1)
                dve.wait_ge(sig["a_mx"], 3 * n + i + 1)
                a, b = tiles[0], tiles[-1] + 1
                dve.tensor_scalar(a_nm[:, a:b], a_mx[:, a:b], -SCALE, None, ALU.mult).then_inc(sig["a_nm"], 1)

            def add_att(n, i, tiles):
                a, b = tiles[0], tiles[-1] + 1
                dve.wait_ge(sig["a_exp"], 3 * n + i + 1)
                dve.reciprocal(a_ri[:, a:b], a_sum[:, a:b]).then_inc(sig["a_ri"], 1)
                dve.wait_ge(sig["a_ri"], 3 * n + i + 1)
                dve.wait_ge(sig["a_o"], 3 * n + i + 1)
                for t in tiles:
                    ins = dve.scalar_tensor_tensor(out=chunk(n)[:, t, :], in0=pu[:, P * t:P * (t + 1)],
                                                   scalar=a_ri[:, t:t + 1], in1=chunk(n)[:, t, :],
                                                   op0=ALU.mult, op1=ALU.add)
                ins.then_inc(sig["a_add"], 1)

            def pro_step(q, slot, cmix):
                if slot == 1:
                    if layer_of(q) == 0:
                        dve.wait_ge(sig["a_add"], 3 * q + 3)
                    else:
                        dve.wait_ge(sig["f_x"], 2 * (q - B) + 2)
                    row_stats(chunk(sequence(q)), r_st, r_mv, q, "r_stats", "r_mvs")
                    dve.tensor_scalar(r_ve[:, :], r_mv[:, :, 1], EPS, None, ALU.add).then_inc(sig["r_vedone"], 1)
                if slot == 3:
                    dve.wait_ge(sig["r_rstd"], q + 1)
                    normalise(r_xn, chunk(sequence(q)), r_mv, r_rs, "r_xn")
                if slot == 8:
                    dve.wait_ge(sig["r_lgps"], q + 1)
                    lg = router_bank(cmix)[:, 0:T * E].rearrange("p (t e) -> p t e", t=T)
                    dve.tensor_reduce(r_mx[:, :], lg, AX_X, ALU.max).then_inc(sig["r_mx"], 1)
                    dve.wait_ge(sig["r_mx"], q + 1)
                    dve.tensor_tensor(r_lg[:, :, :], lg, r_mx[:, :].unsqueeze(2).broadcast_to([P, T, E]),
                                      ALU.subtract).then_inc(sig["r_lg"], 1)
                if slot == 10:
                    dve.wait_ge(sig["r_ex"], q + 1)
                    dve.tensor_reduce(r_sum[:, :], r_ex[:, :, :], AX_X, ALU.add).then_inc(sig["r_sum"], 1)
                    dve.wait_ge(sig["r_sum"], q + 1)
                    dve.reciprocal(r_ri[:, :], r_sum[:, :]).then_inc(sig["r_ri"], 1)
                    dve.wait_ge(sig["r_ri"], q + 1)
                    dve.scalar_tensor_tensor(out=r_p[:, :, 0:E], in0=r_ex[:, :, :], scalar=1.0,
                                             in1=r_ri[:, :].unsqueeze(2).broadcast_to([P, T, E]),
                                             op0=ALU.mult, op1=ALU.mult).then_inc(sig["r_p"], 1)
                    constants_set()
                    dve.wait_ge(sig["r_p"], q + 1)
                    for t in range(T):
                        ins = dve.max(r_top[:, t, :], r_p[:, t, :])
                    ins.then_inc(sig["r_top"], 1)
                if slot == 12:
                    dve.wait_ge(sig["r_top"], q + 1)
                    dve.memset(r_top[:, :, TOP_K:8], -1.0).then_inc(sig["r_pad"], 1)
                    constants_set()
                    dve.wait_ge(sig["r_pad"], q + 1)
                    for t in range(T):
                        ins = dve.match_replace(r_rep[:, t, :], r_top[:, t, :], r_p[:, t, :], -2.0)
                    ins.then_inc(sig["r_rep"], 1)
                    dve.wait_ge(sig["r_rep"], q + 1)
                    dve.tensor_scalar(r_sel[:, :, :], r_rep[:, :, 0:E], 0.0, None, ALU.is_lt).then_inc(sig["r_sel"], 1)
                    dve.wait_ge(sig["r_sel"], q + 1)
                    dve.tensor_tensor(r_ws[:, :, :], r_sel[:, :, :], r_p[:, :, 0:E], ALU.mult).then_inc(sig["r_ws"], 1)
                if slot == 14:
                    dve.wait_ge(sig["r_cnt"], q + 1)
                    wait(dve, "r_carry", q)
                    dve.tensor_tensor(r_pos[:, :, :], pq[:, 0:T * E].rearrange("p (t e) -> p t e", t=T),
                                      r_carry[:, :].unsqueeze(1).broadcast_to([P, T, E]), ALU.add).then_inc(sig["r_pos"], 1)
                    dve.wait_ge(sig["r_pos"], q + 1)
                    dve.wait_ge(sig["r_ws"], q + 1)
                    dve.scalar_tensor_tensor(out=wide(r_w[:, :, :]), in0=wide(r_pos[:, :, :]), scalar=float(CAPACITY),
                                             in1=wide(r_ws[:, :, :]), op0=ALU.is_le, op1=ALU.mult).then_inc(sig["r_w"], 1)
                    if isinstance(q, int) and q == B - 1:
                        dve.memset(r_carry[:, :], 0.0).then_inc(sig["r_carry"], 1)
                    else:
                        dve.tensor_tensor(r_carry[:, :], pq[:, T * E:(T + 1) * E], r_carry[:, :],
                                          ALU.add).then_inc(sig["r_carry"], 1)

            def time_step(m, slot):
                if slot == 0:
                    dve.wait_ge(sig["m_x"], done(m + 1))
                    row_stats(chunk(m), t_st, t_mv, m, "t_stats", "t_mvs")
                    dve.tensor_scalar(t_ve[:, 0:T], t_mv[:, :, 1], EPS, None, ALU.add).then_inc(sig["t_ve"], 1)
                    dve.tensor_scalar(t_ve[:, T:2 * T], t_mv[:, :, 1], 1.0 + EPS, EPS * EPS, ALU.mult,
                                      ALU.add).then_inc(sig["t_ve"], 1)
                if slot == 2:
                    dve.wait_ge(sig["t_rstd"], m + 1)
                    normalise(t_hn, chunk(m), t_mv, t_rs[:, T:2 * T], "t_hn")
                if slot == 5:
                    normalise(t_u, chunk(m), t_mv, t_rs[:, 0:T], "t_u")
                if slot == 6:
                    dve.wait_ge(sig["t_d"], m + 1)
                    for dst, c in ((t_xk, MIX_K), (t_xv, MIX_V), (t_xr, MIX_R)):
                        dve.scalar_tensor_tensor(out=dst[:, :], in0=t_d[:, :], scalar=vec[:, c:c + 1], in1=t_h[:, 0:S],
                                                 op0=ALU.mult, op1=ALU.add).then_inc(sig["t_xk"], 1)
                if slot == 9:
                    dve.wait_ge(sig["t_k"], m + 1)
                    dve.tensor_tensor_scan(out=t_pp[:, 1:1 + S], data0=decay[:, 0:1].to_broadcast([P, S]),
                                           data1=t_k[:, :], initial=NEVER, op0=ALU.add, op1=ALU.max)\
                       .then_inc(sig["t_pp"], 1)
                    dve.wait_ge(sig["t_pp"], m + 1)
                    dve.scalar_tensor_tensor(out=t_qq[:, :], in0=t_k[:, :], scalar=vec[:, FIRST:FIRST + 1],
                                             in1=t_pp[:, 0:S], op0=ALU.add, op1=ALU.max).then_inc(sig["t_qq"], 1)
                    dve.scalar_tensor_tensor(out=t_ea[:, 0, :], in0=t_pp[:, 0:S], scalar=decay[:, 0:1],
                                             in1=t_pp[:, 1:1 + S], op0=ALU.add, op1=ALU.subtract).then_inc(sig["t_a0"], 1)
                    dve.wait_ge(sig["t_qq"], m + 1)
                    dve.scalar_tensor_tensor(out=t_eb[:, 1, :], in0=t_k[:, :], scalar=vec[:, FIRST:FIRST + 1],
                                             in1=t_qq[:, :], op0=ALU.add, op1=ALU.subtract).then_inc(sig["t_b1"], 1)
                if slot == 11:
                    dve.wait_ge(sig["t_ev"], m + 1)
                    dve.tensor_tensor_scan(out=t_aa[:, 1:1 + S], data0=t_ea[:, 0, :], data1=t_ev[:, :], initial=0.0,
                                           op0=ALU.mult, op1=ALU.add).then_inc(sig["t_aa"], 1)
                    dve.tensor_tensor_scan(out=t_bb[:, 1:1 + S], data0=t_ea[:, 0, :], data1=t_ea[:, 1, :], initial=0.0,
                                           op0=ALU.mult, op1=ALU.add).then_inc(sig["t_bb"], 1)
                    dve.wait_ge(sig["t_expb"], m + 1)
                    dve.wait_ge(sig["t_aa"], m + 1)
                    dve.tensor_tensor(t_n1[:, :], t_eb[:, 0, :], t_aa[:, 0:S], ALU.mult).then_inc(sig["t_n1"], 1)
                    dve.wait_ge(sig["t_bb"], m + 1)
                    dve.tensor_tensor(t_d1[:, :], t_eb[:, 0, :], t_bb[:, 0:S], ALU.mult).then_inc(sig["t_d1"], 1)
                if slot == 12:
                    dve.wait_ge(sig["t_d1"], m + 1)
                    dve.tensor_tensor(t_d1[:, :], t_d1[:, :], t_eb[:, 1, :], ALU.add).then_inc(sig["t_den"], 1)
                    dve.wait_ge(sig["t_n2"], m + 1)
                    dve.wait_ge(sig["t_n1"], m + 1)
                    dve.tensor_tensor(t_n1[:, :], t_n1[:, :], t_n2[:, :], ALU.add).then_inc(sig["t_num"], 1)
                    dve.wait_ge(sig["t_den"], m + 1)
                    invert(0)
                if slot == 13:
                    invert(1)
                    invert(2)
                if slot == 14:
                    invert(3)
                if slot == 15:
                    dve.wait_ge(sig["t_ri"], T * m + T)
                    dve.wait_ge(sig["t_num"], m + 1)
                    dve.tensor_tensor(t_ri[:, :], t_n1[:, :], t_ri[:, :], ALU.mult).then_inc(sig["t_y"], 1)
                    dve.wait_ge(sig["t_y"], m + 1)
                    dve.wait_ge(sig["t_r"], m + 1)
                    dve.scalar_tensor_tensor(out=t_n1[:, :], in0=t_r[:, :], scalar=1.0, in1=t_ri[:, :],
                                             op0=ALU.add, op1=ALU.mult).then_inc(sig["t_rw"], 1)
            def channel_step(m, slot):
                if slot == 3:
                    if isinstance(m, int) and m == 0:
                        dve.wait_ge(sig["a_add"], 3 * B)
                        dve.memset(f_h[:, 0:1], 0.0).then_inc(sig["f_zero"], 1)
                    dve.wait_ge(sig["t_ops"], m + 1)
                    dve.wait_ge(sig["t_u"], m + 1)
                    dve.scalar_tensor_tensor(out=wide(t_u2[:, :, :]), in0=pq[:, :], scalar=0.5,
                                             in1=wide(t_u[:, :, :]), op0=ALU.mult, op1=ALU.add).then_inc(sig["t_u2"], 1)
                if slot == 4:
                    dve.wait_ge(sig["t_u2"], m + 1)
                    row_stats(t_u2, a_st, a_mv, m, "f_stats", "f_mvs")
                    dve.tensor_scalar(a_ve[:, 0:T], a_mv[:, :, 1], EPS, None, ALU.add).then_inc(sig["f_ve"], 1)
                if slot == 7:
                    dve.wait_ge(sig["f_rstd"], m + 1)
                    normalise(f_hn, t_u2, a_mv, a_rs, "f_hn")
                    dve.tensor_tensor(wide(chunk(m)), wide(chunk(m)), wide(t_u2[:, :, :]), ALU.add)\
                       .then_inc(sig["f_x"], 1)
                if slot == 10:
                    dve.wait_ge(sig["f_d"], m + 1)
                    for dst, c in ((f_xk, FMIX_K), (f_xr, FMIX_R)):
                        dve.scalar_tensor_tensor(out=dst[:, :], in0=f_d[:, :], scalar=vec[:, c:c + 1], in1=f_h[:, 0:S],
                                                 op0=ALU.mult, op1=ALU.add).then_inc(sig["f_xk"], 1)
                if slot == 17:
                    dve.wait_ge(sig["f_tr2"], m + 1)
                    dve.wait_ge(sig["f_kv"], m + 1)
                    dve.scalar_tensor_tensor(out=f_g[:, :], in0=f_tr[:, :], scalar=1.0, in1=pu[:, :],
                                             op0=ALU.add, op1=ALU.mult).then_inc(sig["f_g"], 1)
                    dve.wait_ge(sig["f_g"], m + 1)
                    dve.wait_ge(sig["f_x"], 2 * m + 1)
                    dve.scalar_tensor_tensor(out=wide(chunk(m)), in0=f_g[:, :], scalar=0.5, in1=wide(chunk(m)),
                                             op0=ALU.mult, op1=ALU.add).then_inc(sig["f_x"], 1)

            def invert(i):
                part = slice(P * i, P * (i + 1))
                dve.reciprocal(t_ri[:, part], t_d1[:, part]).then_inc(sig["t_ri"], 1)

            def iteration(g=None, att=None, tmix=None, cmix=None, pro=None, silu=False):
                for slot in range(UNITS + 1):
                    if g is not None and slot < UNITS:
                        unit(g, slot, silu)
                    if slot == LAG + 1:
                        add_out(g)
                    if att is not None:
                        att_step(att, slot)
                    if tmix is not None:
                        time_step(tmix, slot)
                    if pro is not None:
                        pro_step(pro, slot, cmix)
                    if cmix is not None:
                        channel_step(cmix, slot)

            iteration(att=0)
            iteration(att=1, pro=0)
            dve.wait_ge(sig["in_xr"], 16 * (B - 2))
            iteration(0, att=2, pro=1)
            with dve.Fori(1, B - 3) as g:
                iteration(g, att=g + 2, pro=g + 1)
            dve.wait_ge(sig["in_vec"], 16)
            dve.wait_ge(sig["c_dec"], 1)
            iteration(B - 3, att=B - 1, tmix=0, pro=B - 2)
            iteration(B - 2, tmix=1, cmix=0, pro=B - 1, silu=True)
            iteration(B - 1, tmix=2, cmix=1, pro=B, silu=True)
            iteration(B, tmix=3, cmix=2, pro=B + 1, silu=True)
            with dve.Fori(B + 1, 2 * B - 3) as g:
                iteration(g, tmix=g - (B - 3), cmix=g - (B - 2), pro=g + 1, silu=True)
            iteration(2 * B - 3, cmix=B - 1, pro=2 * B - 2, silu=True)
            iteration(2 * B - 2, pro=2 * B - 1, silu=True)
            iteration(2 * B - 1, silu=True)
            add_out(2 * B)


def kernel(**inputs):
    import numpy as np
    import concourse.bacc as _bacc
    from concourse.bass_utils import run_bass_kernel_spmd as _run

    def get(name):
        return np.asarray(inputs["L0_" + name])

    def packed(blocks):
        return np.ascontiguousarray(np.stack(blocks, axis=1))

    key = get("attn_b_Wkey").T
    val = get("attn_b_Wval").T
    arrays = {
        "x": np.ascontiguousarray(get("attn_a_embeddings")),
        "att_mats": packed([get("attn_a_W_Q").T, get("attn_a_W_K").T, get("attn_a_W_V")]),
        "mats": packed(
            [get("attn_b_" + n).T for n in ("Wk", "Wv", "Wr", "Wo", "Wrec")]
            + [get("ffn_" + n) for n in ("Ws1", "Ws3", "Ws2")]
            + [key[:, P * j:P * (j + 1)] for j in range(FB)]
            + [val[P * j:P * (j + 1), :] for j in range(FB)]),
        "vecs": packed([get("attn_b_" + n).reshape(-1) for n in (
            "ln1_w", "ln1_b", "ln2_w", "ln2_b", "att_tmk", "att_tmv", "att_tmr", "time_decay", "time_first",
            "ffn_tmk", "ffn_tmr")]),
        "w_gate": np.ascontiguousarray(get("ffn_Wg")),
        "w1": np.ascontiguousarray(get("ffn_W1").transpose(1, 0, 2).reshape(D, PAIRS, P)),
        "w3": np.ascontiguousarray(get("ffn_W3").transpose(1, 0, 2).reshape(D, PAIRS, P)),
        "w2": np.ascontiguousarray(get("ffn_W2").reshape(PAIRS, P, D).transpose(1, 0, 2)),
    }
    nc = _bacc.Bacc("TRN2", target_bir_lowering=False, num_devices=1)
    args = [nc.dram_tensor("in_" + n, a.shape, mybir.dt.from_np(a.dtype), kind="ExternalInput").ap() for n, a in arrays.items()]
    args.append(nc.dram_tensor("x_out", (B, S, D), F32, kind="ExternalOutput").ap())
    hybrid_kernel(nc, *args)
    r = _run(nc, [{"in_" + n: a for n, a in arrays.items()}], core_ids=[0])
    return r.results[0]["x_out"]
```

```python
from contextlib import ExitStack

import concourse.bass as bass
from concourse import mybir

ALU = mybir.AluOpType
ACT = mybir.ActivationFunctionType
AX_X = mybir.AxisListType.X
F32 = mybir.dt.float32
F32R = mybir.dt.float32r
BF16 = mybir.dt.bfloat16

P = 128
B = 8
S = 512
D = 128
T = S // P
E = 32
H = 64
TOP_K = 4
CAPACITY = 4 * (B * S * TOP_K) // E
PAIRS = E * H // P
UNITS = PAIRS + 1
GROUPS = 4
GP = PAIRS // GROUPS
GRING = 2
LATE = B - 2
PHASE_FROM = (0, LATE, 2 * B - 2)
LAG = 4
SPLIT_LAG = 2
LOW_ON_POOL = (
    (0, 4, 6, 7, 8, 9, 11, 12, 14, 15),
    (6, 9, 12, 15),
    (2, 9, 14),
)
TANH_UNITS = {False: tuple(range(9, 14)), True: (10,)}
HIDDEN_AT = (0, 1) * 7 + (0, 1, 2)
SPLIT_AT = (0, 1, 2) * 3 + (0, 1, 2, 3) * 2
FB = 4
EPS = 1e-5
SCALE = 1.0 / float(D) ** 0.5
MASKED = -1.0e30
NEVER = -1.0e38
BASE = 1

LN1_W, LN1_B, LN2_W, LN2_B, MIX_K, MIX_V, MIX_R, DECAY, FIRST, FMIX_K, FMIX_R = range(11)
M_K, M_V, M_R, M_O, M_REC, M_S1, M_S3, M_S2, M_VAL = 0, 1, 2, 3, 4, 5, 6, 7, 8
N_MATS = 12


def since_last_use(places, p):
    return next(n for n in range(1, len(places) + 1) if places[(p - n) % len(places)] == places[p])


def hybrid_kernel(nc, x_in, att_mats, mats, key_in, vecs, w_gate, w1_in, w3_in, w2_in, x_out):
    with ExitStack() as ctx:
        def sb(name, shape, dt=F32):
            return ctx.enter_context(nc.sbuf_tensor(name, shape, dt))

        def bank(name, dt=F32):
            return ctx.enter_context(nc.psum_tensor(name, [P, 512], dt))

        def sem(name):
            return ctx.enter_context(nc.semaphore(name))

        def wide(ap):
            return ap.rearrange("p t d -> p (t d)")

        x_sb = sb("x_sb", [P, B, T, D])
        am = sb("am", [P, 3, D])
        mt = sb("mt", [P, N_MATS, D])
        vec = sb("vec", [P, 11])
        wg = sb("wg", [P, E])
        w1h = sb("w1h", [P, UNITS, P], F32R)
        w1l = sb("w1l", [P, UNITS, P], F32R)
        w3h = sb("w3h", [P, UNITS, P], F32R)
        w3l = sb("w3l", [P, UNITS, P], F32R)
        key_h = sb("key_h", [P, FB * P], F32R)
        key_l = sb("key_l", [P, FB * P], F32R)
        w2h = sb("w2h", [P, UNITS, P], F32R)
        w2l = sb("w2l", [P, UNITS, P], F32R)
        qk_m = sb("qk_m", [P, D])
        ident = sb("ident", [P, P])
        ident_b = sb("ident_b", [P, P], BF16)
        causal_b = sb("causal_b", [P, P], BF16)
        tri_b = sb("tri_b", [P, P], BF16)
        ones_b = sb("ones_b", [P, P], BF16)
        minus_half = sb("minus_half", [P, 2 * T])
        decay = sb("decay", [P, 1])

        a_st = sb("a_st", [P, T, 6])
        a_mv = sb("a_mv", [P, T, 2])
        a_ve = sb("a_ve", [P, T])
        a_rs = sb("a_rs", [P, T])
        a_xn = sb("a_xn", [P, T, D])
        a_xT = sb("a_xT", [P, 1 + S])
        a_g = sb("a_g", [P, S])
        a_v = sb("a_v", [P, T, D])
        a_p = sb("a_p", [P, S])
        a_pT = sb("a_pT", [P, S])
        a_mx = sb("a_mx", [P, T])
        a_nm = sb("a_nm", [P, T])
        a_sum = sb("a_sum", [P, T])
        a_ri = sb("a_ri", [P, T])

        r_st = sb("r_st", [P, T, 6])
        r_mv = sb("r_mv", [P, T, 2])
        r_ve = sb("r_ve", [P, T])
        r_rs = sb("r_rs", [P, T])
        r_mx = sb("r_mx", [P, T])
        r_lg = sb("r_lg", [P, T, E])
        r_ex = r_lg
        r_sum = sb("r_sum", [P, T])
        r_ri = sb("r_ri", [P, T])
        r_p = sb("r_p", [P, T, E + TOP_K])
        r_top = sb("r_top", [P, T, 8])
        r_rep = sb("r_rep", [P, T, E + TOP_K])
        r_sel = sb("r_sel", [P, T, E], BF16)
        r_ws = sb("r_ws", [P, T, E])
        r_pos = sb("r_pos", [P, T, E])
        r_w = sb("r_w", [P, T, E])
        r_carry = sb("r_carry", [P, E])
        r_wT = sb("r_wT", [E, S])

        m_xh = sb("m_xh", [P, 2, S], F32R)
        m_xl = sb("m_xl", [P, 2, S], F32R)
        m_wb = sb("m_wb", [P, GRING * GP, S])
        w_stage = m_wb[:, :, :].rearrange("p a (b c) -> p (a b) c", c=P)
        m_th = sb("m_th", [P, 2, S])
        m_v = sb("m_v", [P, 2, S])
        m_h = sb("m_h", [P, 3, S])
        m_hh = sb("m_hh", [P, 4, S], F32R)
        m_hl = sb("m_hl", [P, 4, S], F32R)
        m_y = sb("m_y", [P, S])

        t_u = sb("t_u", [P, T, D])
        t_h = sb("t_h", [P, 1 + S])
        t_xk = sb("t_xk", [P, S])
        t_xv = sb("t_xv", [P, S])
        t_xr = sb("t_xr", [P, S])
        t_k = sb("t_k", [P, S])
        t_v = sb("t_v", [P, S])
        t_r = sb("t_r", [P, S])
        t_pp = sb("t_pp", [P, 1 + S])
        t_aa = sb("t_aa", [P, 1 + S])
        t_bb = sb("t_bb", [P, 1 + S])
        t_qq = sb("t_qq", [P, S])
        t_ea = sb("t_ea", [P, 2, S])
        t_eb = sb("t_eb", [P, 2, S])
        t_n1 = sb("t_n1", [P, S])
        t_ri = sb("t_ri", [P, S])
        t_u2 = sb("t_u2", [P, T, D])
        f_kk = sb("f_kk", [P, FB, S])
        f_tr = sb("f_tr", [P, S])
        f_xh = sb("f_xh", [P, S], F32R)
        f_xl = sb("f_xl", [P, S], F32R)
        t_ev, t_n2, t_d1, t_d = t_xk, t_xv, t_xr, t_n1
        t_hn = t_ri[:, :].rearrange("p (t d) -> p t d", t=T)
        w2_stage = f_kk[:, :, :].rearrange("p a (b c) -> p (a b) c", c=P)
        f_hn, f_h, f_d, f_xk, f_xr = a_xn, a_xT, a_g, a_p, a_pT
        f_g = a_p[:, :]
        r_xn, r_xT = t_k[:, :].rearrange("p (t d) -> p t d", t=T), t_v
        key_stage = t_k[:, :]
        r_nm, t_nm, f_nm = sb("r_nm", [P, T]), sb("t_nm", [P, 2 * T]), a_nm
        t_st, t_mv = sb("t_st", [P, T, 6]), sb("t_mv", [P, T, 2])
        t_ve, t_rs = sb("t_ve", [P, 2 * T]), sb("t_rs", [P, 2 * T])

        pa = [bank("pa0"), bank("pa1")]
        pb = [bank("pb0"), bank("pb1")]
        py = bank("py")
        pq = bank("pq")
        pu, pv = bank("pu"), bank("pv")

        w_scratch = nc.dram_tensor("w_scratch", [2 * B, GROUPS, GP, 2, S], F32, kind="Internal").ap()

        names = (
            "in_x0 in_x1 in_xr in_am in_vec in_wg in_w1 in_w3 in_w2 in_mt in_key "
            "c_pool c_dve c_dec0 c_dec c_qkm_ps c_qkm "
            "a_stats a_mvs a_vedone a_rstd a_xn a_tr a_xT a_gps a_vps a_g a_v a_s a_mx a_nm a_exp a_pT a_pTs a_o a_ri a_add "
            "r_stats r_mvs r_vedone r_rstd r_nm r_xn r_tr r_xT m_xh m_xl r_lgps r_mx r_lg r_ex r_sum r_ri r_p r_top r_pad r_rep "
            "r_sel r_ws r_cnt r_pos r_w r_carry r_wTps r_wT w_out "
            "c_wh c_wl m_a m_b m_th m_u m_u_late m_v m_h m_hh "
            "m_hl_dve0 m_hl_pool0 m_hl_dve1 m_hl_pool1 m_hl_dve2 m_hl_pool2 m_y m_ys m_yT m_x "
            "t_stats t_mvs t_ve t_rstd t_nm t_hn t_tr t_h t_d t_xk t_kps t_vps t_rps t_k t_v t_r t_pp t_a0 t_a1 t_qq t_b0 t_b1 "
            "t_expa t_expb t_ev t_n2 t_aa t_bb t_n1 t_d1 t_den t_num t_ri t_y t_rw t_ops t_u t_u2 "
            "f_stats f_mvs f_ve f_rstd f_nm f_hn f_tr f_h f_d f_xk f_xh f_xl f_key f_rk f_kk f_rec f_zero f_tr2 f_kv f_g f_x "
            "out_done stats_seen"
        ).split()
        sig = {n: sem("s_" + n) for n in names}
        wb_first = [sem(f"s_wb_first{p}") for p in range(GP)]
        wb_in = [sem(f"s_wb_in{j}") for j in range(GROUPS)]

        def wait(eng, name, value):
            if not (isinstance(value, int) and value <= 0):
                eng.wait_ge(sig[name], value)

        def done(n):
            return n + BASE

        block = ctx.enter_context(nc.Block())
        xv = x_in.rearrange("b (t p) d -> b p t d", p=P)
        ov = x_out.rearrange("b (t p) d -> b p t d", p=P)

        def layer_of(q):
            return (0 if q < B else 1) if isinstance(q, int) else (0 if q.max_val < B else 1)

        def sequence(q):
            return q if layer_of(q) == 0 else q - B

        def sequence_before(g):
            if isinstance(g, int):
                return (g - 1) % B
            return sequence(g) - 1

        def unit_before(g, p, lag):
            return (g, p - lag) if p >= lag else (g - 1, UNITS + p - lag)

        def gated(p):
            return m_v[:, p % 2, :] if p < PAIRS else m_h[:, HIDDEN_AT[p], :]

        def wait_weighted(eng, g, p):
            if isinstance(g, int) and g < 0:
                return
            eng.wait_ge(sig["m_h"], done(PAIRS * g + p + 1))

        def front(step):
            step(att=1, pro=0, lead=5)

        def is_late(g):
            return (g if isinstance(g, int) else g.max_val) >= LATE

        def by_tanh(g, p):
            return p in TANH_UNITS[is_late(g)]

        def phase(g):
            last = g if isinstance(g, int) else g.max_val
            return sum(last >= first for first in PHASE_FROM[1:])

        def low_on_pool(g, p):
            return p in LOW_ON_POOL[phase(g)]

        def low_signal(g, p):
            pool, i = low_on_pool(g, p), phase(g)
            units = [u for u in range(UNITS) if low_on_pool(g, u) == pool]
            return f"m_hl_{'pool' if pool else 'dve'}{i}", len(units) * (g - PHASE_FROM[i]) + units.index(p) + 1

        def wait_split(eng, g, p):
            if isinstance(g, int) and g < 0:
                return
            name, count = low_signal(g, p)
            eng.wait_ge(sig[name], count)

        def split_low(eng, g, p):
            if isinstance(g, int) and g < 0:
                return
            at = SPLIT_AT[p]
            eng.wait_ge(sig["m_hh"], UNITS * g + p + 1)
            eng.tensor_tensor(m_hl[:, at, :], m_h[:, HIDDEN_AT[p], :], m_hh[:, at, :].bitcast(F32), ALU.subtract)\
               .then_inc(sig[low_signal(g, p)[0]], 1)

        def chunk(c):
            return x_sb[:, c, :, :]

        def out_bank(tmix, cmix):
            return pq if tmix is None and cmix is None else pv

        def router_bank(cmix):
            return pq if cmix is None else pv

        @block.sync
        def _(sp):
            sp.dma_start(chunk(0), xv[0]).then_inc(sig["in_x0"], 16)
            sp.dma_start(w_stage[:, 0:PAIRS, :], w1_in).then_inc(sig["in_w1"], 16)
            sp.dma_start(w_stage[:, PAIRS:2 * PAIRS, :], w3_in).then_inc(sig["in_w3"], 16)
            sp.dma_start(chunk(1), xv[1]).then_inc(sig["in_x1"], 16)
            sp.dma_start(wg[:, :], w_gate).then_inc(sig["in_wg"], 16)
            sp.dma_start(w2_stage, w2_in).then_inc(sig["in_w2"], 16)
            sp.dma_start(mt[:, :, :], mats).then_inc(sig["in_mt"], 16)
            sp.dma_start(key_stage, key_in).then_inc(sig["in_key"], 16)
            for c in range(2, B):
                sp.dma_start(chunk(c), xv[c]).then_inc(sig["in_xr"], 16)
            for name in ("m_v", "m_h", "m_y", "m_x"):
                sp.sem_inc(sig[name], BASE)

            def spread_weights(q):
                sp.wait_ge(sig["r_wT"], q + 1)
                sp.dma_start(w_scratch[q].rearrange("j a h s -> (j a h) s"), r_wT[:, :]).then_inc(sig["w_out"], 16)
                sp.wait_ge(sig["w_out"], 16 * q + 16)
                for j in range(GROUPS):
                    if j >= GRING:
                        sp.wait_ge(sig["m_h"], done(PAIRS * q + GP * (j - GRING + 1)))
                    elif isinstance(q, int) and q == 0:
                        sp.wait_ge(sig["c_wl"], 2)
                    else:
                        sp.wait_ge(sig["m_h"], done(PAIRS * (q - 1) + GP * (GROUPS - GRING + j + 1)))
                    at = GP * (j % GRING)
                    if isinstance(q, int) and q == 0 and j == 0:
                        for p in range(GP):
                            for h in range(2):
                                sp.dma_start(m_wb[H * h:H * (h + 1), p, :],
                                             w_scratch[q, j, p, h, :].partition_broadcast(H)).then_inc(wb_first[p], 16)
                        continue
                    for h in range(2):
                        sp.dma_start(m_wb[H * h:H * (h + 1), at:at + GP, :],
                                     w_scratch[q, j, :, h, :].partition_broadcast(H)).then_inc(wb_in[j], 16)

            def store(c):
                sp.wait_ge(sig["m_x"], done(B + c + 1))
                sp.dma_start(ov[c], chunk(c)).then_inc(sig["out_done"], 16)

            spread_weights(0)
            with sp.Fori(1, B + 2) as q:
                spread_weights(q)
            with sp.Fori(B + 2, 2 * B) as q:
                spread_weights(q)
                store(q - (B + 2))
            store(B - 2)
            store(B - 1)
            sp.wait_ge(sig["out_done"], 16 * B)

        @block.gpsimd
        def _(pool):
            pool.memset(ident[:, :], 0.0).then_inc(sig["c_pool"], 1)
            pool.memset(ident_b[:, :], 0.0).then_inc(sig["c_pool"], 1)
            pool.memset(causal_b[:, :], 0.0).then_inc(sig["c_pool"], 1)
            pool.memset(tri_b[:, :], 1.0).then_inc(sig["c_pool"], 1)
            pool.memset(ones_b[:, :], 1.0).then_inc(sig["c_pool"], 1)
            pool.memset(minus_half[:, :], -0.5).then_inc(sig["c_pool"], 1)
            pool.wait_ge(sig["c_pool"], 6)
            for m in (ident, ident_b):
                pool.affine_select(out=m[:, :], in_=m[:, :], compare_op=ALU.not_equal, fill=1.0, base=0,
                                   pattern=[[-1, P]], channel_multiplier=1).then_inc(sig["c_pool"], 1)
            pool.affine_select(out=causal_b[:, :], in_=causal_b[:, :], compare_op=ALU.is_ge, fill=MASKED, base=0,
                               pattern=[[-1, P]], channel_multiplier=1).then_inc(sig["c_pool"], 1)
            pool.affine_select(out=tri_b[:, :], in_=tri_b[:, :], compare_op=ALU.is_ge, fill=0.0, base=0,
                               pattern=[[1, P]], channel_multiplier=-1).then_inc(sig["c_pool"], 1)

            def rsqrt(out, in_, ready, n, signal):
                pool.wait_ge(sig[ready], n)
                pool.tensor_tensor(out, in_, minus_half[:, 0:out.shape[1]], ALU.pow).then_inc(sig[signal], 1)

            def unit(g, p):
                if p == PAIRS:
                    return
                if isinstance(g, int) and g == 0 and p < GP:
                    pool.wait_ge(wb_first[p], 32)
                elif p % GP == 0:
                    pool.wait_ge(wb_in[p // GP], 32 * g + 32 if p else 32 * g)
                pool.wait_ge(sig["m_v"], done(UNITS * g + p + 1))
                wait_split(pool, *unit_before(g, p, since_last_use(HIDDEN_AT, p)))
                pool.tensor_tensor(m_h[:, HIDDEN_AT[p], :], gated(p), m_wb[:, p % (GRING * GP), :],
                                   ALU.mult).then_inc(sig["m_h"], 1)

            def split_weights(blocks, high, low, src, loaded):
                pool.wait_ge(sig[loaded[0]], 16)
                pool.wait_ge(sig["c_wh"], loaded[1])
                pool.tensor_tensor(low[:, blocks, :], src, high[:, blocks, :].bitcast(F32),
                                   ALU.subtract).then_inc(sig["c_wl"], 1)

            def pro_step(q, slot):
                if slot == 2:
                    rsqrt(r_rs[:, :], r_ve[:, :], "r_vedone", q + 1, "r_rstd")
                if slot == 6:
                    pool.wait_ge(sig["r_xT"], q + 1)
                    pool.wait_ge(sig["m_xh"], q + 1)
                    pool.tensor_tensor(m_xl[:, q % 2, :], r_xT[:, :], m_xh[:, q % 2, :].bitcast(F32),
                                       ALU.subtract).then_inc(sig["m_xl"], 1)

            def time_step(m, slot):
                if slot == 0:
                    rsqrt(t_rs[:, :], t_ve[:, :], "t_ve", 2 * m + 2, "t_rstd")
                if slot == 4:
                    pool.wait_ge(sig["t_h"], m + 1)
                    pool.tensor_tensor(t_d[:, :], t_h[:, 1:1 + S], t_h[:, 0:S], ALU.subtract).then_inc(sig["t_d"], 1)
                if slot == 8:
                    pool.wait_ge(sig["t_pp"], m + 1)
                    pool.tensor_tensor(t_ea[:, 1, :], t_k[:, :], t_pp[:, 1:1 + S], ALU.subtract).then_inc(sig["t_a1"], 1)
                    pool.wait_ge(sig["t_qq"], m + 1)
                    pool.tensor_tensor(t_eb[:, 0, :], t_pp[:, 0:S], t_qq[:, :], ALU.subtract).then_inc(sig["t_b0"], 1)
                if slot == 9:
                    pool.wait_ge(sig["t_expa"], m + 1)
                    pool.tensor_tensor(t_ev[:, :], t_ea[:, 1, :], t_v[:, :], ALU.mult).then_inc(sig["t_ev"], 1)
                    pool.wait_ge(sig["t_expb"], m + 1)
                    pool.tensor_tensor(t_n2[:, :], t_eb[:, 1, :], t_v[:, :], ALU.mult).then_inc(sig["t_n2"], 1)

            def channel_step(m, slot):
                if slot == 10:
                    pool.wait_ge(sig["t_u2"], m + 1)
                    pool.wait_ge(sig["t_u"], m + 1)
                    pool.tensor_tensor(wide(chunk(m)), wide(chunk(m)), wide(t_u2[:, :, :]), ALU.add)\
                        .then_inc(sig["f_x"], 1)
                if slot == 3:
                    rsqrt(a_rs[:, :], a_ve[:, :], "f_ve", m + 1, "f_rstd")
                if slot == 6:
                    pool.wait_ge(sig["f_h"], m + 1)
                    pool.tensor_tensor(f_d[:, :], f_h[:, 1:1 + S], f_h[:, 0:S], ALU.subtract).then_inc(sig["f_d"], 1)

            def iteration(g=None, att=None, tmix=None, cmix=None, pro=None, lead=0):
                for slot in range(-lead, UNITS + 1):
                    if g is not None and slot < UNITS:
                        unit(g, slot)
                        before = unit_before(g, slot, 1)
                        if low_on_pool(*before):
                            split_low(pool, *before)
                    if att is not None and slot == 0:
                        rsqrt(a_rs[:, :], a_ve[:, :], "a_vedone", att + 1, "a_rstd")
                    if cmix is not None:
                        channel_step(cmix, slot)
                    if tmix is not None:
                        time_step(tmix, slot)
                    if pro is not None:
                        pro_step(pro, slot + lead)

            iteration(att=0)
            split_weights(slice(0, PAIRS), w1h, w1l, w_stage[:, 0:PAIRS, :], ("in_w1", 1))
            split_weights(slice(0, PAIRS), w3h, w3l, w_stage[:, PAIRS:2 * PAIRS, :], ("in_w3", 2))
            split_weights(slice(0, PAIRS), w2h, w2l, w2_stage, ("in_w2", 3))
            split_weights(slice(PAIRS, UNITS), w1h, w1l, mt[:, M_S1:M_S1 + 1, :], ("in_mt", 4))
            split_weights(slice(PAIRS, UNITS), w3h, w3l, mt[:, M_S3:M_S3 + 1, :], ("in_mt", 5))
            split_weights(slice(PAIRS, UNITS), w2h, w2l, mt[:, M_S2:M_S2 + 1, :], ("in_mt", 6))
            pool.wait_ge(sig["in_key"], 16)
            pool.wait_ge(sig["c_wh"], 7)
            pool.tensor_tensor(key_l[:, :], key_stage, key_h[:, :].bitcast(F32), ALU.subtract).then_inc(sig["c_wl"], 1)
            front(iteration)
            iteration(0, att=2, pro=1)
            with pool.Fori(1, B - 3) as g:
                iteration(g, att=g + 2, pro=g + 1)
            iteration(B - 3, att=B - 1, tmix=0, pro=B - 2)
            iteration(B - 2, tmix=1, cmix=0, pro=B - 1)
            iteration(B - 1, tmix=2, cmix=1, pro=B)
            iteration(B, tmix=3, cmix=2, pro=B + 1)
            with pool.Fori(B + 1, 2 * B - 3) as g:
                iteration(g, tmix=g - (B - 3), cmix=g - (B - 2), pro=g + 1)
            iteration(2 * B - 3, cmix=B - 1, pro=2 * B - 2)
            iteration(2 * B - 2, pro=2 * B - 1)
            iteration(2 * B - 1)
            if low_on_pool(2 * B - 1, UNITS - 1):
                split_low(pool, 2 * B - 1, UNITS - 1)

        @block.scalar
        def _(act):
            act.dma_start(am[:, :, :], att_mats).then_inc(sig["in_am"], 16)
            act.dma_start(vec[:, :], vecs).then_inc(sig["in_vec"], 16)
            act.wait_ge(sig["in_vec"], 16)
            act.activation(decay[:, :], vec[:, DECAY:DECAY + 1], ACT.Exp).then_inc(sig["c_dec0"], 1)
            act.wait_ge(sig["c_qkm_ps"], 1)
            act.activation(qk_m[:, :], pv[:, 0:D], ACT.Copy).then_inc(sig["c_qkm"], 1)

            def unit(g, p, late):
                k = UNITS * g + p
                act.wait_ge(sig["m_a"], k + 1)
                if not (isinstance(k, int) and k < 2):
                    act.wait_ge(sig["m_v"], done(k) if p == 0 else done(k - 1))
                if p not in TANH_UNITS[late]:
                    ins = act.activation(m_th[:, p % 2, :], pa[p % 2][:, :], ACT.Silu)
                else:
                    ins = act.activation(m_th[:, p % 2, :], pa[p % 2][:, :], ACT.Tanh, scale=0.5)
                ins.then_inc(sig["m_th"], 1)

            def att_step(n, slot):
                if slot == 4:
                    act.wait_ge(sig["a_tr"], n + 1)
                    act.activation(a_xT[:, 0:S], pu[:, :], ACT.Copy).then_inc(sig["a_xT"], 1)
                if slot == 7:
                    act.wait_ge(sig["a_gps"], n + 1)
                    act.activation(a_g[:, :], pv[:, :], ACT.Copy).then_inc(sig["a_g"], 1)
                    act.wait_ge(sig["a_vps"], n + 1)
                    act.activation(wide(a_v[:, :, :]), pu[:, :], ACT.Copy).then_inc(sig["a_v"], 1)
                if slot == 8:
                    att_exp(n, 0, (0, 1), (0, P))
                if slot == 10:
                    turn_probs(n, 0, 3)
                    att_exp(n, 1, (2,), (0,))
                if slot == 11:
                    turn_probs(n, 1, 3)
                if slot == 13:
                    att_exp(n, 2, (3,), (0,))
                if slot == 14:
                    turn_probs(n, 2, 4)

            def att_exp(n, i, tiles, at):
                act.wait_ge(sig["a_nm"], 3 * n + i + 1)
                wait(act, "a_pT", 3 * n + i)
                for t, o in zip(tiles, at):
                    ins = act.activation(a_p[:, o:o + P * (t + 1)], pv[:, o:o + P * (t + 1)], ACT.Exp,
                                         bias=a_nm[:, t:t + 1], scale=SCALE, accum_out=a_sum[:, t:t + 1])
                ins.then_inc(sig["a_exp"], 1)

            def turn_probs(n, i, blocks):
                act.wait_ge(sig["a_pT"], 3 * n + i + 1)
                act.activation(a_pT[:, 0:P * blocks], pu[:, 0:P * blocks], ACT.Copy).then_inc(sig["a_pTs"], 1)

            def pro_step(q, slot, cmix):
                if slot == 5:
                    vectors_loaded()
                    act.wait_ge(sig["r_nm"], q + 1)
                    normalise(r_xn, chunk(sequence(q)), r_rs, r_nm, "r_xn")
                if slot == 7:
                    act.wait_ge(sig["r_tr"], q + 1)
                    act.activation(r_xT[:, :], router_bank(cmix)[:, :], ACT.Copy).then_inc(sig["r_xT"], 1)
                    act.activation(m_xh[:, q % 2, :], router_bank(cmix)[:, :], ACT.Copy).then_inc(sig["m_xh"], 1)
                if slot == 9:
                    act.wait_ge(sig["r_lg"], q + 1)
                    act.activation(wide(r_ex[:, :, :]), wide(r_lg[:, :, :]), ACT.Exp).then_inc(sig["r_ex"], 1)
                if slot == 14:
                    act.wait_ge(sig["r_wTps"], q + 1)
                    wait(act, "w_out", 16 * q)
                    act.activation(r_wT[:, :], pq[0:E, :], ACT.Copy).then_inc(sig["r_wT"], 1)

            def time_step(m, slot):
                if slot == 3:
                    vectors_loaded()
                    act.wait_ge(sig["t_nm"], 2 * m + 2)
                    normalise(t_hn, chunk(m), t_rs[:, T:2 * T], t_nm[:, T:2 * T], "t_hn")
                if slot == 4:
                    vectors_loaded()
                    wait(act, "t_u2", m)
                    normalise(t_u, chunk(m), t_rs[:, 0:T], t_nm[:, 0:T], "t_u")
                    act.wait_ge(sig["t_tr"], m + 1)
                    act.activation(t_h[:, 1:1 + S], pq[:, :], ACT.Identity, bias=vec[:, LN1_B:LN1_B + 1],
                                   scale=vec[:, LN1_W:LN1_W + 1]).then_inc(sig["t_h"], 1)
                if slot == 8:
                    act.wait_ge(sig["t_kps"], m + 1)
                    act.activation(t_k[:, :], pq[:, :], ACT.Copy).then_inc(sig["t_k"], 1)
                if slot == 9:
                    act.wait_ge(sig["t_vps"], m + 1)
                    act.activation(t_v[:, :], pq[:, :], ACT.Copy).then_inc(sig["t_v"], 1)
                if slot == 11:
                    act.wait_ge(sig["t_rps"], m + 1)
                    act.activation(t_r[:, :], pq[:, :], ACT.Tanh, scale=0.5).then_inc(sig["t_r"], 1)
                if slot == 10:
                    act.wait_ge(sig["t_a0"], m + 1)
                    act.wait_ge(sig["t_a1"], m + 1)
                    act.activation(wide(t_ea[:, :, :]), wide(t_ea[:, :, :]), ACT.Exp).then_inc(sig["t_expa"], 1)
                    act.wait_ge(sig["t_b0"], m + 1)
                    act.wait_ge(sig["t_b1"], m + 1)
                    act.activation(wide(t_eb[:, :, :]), wide(t_eb[:, :, :]), ACT.Exp).then_inc(sig["t_expb"], 1)

            def channel_step(m, slot):
                if slot == 8:
                    act.wait_ge(sig["f_xk"], 2 * m + 1)
                    act.activation(f_xh[:, :], f_xk[:, :], ACT.Copy).then_inc(sig["f_xh"], 1)
                if slot == 6:
                    act.wait_ge(sig["f_nm"], m + 1)
                    normalise(f_hn, t_u2, a_rs, f_nm, "f_hn")
                if slot == 7:
                    act.wait_ge(sig["f_tr"], m + 1)
                    act.activation(f_h[:, 1:1 + S], pu[:, :], ACT.Identity, bias=vec[:, LN2_B:LN2_B + 1],
                                   scale=vec[:, LN2_W:LN2_W + 1]).then_inc(sig["f_h"], 1)
                if slot == 10:
                    relu_square(m, 0, pv)
                if slot == 11:
                    act.wait_ge(sig["f_rec"], m + 1)
                    act.activation(f_tr[:, :], pu[:, :], ACT.Tanh, scale=0.5).then_inc(sig["f_tr2"], 1)
                if slot == 12:
                    relu_square(m, 1, pv)
                if slot == 14:
                    relu_square(m, 2, pu)
                if slot == 15:
                    relu_square(m, 3, pv)

            def relu_square(m, j, ps):
                act.wait_ge(sig["f_key"], FB * m + j + 1)
                act.activation(f_kk[:, j, :], ps[:, :], ACT.Relu).then_inc(sig["f_rk"], 1)
                act.wait_ge(sig["f_rk"], FB * m + j + 1)
                act.activation(f_kk[:, j, :], f_kk[:, j, :], ACT.Square).then_inc(sig["f_kk"], 1)

            def vectors_loaded():
                act.wait_ge(sig["in_vec"], 16)

            def normalise(dst, src, rs, nm, signal):
                for t in range(T):
                    ins = act.activation(dst[:, t, :], src[:, t, :], ACT.Identity, bias=nm[:, t:t + 1],
                                         scale=rs[:, t:t + 1])
                ins.then_inc(sig[signal], 1)

            def split_high(g, p):
                if isinstance(g, int) and g < 0:
                    return
                k = UNITS * g + p
                if p < PAIRS:
                    wait_weighted(act, g, p)
                else:
                    act.wait_ge(sig["m_v"], done(k + 1))
                wait(act, "m_y", done(k + 1 - since_last_use(SPLIT_AT, p)))
                act.activation(m_hh[:, SPLIT_AT[p], :], m_h[:, HIDDEN_AT[p], :], ACT.Copy).then_inc(sig["m_hh"], 1)

            def out_copy(g):
                if g is None or (isinstance(g, int) and g == 0):
                    return
                act.wait_ge(sig["m_y"], done(UNITS * g))
                act.activation(m_y[:, :], py[:, :], ACT.Copy).then_inc(sig["m_ys"], 1)

            def iteration(g=None, att=None, tmix=None, cmix=None, pro=None, late=False, lead=0):
                for slot in range(-lead, UNITS + 1):
                    if g is not None and slot < UNITS:
                        unit(g, slot, late)
                        split_high(*unit_before(g, slot, SPLIT_LAG))
                    if slot == 3:
                        out_copy(g)
                    if att is not None:
                        att_step(att, slot)
                    if cmix is not None:
                        channel_step(cmix, slot)
                    if pro is not None:
                        pro_step(pro, slot + lead, cmix)
                    if tmix is not None:
                        time_step(tmix, slot)

            iteration(att=0)
            front(iteration)
            iteration(0, att=2, pro=1)
            with act.Fori(1, B - 3) as g:
                iteration(g, att=g + 2, pro=g + 1)
            iteration(B - 3, att=B - 1, tmix=0, pro=B - 2)
            iteration(B - 2, tmix=1, cmix=0, pro=B - 1, late=True)
            iteration(B - 1, tmix=2, cmix=1, pro=B, late=True)
            iteration(B, tmix=3, cmix=2, pro=B + 1, late=True)
            with act.Fori(B + 1, 2 * B - 3) as g:
                iteration(g, tmix=g - (B - 3), cmix=g - (B - 2), pro=g + 1, late=True)
            iteration(2 * B - 3, cmix=B - 1, pro=2 * B - 2, late=True)
            iteration(2 * B - 2, pro=2 * B - 1, late=True)
            iteration(2 * B - 1, late=True)
            for p in range(UNITS - SPLIT_LAG, UNITS):
                split_high(2 * B - 1, p)
            out_copy(2 * B)

        @block.tensor
        def _(pe):
            pe.wait_ge(sig["c_pool"], 10)
            pe.wait_ge(sig["in_am"], 16)
            pe.matmul(pv[:, 0:D], am[:, 0, :], am[:, 1, :], start=True, stop=True).then_inc(sig["c_qkm_ps"], 1)

            def turn(ps, src, signal):
                for t in range(T):
                    ins = pe.transpose(ps[:, P * t:P * (t + 1)], src[:, t, :], ident[:, :])
                ins.then_inc(sig[signal], 1)

            def unit(g, p):
                k = UNITS * g + p
                if p == 0:
                    pe.wait_ge(sig["m_xl"], g + 1)
                    pe.wait_ge(sig["m_xh"], g + 1)
                lag = 1 if p == 0 else 2
                before = unit_before(g, p, lag)
                if by_tanh(*before):
                    wait(pe, "m_v", done(k + 1 - lag))
                else:
                    wait(pe, "m_th", k + 1 - lag)
                up(pa[p % 2], w1h, w1l, g, p).then_inc(sig["m_a"], 1)
                wait(pe, "m_v", done(k + 1 - lag))
                up(pb[p % 2], w3h, w3l, g, p).then_inc(sig["m_b"], 1)

            def up(ps, high, low, g, p):
                xh, xl = m_xh[:, g % 2, :], m_xl[:, g % 2, :]
                pe.matmul(ps[:, :], high[:, p, :], xh, start=True, stop=False)
                pe.matmul(ps[:, :], high[:, p, :], xl, start=False, stop=False)
                return pe.matmul(ps[:, :], low[:, p, :], xh, start=False, stop=True)

            def out_product(g, p):
                k = UNITS * g + p
                if p == 0:
                    wait(pe, "m_ys", g)
                pe.wait_ge(sig["m_hh"], k + 1)
                wait_split(pe, g, p)
                hh, hl = m_hh[:, SPLIT_AT[p], :], m_hl[:, SPLIT_AT[p], :]
                pe.matmul(py[:, :], w2h[:, p, :], hh, start=(p == 0), stop=False)
                pe.matmul(py[:, :], w2l[:, p, :], hh, start=False, stop=False)
                pe.matmul(py[:, :], w2h[:, p, :], hl, start=False, stop=(p == UNITS - 1)).then_inc(sig["m_y"], 1)

            def out_step(g, slot):
                if slot >= LAG:
                    out_product(g, slot - LAG)
                elif not (isinstance(g, int) and g == 0):
                    out_product(g - 1, UNITS - LAG + slot)

            def out_turn(g, ps, q=None):
                if g is None or (isinstance(g, int) and g == 0):
                    return
                pe.wait_ge(sig["m_ys"], g)
                if q is not None:
                    pe.wait_ge(sig["r_wT"], q)
                for t in range(T):
                    ins = pe.transpose(ps[:, P * t:P * (t + 1)], m_y[:, P * t:P * (t + 1)], ident[:, :])
                ins.then_inc(sig["m_yT"], 1)

            def att_step(n, slot, n_chunk, n_chunk_in_pv):
                if slot == 3:
                    pe.wait_ge(sig["a_xn"], n + 1)
                    turn(pu, a_xn, "a_tr")
                if slot == 6:
                    pe.wait_ge(sig["c_qkm"], 1)
                    pe.wait_ge(sig["a_xT"], n + 1)
                    if n_chunk is not None and n_chunk_in_pv:
                        pe.wait_ge(sig["m_x"], done(n_chunk))
                    pe.matmul(pv[:, :], qk_m[:, :], a_xT[:, 0:S], start=True, stop=True).then_inc(sig["a_gps"], 1)
                    for t in range(T):
                        ins = pe.matmul(pu[:, P * t:P * (t + 1)], a_xT[:, P * t:P * (t + 1)], am[:, 2, :],
                                        start=True, stop=True)
                    ins.then_inc(sig["a_vps"], 1)
                if slot == 8:
                    pe.wait_ge(sig["a_g"], n + 1)
                    scores(n, (0, 1), (0, P))
                if slot == 10:
                    pe.wait_ge(sig["a_v"], n + 1)
                    probs(n, 0, 3)
                    scores(n, (2,), (0,))
                    values(n, 0, (0, 1), (0, P))
                if slot == 11:
                    probs(n, 1, 3)
                if slot == 12:
                    scores(n, (3,), (0,))
                if slot == 13:
                    values(n, 1, (2,), (0,))
                if slot == 14:
                    probs(n, 2, 4)
                if slot == 16:
                    values(n, 2, (3,), (0,))

            def scores(n, tiles, at):
                for t, o in zip(tiles, at):
                    q = slice(P * t, P * (t + 1))
                    pe.matmul(pv[:, o:o + P * (t + 1)], a_g[:, q], a_xT[:, 0:P * (t + 1)], start=True, stop=False)
                    ins = pe.matmul(pv[:, o + P * t:o + P * (t + 1)], ident_b[:, :], causal_b[:, :],
                                    start=False, stop=True)
                ins.then_inc(sig["a_s"], 1)

            def probs(n, i, blocks):
                pe.wait_ge(sig["a_exp"], 3 * n + i + 1)
                wait(pe, "a_add", 3 * n + i)
                for j in range(blocks):
                    ins = pe.transpose(pu[:, P * j:P * (j + 1)], a_p[:, P * j:P * (j + 1)], ident[:, :])
                ins.then_inc(sig["a_pT"], 1)

            def values(n, i, tiles, at):
                pe.wait_ge(sig["a_pTs"], 3 * n + i + 1)
                for t, o in zip(tiles, at):
                    for j in range(t + 1):
                        ins = pe.matmul(pu[:, P * t:P * (t + 1)], a_pT[:, o + P * j:o + P * (j + 1)], a_v[:, j, :],
                                        start=(j == 0), stop=(j == t))
                ins.then_inc(sig["a_o"], 1)

            def pro_step(q, slot, tmix, cmix):
                ps = router_bank(cmix)
                if slot == 6:
                    pe.wait_ge(sig["r_xn"], q + 1)
                    if cmix is not None:
                        pe.wait_ge(sig["m_x"], done(q - 1))
                    elif tmix is not None:
                        pe.wait_ge(sig["t_h"], tmix + 1)
                    elif not (isinstance(q, int) and q < 2):
                        pe.wait_ge(sig["m_x"], done(q - 1))
                    else:
                        wait(pe, "r_wT", q)
                    turn(ps, r_xn, "r_tr")
                if slot == 8:
                    pe.wait_ge(sig["m_xh"], q + 1)
                    for t in range(T):
                        ins = pe.matmul(ps[:, E * t:E * (t + 1)], r_xT[:, P * t:P * (t + 1)], wg[:, :],
                                        start=True, stop=True)
                    ins.then_inc(sig["r_lgps"], 1)
                if slot == 13:
                    pe.wait_ge(sig["r_sel"], q + 1)
                    if tmix is not None:
                        pe.wait_ge(sig["t_r"], tmix + 1)
                    for t in range(T):
                        later = T - t
                        pe.matmul(pq[:, E * (t + 1):E * (T + 1)].rearrange("p (a e) -> p a e", a=later),
                                  ones_b[:, :], r_sel[:, t:t + 1, :].broadcast_to([P, later, E]),
                                  start=(t == 0), stop=False, skip_group_check=True)
                        ins = pe.matmul(pq[:, E * t:E * (t + 1)], tri_b[:, :], r_sel[:, t, :],
                                        start=False, stop=(t == T - 1), skip_group_check=True)
                    ins.then_inc(sig["r_cnt"], 1)
                if slot == 14:
                    pe.wait_ge(sig["r_w"], q + 1)
                    pe.wait_ge(sig["r_carry"], q + 1)
                    for t in range(T):
                        ins = pe.transpose(pq[0:E, P * t:P * (t + 1)], r_w[:, t, :], ident[:, :])
                    ins.then_inc(sig["r_wTps"], 1)

            def time_step(m, slot, q, cmix):
                if slot == 4:
                    pe.wait_ge(sig["t_hn"], m + 1)
                    pe.wait_ge(sig["r_wT"], q)
                    wait(pe, "t_u2", m)
                    turn(pq, t_hn, "t_tr")
                if slot == 8:
                    pe.wait_ge(sig["t_xk"], 3 * m + 3)
                    if cmix is None:
                        pe.wait_ge(sig["r_lg"], q + 1)
                    pe.matmul(pq[:, :], mt[:, M_K, :], t_xk[:, :], start=True, stop=True).then_inc(sig["t_kps"], 1)
                if slot == 9:
                    pe.wait_ge(sig["t_k"], m + 1)
                    pe.matmul(pq[:, :], mt[:, M_V, :], t_xv[:, :], start=True, stop=True).then_inc(sig["t_vps"], 1)
                if slot == 10:
                    pe.wait_ge(sig["t_v"], m + 1)
                    pe.matmul(pq[:, :], mt[:, M_R, :], t_xr[:, :], start=True, stop=True).then_inc(sig["t_rps"], 1)
            def channel_step(m, slot, q):
                if slot == 3:
                    pe.wait_ge(sig["t_rw"], m + 1)
                    pe.wait_ge(sig["r_wT"], q)
                    for t in range(T):
                        ins = pe.matmul(pq[:, P * t:P * (t + 1)], t_n1[:, P * t:P * (t + 1)], mt[:, M_O, :],
                                        start=True, stop=True)
                    ins.then_inc(sig["t_ops"], 1)
                if slot == 7:
                    pe.wait_ge(sig["f_hn"], m + 1)
                    turn(pu, f_hn, "f_tr")
                if slot == 10:
                    pe.wait_ge(sig["f_xh"], m + 1)
                    pe.wait_ge(sig["f_xl"], m + 1)
                    key(m, 0, pv)
                if slot == 11:
                    pe.wait_ge(sig["f_xk"], 2 * m + 2)
                    for t in range(T):
                        ins = pe.matmul(pu[:, P * t:P * (t + 1)], f_xr[:, P * t:P * (t + 1)], mt[:, M_REC, :],
                                        start=True, stop=True)
                    ins.then_inc(sig["f_rec"], 1)
                    pe.wait_ge(sig["f_rk"], FB * m + 1)
                    key(m, 1, pv)
                if slot == 12:
                    pe.wait_ge(sig["f_tr2"], m + 1)
                    key(m, 2, pu)
                if slot == 13:
                    pe.wait_ge(sig["f_rk"], FB * m + 2)
                    key(m, 3, pv)
                if slot == 16:
                    pe.wait_ge(sig["f_kk"], FB * m + FB)
                    for t in range(T):
                        for j in range(FB):
                            ins = pe.matmul(pu[:, P * t:P * (t + 1)], f_kk[:, j, P * t:P * (t + 1)],
                                            mt[:, M_VAL + j, :], start=(j == 0), stop=(j == FB - 1))
                    ins.then_inc(sig["f_kv"], 1)

            def key(m, j, ps):
                block = slice(P * j, P * (j + 1))
                pe.matmul(ps[:, :], key_h[:, block], f_xh[:, :], start=True, stop=False)
                pe.matmul(ps[:, :], key_l[:, block], f_xh[:, :], start=False, stop=False)
                pe.matmul(ps[:, :], key_h[:, block], f_xl[:, :], start=False, stop=True).then_inc(sig["f_key"], 1)

            def iteration(g=None, att=None, tmix=None, cmix=None, pro=None, lead=0):
                for slot in range(-lead, UNITS):
                    if g is not None:
                        unit(g, slot)
                        out_step(g, slot)
                        if slot == 4:
                            out_turn(g, out_bank(tmix, cmix), pro)
                    if att is not None:
                        att_step(att, slot, g, tmix is not None)
                    if cmix is not None:
                        channel_step(cmix, slot, cmix + B - 1)
                    if pro is not None:
                        pro_step(pro, slot + lead, tmix, cmix)
                    if tmix is not None:
                        time_step(tmix, slot, pro, cmix)

            iteration(att=0)
            pe.wait_ge(sig["in_wg"], 16)
            front(iteration)
            pe.wait_ge(sig["in_mt"], 16)
            pe.wait_ge(sig["c_wl"], 7)
            pe.wait_ge(sig["c_wh"], 7)
            iteration(0, att=2, pro=1)
            with pe.Fori(1, B - 3) as g:
                iteration(g, att=g + 2, pro=g + 1)
            iteration(B - 3, att=B - 1, tmix=0, pro=B - 2)
            iteration(B - 2, tmix=1, cmix=0, pro=B - 1)
            iteration(B - 1, tmix=2, cmix=1, pro=B)
            iteration(B, tmix=3, cmix=2, pro=B + 1)
            with pe.Fori(B + 1, 2 * B - 3) as g:
                iteration(g, tmix=g - (B - 3), cmix=g - (B - 2), pro=g + 1)
            iteration(2 * B - 3, cmix=B - 1, pro=2 * B - 2)
            iteration(2 * B - 2, pro=2 * B - 1)
            iteration(2 * B - 1)
            for p in range(UNITS - LAG, UNITS):
                out_product(2 * B - 1, p)
            out_turn(2 * B, pq)

        @block.vector
        def _(dve):
            for ap, value in ((r_p[:, :, E:E + TOP_K], -1.0), (r_carry[:, :], 0.0), (t_h[:, 0:1], 0.0),
                              (t_pp[:, 0:1], NEVER), (t_aa[:, 0:1], 0.0), (t_bb[:, 0:1], 0.0)):
                dve.memset(ap, value).then_inc(sig["c_dve"], 1)
            dve.wait_ge(sig["c_dve"], 6)

            def constants_set():
                dve.wait_ge(sig["c_dve"], 6)

            def row_stats(src, st, mv, n, s_st, s_mv):
                for t in range(T):
                    ins = dve.bn_stats(st[:, t, :], src[:, t, :])
                ins.then_inc(sig[s_st], 1)
                dve.wait_ge(sig[s_st], n + 1)
                dve.sem_inc(sig["stats_seen"], 1)
                for t in range(T):
                    ins = dve.bn_aggr(mv[:, t, :], st[:, t, :])
                ins.then_inc(sig[s_mv], 1)
                dve.wait_ge(sig[s_mv], n + 1)

            def shifts(dst, mv, rs, signal):
                dve.scalar_tensor_tensor(out=dst, in0=mv[:, :, 0], scalar=-1.0, in1=rs, op0=ALU.mult,
                                         op1=ALU.mult).then_inc(sig[signal], 1)

            def normalise(dst, src, mv, rs, signal):
                for t in range(T):
                    ins = dve.tensor_scalar(dst[:, t, :], src[:, t, :], mv[:, t, 0:1], rs[:, t:t + 1],
                                            ALU.subtract, ALU.mult)
                ins.then_inc(sig[signal], 1)

            def unit(g, p, late):
                def wait_place():
                    if p < PAIRS:
                        wait_weighted(dve, *((g, p - 2) if p >= 2 else (g - 1, PAIRS - 2 + p)))
                    else:
                        wait_split(dve, g - 1, p)

                def low():
                    before = unit_before(g, p, SPLIT_LAG)
                    if not low_on_pool(*before):
                        split_low(dve, *before)

                k = UNITS * g + p
                r = p % 2
                dve.wait_ge(sig["m_th"], k + 1)
                if p not in TANH_UNITS[late]:
                    low()
                    dve.wait_ge(sig["m_b"], k + 1)
                    wait_place()
                    dve.tensor_tensor(gated(p), m_th[:, r, :], pb[r][:, :], ALU.mult).then_inc(sig["m_v"], 1)
                    return
                tanh = TANH_UNITS[late]
                through, before = ("m_u_late", LATE) if late else ("m_u", 0)
                count = len(tanh) * (g - before) + tanh.index(p) + 1
                dve.scalar_tensor_tensor(out=m_th[:, r, :], in0=m_th[:, r, :], scalar=1.0, in1=pa[r][:, :],
                                         op0=ALU.add, op1=ALU.mult).then_inc(sig[through], 1)
                low()
                dve.wait_ge(sig["m_b"], k + 1)
                dve.wait_ge(sig[through], count)
                wait_place()
                dve.scalar_tensor_tensor(out=gated(p), in0=m_th[:, r, :], scalar=0.5, in1=pb[r][:, :],
                                         op0=ALU.mult, op1=ALU.mult).then_inc(sig["m_v"], 1)

            def add_out(g, ps):
                if g is None or (isinstance(g, int) and g == 0):
                    return
                c = sequence_before(g)
                dve.wait_ge(sig["m_yT"], g)
                dve.tensor_tensor(wide(chunk(c)), wide(chunk(c)), ps[:, :], ALU.add).then_inc(sig["m_x"], 1)

            def att_step(n, slot):
                if slot == 0:
                    if isinstance(n, int):
                        dve.wait_ge(sig["in_x0" if n == 0 else "in_x1"], 16)
                    row_stats(chunk(n), a_st, a_mv, n, "a_stats", "a_mvs")
                    dve.tensor_scalar(a_ve[:, 0:T], a_mv[:, :, 1], EPS, None, ALU.add).then_inc(sig["a_vedone"], 1)
                if slot == 1:
                    dve.wait_ge(sig["a_rstd"], n + 1)
                    normalise(a_xn, chunk(n), a_mv, a_rs, "a_xn")
                if isinstance(n, int) and n == 0:
                    if slot == 4:
                        high_part(0, "in_w1", 0)
                    if slot == 8:
                        high_part(1, "in_w3", 0)
                    if slot == 12:
                        high_part(2, "in_w2", 0)
                    if slot == 12:
                        for i in range(3):
                            high_part(i, "in_mt", 1)
                        dve.wait_ge(sig["in_key"], 16)
                        dve.tensor_copy(key_h[:, :], key_stage).then_inc(sig["c_wh"], 1)
                if slot == 8:
                    row_max(n, 0, (0, 1), (0, P))
                if slot == 10:
                    row_max(n, 1, (2,), (0,))
                    add_att(n, 0, (0, 1))
                if slot == 12:
                    row_max(n, 2, (3,), (0,))
                    add_att(n, 1, (2,))
                if slot == 17:
                    add_att(n, 2, (3,))

            def high_part(i, loaded, shared):
                high = (w1h, w3h, w2h)[i]
                dve.wait_ge(sig[loaded], 16)
                if shared:
                    m = (M_S1, M_S3, M_S2)[i]
                    dve.tensor_copy(high[:, PAIRS, :], mt[:, m, :]).then_inc(sig["c_wh"], 1)
                else:
                    src = (w_stage[:, 0:PAIRS, :], w_stage[:, PAIRS:2 * PAIRS, :], w2_stage)[i]
                    dve.tensor_copy(high[:, 0:PAIRS, :], src).then_inc(sig["c_wh"], 1)

            def row_max(n, i, tiles, at):
                dve.wait_ge(sig["a_s"], 3 * n + i + 1)
                for t, o in zip(tiles, at):
                    ins = dve.tensor_reduce(a_mx[:, t:t + 1], pv[:, o:o + P * (t + 1)], AX_X, ALU.max)
                ins.then_inc(sig["a_mx"], 1)
                dve.wait_ge(sig["a_mx"], 3 * n + i + 1)
                a, b = tiles[0], tiles[-1] + 1
                dve.tensor_scalar(a_nm[:, a:b], a_mx[:, a:b], -SCALE, None, ALU.mult).then_inc(sig["a_nm"], 1)

            def add_att(n, i, tiles):
                a, b = tiles[0], tiles[-1] + 1
                dve.wait_ge(sig["a_exp"], 3 * n + i + 1)
                dve.reciprocal(a_ri[:, a:b], a_sum[:, a:b]).then_inc(sig["a_ri"], 1)
                dve.wait_ge(sig["a_ri"], 3 * n + i + 1)
                dve.wait_ge(sig["a_o"], 3 * n + i + 1)
                for t in tiles:
                    ins = dve.scalar_tensor_tensor(out=chunk(n)[:, t, :], in0=pu[:, P * t:P * (t + 1)],
                                                   scalar=a_ri[:, t:t + 1], in1=chunk(n)[:, t, :],
                                                   op0=ALU.mult, op1=ALU.add)
                ins.then_inc(sig["a_add"], 1)

            def pro_step(q, slot, cmix):
                if slot == 2:
                    if layer_of(q) == 0:
                        dve.wait_ge(sig["a_add"], 3 * q + 3)
                    else:
                        dve.wait_ge(sig["f_x"], 2 * (q - B) + 2)
                    row_stats(chunk(sequence(q)), r_st, r_mv, q, "r_stats", "r_mvs")
                    dve.tensor_scalar(r_ve[:, :], r_mv[:, :, 1], EPS, None, ALU.add).then_inc(sig["r_vedone"], 1)
                if slot == 4:
                    dve.wait_ge(sig["r_rstd"], q + 1)
                    shifts(r_nm[:, :], r_mv, r_rs[:, :], "r_nm")
                if slot == 8:
                    dve.wait_ge(sig["r_lgps"], q + 1)
                    lg = router_bank(cmix)[:, 0:T * E].rearrange("p (t e) -> p t e", t=T)
                    dve.tensor_reduce(r_mx[:, :], lg, AX_X, ALU.max).then_inc(sig["r_mx"], 1)
                    dve.wait_ge(sig["r_mx"], q + 1)
                    dve.tensor_tensor(r_lg[:, :, :], lg, r_mx[:, :].unsqueeze(2).broadcast_to([P, T, E]),
                                      ALU.subtract).then_inc(sig["r_lg"], 1)
                if slot == 9:
                    dve.wait_ge(sig["r_ex"], q + 1)
                    dve.tensor_reduce(r_sum[:, :], r_ex[:, :, :], AX_X, ALU.add).then_inc(sig["r_sum"], 1)
                    dve.wait_ge(sig["r_sum"], q + 1)
                    dve.reciprocal(r_ri[:, :], r_sum[:, :]).then_inc(sig["r_ri"], 1)
                    dve.wait_ge(sig["r_ri"], q + 1)
                    dve.scalar_tensor_tensor(out=r_p[:, :, 0:E], in0=r_ex[:, :, :], scalar=1.0,
                                             in1=r_ri[:, :].unsqueeze(2).broadcast_to([P, T, E]),
                                             op0=ALU.mult, op1=ALU.mult).then_inc(sig["r_p"], 1)
                if slot == 10:
                    constants_set()
                    dve.wait_ge(sig["r_p"], q + 1)
                    for t in range(T):
                        ins = dve.max(r_top[:, t, :], r_p[:, t, :])
                    ins.then_inc(sig["r_top"], 1)
                    dve.wait_ge(sig["r_top"], q + 1)
                    dve.memset(r_top[:, :, TOP_K:8], -1.0).then_inc(sig["r_pad"], 1)
                    constants_set()
                    dve.wait_ge(sig["r_pad"], q + 1)
                    for t in range(T):
                        ins = dve.match_replace(r_rep[:, t, :], r_top[:, t, :], r_p[:, t, :], -2.0)
                    ins.then_inc(sig["r_rep"], 1)
                    dve.wait_ge(sig["r_rep"], q + 1)
                    dve.tensor_scalar(r_sel[:, :, :], r_rep[:, :, 0:E], 0.0, None, ALU.is_lt).then_inc(sig["r_sel"], 1)
                    dve.wait_ge(sig["r_sel"], q + 1)
                    dve.tensor_tensor(r_ws[:, :, :], r_sel[:, :, :], r_p[:, :, 0:E], ALU.mult).then_inc(sig["r_ws"], 1)
                if slot == 12:
                    dve.wait_ge(sig["r_cnt"], q + 1)
                    wait(dve, "r_carry", q)
                    dve.tensor_tensor(r_pos[:, :, :], pq[:, 0:T * E].rearrange("p (t e) -> p t e", t=T),
                                      r_carry[:, :].unsqueeze(1).broadcast_to([P, T, E]), ALU.add).then_inc(sig["r_pos"], 1)
                    dve.wait_ge(sig["r_pos"], q + 1)
                    dve.wait_ge(sig["r_ws"], q + 1)
                    dve.scalar_tensor_tensor(out=wide(r_w[:, :, :]), in0=wide(r_pos[:, :, :]), scalar=float(CAPACITY),
                                             in1=wide(r_ws[:, :, :]), op0=ALU.is_le, op1=ALU.mult).then_inc(sig["r_w"], 1)
                    if isinstance(q, int) and q == B - 1:
                        dve.memset(r_carry[:, :], 0.0).then_inc(sig["r_carry"], 1)
                    else:
                        dve.tensor_tensor(r_carry[:, :], pq[:, T * E:(T + 1) * E], r_carry[:, :],
                                          ALU.add).then_inc(sig["r_carry"], 1)

            def time_step(m, slot):
                if slot == 0:
                    dve.wait_ge(sig["m_x"], done(m + 1))
                    row_stats(chunk(m), t_st, t_mv, m, "t_stats", "t_mvs")
                    dve.tensor_scalar(t_ve[:, 0:T], t_mv[:, :, 1], EPS, None, ALU.add).then_inc(sig["t_ve"], 1)
                    dve.tensor_scalar(t_ve[:, T:2 * T], t_mv[:, :, 1], 1.0 + EPS, EPS * EPS, ALU.mult,
                                      ALU.add).then_inc(sig["t_ve"], 1)
                if slot == 2:
                    dve.wait_ge(sig["t_rstd"], m + 1)
                    shifts(t_nm[:, T:2 * T], t_mv, t_rs[:, T:2 * T], "t_nm")
                    shifts(t_nm[:, 0:T], t_mv, t_rs[:, 0:T], "t_nm")
                if slot == 6:
                    dve.wait_ge(sig["t_d"], m + 1)
                    for dst, c in ((t_xk, MIX_K), (t_xv, MIX_V), (t_xr, MIX_R)):
                        dve.scalar_tensor_tensor(out=dst[:, :], in0=t_d[:, :], scalar=vec[:, c:c + 1], in1=t_h[:, 0:S],
                                                 op0=ALU.mult, op1=ALU.add).then_inc(sig["t_xk"], 1)
                if slot == 9:
                    dve.wait_ge(sig["t_k"], m + 1)
                    dve.tensor_tensor_scan(out=t_pp[:, 1:1 + S], data0=decay[:, 0:1].to_broadcast([P, S]),
                                           data1=t_k[:, :], initial=NEVER, op0=ALU.add, op1=ALU.max)\
                       .then_inc(sig["t_pp"], 1)
                    dve.wait_ge(sig["t_pp"], m + 1)
                    dve.scalar_tensor_tensor(out=t_qq[:, :], in0=t_k[:, :], scalar=vec[:, FIRST:FIRST + 1],
                                             in1=t_pp[:, 0:S], op0=ALU.add, op1=ALU.max).then_inc(sig["t_qq"], 1)
                    dve.scalar_tensor_tensor(out=t_ea[:, 0, :], in0=t_pp[:, 0:S], scalar=decay[:, 0:1],
                                             in1=t_pp[:, 1:1 + S], op0=ALU.add, op1=ALU.subtract).then_inc(sig["t_a0"], 1)
                    dve.wait_ge(sig["t_qq"], m + 1)
                    dve.scalar_tensor_tensor(out=t_eb[:, 1, :], in0=t_k[:, :], scalar=vec[:, FIRST:FIRST + 1],
                                             in1=t_qq[:, :], op0=ALU.add, op1=ALU.subtract).then_inc(sig["t_b1"], 1)
                if slot == 11:
                    dve.wait_ge(sig["t_ev"], m + 1)
                    dve.tensor_tensor_scan(out=t_aa[:, 1:1 + S], data0=t_ea[:, 0, :], data1=t_ev[:, :], initial=0.0,
                                           op0=ALU.mult, op1=ALU.add).then_inc(sig["t_aa"], 1)
                    dve.tensor_tensor_scan(out=t_bb[:, 1:1 + S], data0=t_ea[:, 0, :], data1=t_ea[:, 1, :], initial=0.0,
                                           op0=ALU.mult, op1=ALU.add).then_inc(sig["t_bb"], 1)
                    dve.wait_ge(sig["t_expb"], m + 1)
                    dve.wait_ge(sig["t_aa"], m + 1)
                    dve.tensor_tensor(t_n1[:, :], t_eb[:, 0, :], t_aa[:, 0:S], ALU.mult).then_inc(sig["t_n1"], 1)
                    dve.wait_ge(sig["t_bb"], m + 1)
                    dve.tensor_tensor(t_d1[:, :], t_eb[:, 0, :], t_bb[:, 0:S], ALU.mult).then_inc(sig["t_d1"], 1)
                if slot == 12:
                    dve.wait_ge(sig["t_d1"], m + 1)
                    dve.tensor_tensor(t_d1[:, :], t_d1[:, :], t_eb[:, 1, :], ALU.add).then_inc(sig["t_den"], 1)
                    dve.wait_ge(sig["t_n2"], m + 1)
                    dve.wait_ge(sig["t_n1"], m + 1)
                    dve.tensor_tensor(t_n1[:, :], t_n1[:, :], t_n2[:, :], ALU.add).then_inc(sig["t_num"], 1)
                if slot == 14:
                    dve.wait_ge(sig["t_den"], m + 1)
                    invert(0)
                if slot == 15:
                    invert(1)
                if slot == 14:
                    invert(2)
                    invert(3)
                if slot == 16:
                    dve.wait_ge(sig["t_ri"], T * m + T)
                    dve.wait_ge(sig["t_num"], m + 1)
                    dve.tensor_tensor(t_ri[:, :], t_n1[:, :], t_ri[:, :], ALU.mult).then_inc(sig["t_y"], 1)
                if slot == 17:
                    dve.wait_ge(sig["t_y"], m + 1)
                    dve.wait_ge(sig["t_r"], m + 1)
                    dve.scalar_tensor_tensor(out=t_n1[:, :], in0=t_r[:, :], scalar=1.0, in1=t_ri[:, :],
                                             op0=ALU.add, op1=ALU.mult).then_inc(sig["t_rw"], 1)
            def channel_step(m, slot):
                if slot == 8:
                    dve.wait_ge(sig["f_xh"], m + 1)
                    dve.tensor_tensor(f_xl[:, :], f_xk[:, :], f_xh[:, :].bitcast(F32), ALU.subtract).then_inc(sig["f_xl"], 1)
                if slot == 2:
                    if isinstance(m, int) and m == 0:
                        dve.wait_ge(sig["a_add"], 3 * B)
                        dve.memset(f_h[:, 0:1], 0.0).then_inc(sig["f_zero"], 1)
                    dve.wait_ge(sig["t_ops"], m + 1)
                    dve.wait_ge(sig["t_u"], m + 1)
                    dve.scalar_tensor_tensor(out=wide(t_u2[:, :, :]), in0=pq[:, :], scalar=0.5,
                                             in1=wide(t_u[:, :, :]), op0=ALU.mult, op1=ALU.add).then_inc(sig["t_u2"], 1)
                if slot == 3:
                    dve.wait_ge(sig["t_u2"], m + 1)
                    row_stats(t_u2, a_st, a_mv, m, "f_stats", "f_mvs")
                    dve.tensor_scalar(a_ve[:, 0:T], a_mv[:, :, 1], EPS, None, ALU.add).then_inc(sig["f_ve"], 1)
                if slot == 4:
                    dve.wait_ge(sig["f_rstd"], m + 1)
                    shifts(f_nm[:, :], a_mv, a_rs[:, 0:T], "f_nm")
                if slot == 7:
                    dve.wait_ge(sig["f_d"], m + 1)
                    for dst, c in ((f_xk, FMIX_K), (f_xr, FMIX_R)):
                        dve.scalar_tensor_tensor(out=dst[:, :], in0=f_d[:, :], scalar=vec[:, c:c + 1], in1=f_h[:, 0:S],
                                                 op0=ALU.mult, op1=ALU.add).then_inc(sig["f_xk"], 1)
                if slot == 17:
                    dve.wait_ge(sig["f_tr2"], m + 1)
                    dve.wait_ge(sig["f_kv"], m + 1)
                    dve.scalar_tensor_tensor(out=f_g, in0=f_tr[:, :], scalar=1.0, in1=pu[:, :],
                                             op0=ALU.add, op1=ALU.mult).then_inc(sig["f_g"], 1)
                    dve.wait_ge(sig["f_g"], m + 1)
                    dve.wait_ge(sig["f_x"], 2 * m + 1)
                    dve.scalar_tensor_tensor(out=wide(chunk(m)), in0=f_g, scalar=0.5, in1=wide(chunk(m)),
                                             op0=ALU.mult, op1=ALU.add).then_inc(sig["f_x"], 1)

            def invert(i):
                part = slice(P * i, P * (i + 1))
                dve.reciprocal(t_ri[:, part], t_d1[:, part]).then_inc(sig["t_ri"], 1)

            def iteration(g=None, att=None, tmix=None, cmix=None, pro=None, late=False, lead=0):
                for slot in range(-lead, UNITS + 1):
                    if g is not None and slot < UNITS:
                        unit(g, slot, late)
                    if slot == 4:
                        add_out(g, out_bank(tmix, cmix))
                    if att is not None:
                        att_step(att, slot)
                    if tmix is not None:
                        time_step(tmix, slot)
                    if pro is not None:
                        pro_step(pro, slot + lead, cmix)
                    if cmix is not None:
                        channel_step(cmix, slot)

            iteration(att=0)
            dve.wait_ge(sig["c_dec0"], 1)
            dve.tensor_scalar(decay[:, :], decay[:, :], -1.0, None, ALU.mult).then_inc(sig["c_dec"], 1)
            front(iteration)
            dve.wait_ge(sig["in_xr"], 16 * (B - 2))
            iteration(0, att=2, pro=1)
            with dve.Fori(1, B - 3) as g:
                iteration(g, att=g + 2, pro=g + 1)
            dve.wait_ge(sig["in_vec"], 16)
            dve.wait_ge(sig["c_dec"], 1)
            iteration(B - 3, att=B - 1, tmix=0, pro=B - 2)
            iteration(B - 2, tmix=1, cmix=0, pro=B - 1, late=True)
            iteration(B - 1, tmix=2, cmix=1, pro=B, late=True)
            iteration(B, tmix=3, cmix=2, pro=B + 1, late=True)
            with dve.Fori(B + 1, 2 * B - 3) as g:
                iteration(g, tmix=g - (B - 3), cmix=g - (B - 2), pro=g + 1, late=True)
            iteration(2 * B - 3, cmix=B - 1, pro=2 * B - 2, late=True)
            iteration(2 * B - 2, pro=2 * B - 1, late=True)
            iteration(2 * B - 1, late=True)
            for p in range(UNITS - SPLIT_LAG, UNITS):
                if not low_on_pool(2 * B - 1, p):
                    split_low(dve, 2 * B - 1, p)
            add_out(2 * B, pq)


def kernel(**inputs):
    import numpy as np
    import concourse.bacc as _bacc
    from concourse.bass_utils import run_bass_kernel_spmd as _run

    def get(name):
        return np.asarray(inputs["L0_" + name])

    def packed(blocks):
        return np.ascontiguousarray(np.stack(blocks, axis=1))

    key = get("attn_b_Wkey").T
    val = get("attn_b_Wval").T
    arrays = {
        "x": np.ascontiguousarray(get("attn_a_embeddings")),
        "att_mats": packed([get("attn_a_W_Q").T, get("attn_a_W_K").T, get("attn_a_W_V")]),
        "mats": packed(
            [get("attn_b_" + n).T for n in ("Wk", "Wv", "Wr", "Wo", "Wrec")]
            + [get("ffn_" + n) for n in ("Ws1", "Ws3", "Ws2")]
            + [val[P * j:P * (j + 1), :] for j in range(FB)]),
        "key": np.ascontiguousarray(key),
        "vecs": packed([get("attn_b_" + n).reshape(-1) for n in (
            "ln1_w", "ln1_b", "ln2_w", "ln2_b", "att_tmk", "att_tmv", "att_tmr", "time_decay", "time_first",
            "ffn_tmk", "ffn_tmr")]),
        "w_gate": np.ascontiguousarray(get("ffn_Wg")),
        "w1": np.ascontiguousarray(get("ffn_W1").transpose(1, 0, 2).reshape(D, PAIRS, P)),
        "w3": np.ascontiguousarray(get("ffn_W3").transpose(1, 0, 2).reshape(D, PAIRS, P)),
        "w2": np.ascontiguousarray(get("ffn_W2").reshape(PAIRS, P, D).transpose(1, 0, 2)),
    }
    nc = _bacc.Bacc("TRN2", target_bir_lowering=False, num_devices=1)
    args = [nc.dram_tensor("in_" + n, a.shape, mybir.dt.from_np(a.dtype), kind="ExternalInput").ap() for n, a in arrays.items()]
    args.append(nc.dram_tensor("x_out", (B, S, D), F32, kind="ExternalOutput").ap())
    hybrid_kernel(nc, *args)
    r = _run(nc, [{"in_" + n: a for n, a in arrays.items()}], core_ids=[0])
    return r.results[0]["x_out"]
```
